# Optimizing a Trainium2 kernel written in Bass

```python
import numpy as np
import jax
import jax.numpy as jnp

def _softmax(x, axis=-1):
    return jax.nn.softmax(x, axis=axis)

def _gelu(x):
    return jax.nn.gelu(x, approximate=True)

def _silu(x):
    return jax.nn.silu(x)

def _sigmoid(x):
    return jax.nn.sigmoid(x)

def _layernorm(x, axis=-1, eps=1e-05):
    m = jnp.mean(x, axis=axis, keepdims=True)
    v = jnp.var(x, axis=axis, keepdims=True)
    return (x - m) / jnp.sqrt(v + eps)

def _scatter_add(tgt, idx, src, axis=0):
    return tgt.at[idx].add(src)

def _segment_sum(src, seg, n):
    return jax.ops.segment_sum(src, seg, n)
kernel_name = 'mk_gnn_resnorm_d4_gnn_r32_02085e'

def setup_inputs(seed: int=0):
    np.random.seed(seed)
    _w = jnp.asarray

    def _rec_inputs():
        import jax
        import jax.numpy as jnp
        _gk = jax.random.key(seed)
        x = -0.0003713 + 1 * jax.random.normal(jax.random.fold_in(_gk, 1), (3125, 256), jnp.float32)
        src = jax.random.randint(jax.random.fold_in(_gk, 2), (50000,), 0, 3125, jnp.int32)
        dst = jnp.minimum((3125 * jax.random.uniform(jax.random.fold_in(_gk, 3), (50000,)) ** 2.0).astype(jnp.int32), 99999)
        _o = jnp.argsort(dst, stable=True)
        src = src[_o]
        dst = dst[_o]
        edge_type_8 = jax.random.randint(jax.random.fold_in(_gk, 13), (50000,), 0, 8, jnp.int32)
        edge_weight = jax.random.uniform(jax.random.fold_in(_gk, 14), (50000,), jnp.float32, 0.0, 1)
        node_type_4 = jax.random.randint(jax.random.fold_in(_gk, 15), (3125,), 0, 4, jnp.int32)
        return (x, src, dst, edge_type_8, edge_weight, node_type_4)
    x, src, dst, edge_type_8, edge_weight, node_type_4 = _rec_inputs()

    def _L0_gnn_setup():
        import jax, jax.numpy as jnp
        import numpy as np
        N_NODES = 50000
        key = jax.random.key(seed)
        k1, k2, k3 = jax.random.split(key, 3)
        x = jax.random.normal(k1, (N_NODES, 256), dtype=jnp.float32)
        W = jax.random.normal(k2, (256, 256), dtype=jnp.float32) * (1.0 / np.sqrt(256))
        edge_index = jax.random.randint(k3, (2, 50000), 0, N_NODES, dtype=jnp.int64)
        return {'x': x, 'W': W, 'edge_index': edge_index}
    _L0_gnn_all = _L0_gnn_setup()
    _L0_gnn_in = {k: v for k, v in _L0_gnn_all.items() if k in ('W',)}
    del _L0_gnn_all

    def _L1_gnn_setup():
        import jax, jax.numpy as jnp
        import numpy as np
        N_NODES = 3125
        N_EDGES = 100000
        DIM_IN = 256
        DIM_OUT = 256
        key = jax.random.key(seed)
        ks = jax.random.split(key, 8)
        feat_in = jax.random.normal(ks[0], (N_NODES, DIM_IN), dtype=jnp.float32)
        edge_row = jax.random.randint(ks[1], (N_EDGES,), 0, N_NODES, dtype=jnp.int32)
        edge_col = jax.random.randint(ks[2], (N_EDGES,), 0, N_NODES, dtype=jnp.int32)
        edge_val = jax.random.uniform(ks[3], (N_EDGES,), dtype=jnp.float32)
        s1 = 1.0 / np.sqrt(DIM_IN)
        s2 = 1.0 / np.sqrt(DIM_OUT)
        W1 = jax.random.normal(ks[4], (DIM_IN, DIM_OUT), dtype=jnp.float32) * s1
        b1 = jnp.zeros((DIM_OUT,), dtype=jnp.float32)
        W2 = jax.random.normal(ks[5], (DIM_OUT, DIM_OUT), dtype=jnp.float32) * s2
        b2 = jnp.zeros((DIM_OUT,), dtype=jnp.float32)
        eps = jnp.zeros((1,), dtype=jnp.float32)
        offset = jnp.zeros((DIM_OUT,), dtype=jnp.float32)
        scale = jnp.ones((DIM_OUT,), dtype=jnp.float32)
        return {'feat_in': feat_in, 'edge_row': edge_row, 'edge_col': edge_col, 'edge_val': edge_val, 'W1': W1, 'b1': b1, 'W2': W2, 'b2': b2, 'eps': eps, 'offset': offset, 'scale': scale}
    _L1_gnn_all = _L1_gnn_setup()
    _L1_gnn_in = {k: v for k, v in _L1_gnn_all.items() if k in ('W1', 'b1', 'W2', 'b2', 'eps', 'offset', 'scale')}
    del _L1_gnn_all

    def _L2_gnn_setup():
        import jax, jax.numpy as jnp
        import numpy as np
        N_NODES = 50000
        N_EDGES = 25000
        DIM = 256
        HEADS = 8
        DIM_OUT = 32
        key = jax.random.key(seed)
        ks = jax.random.split(key, 9)
        s = 1.0 / np.sqrt(DIM)
        inner = HEADS * DIM_OUT
        return {'x': jax.random.normal(ks[0], (N_NODES, DIM), dtype=jnp.float32), 'Wq': jax.random.uniform(ks[1], (DIM, inner), jnp.float32, -s, s), 'bq': jax.random.uniform(ks[2], (inner,), jnp.float32, -s, s), 'Wk': jax.random.uniform(ks[3], (DIM, inner), jnp.float32, -s, s), 'bk': jax.random.uniform(ks[4], (inner,), jnp.float32, -s, s), 'Wv': jax.random.uniform(ks[5], (DIM, inner), jnp.float32, -s, s), 'bv': jax.random.uniform(ks[6], (inner,), jnp.float32, -s, s), 'src': jax.random.randint(ks[7], (N_EDGES,), 0, N_NODES), 'dst': jax.random.randint(ks[8], (N_EDGES,), 0, N_NODES)}
    _L2_gnn_all = _L2_gnn_setup()
    _L2_gnn_in = {k: v for k, v in _L2_gnn_all.items() if k in ('Wq', 'bq', 'Wk', 'bk', 'Wv', 'bv')}
    del _L2_gnn_all

    def _L3_gnn_setup():
        import jax, jax.numpy as jnp
        import numpy as np
        N_NODES = 625
        N_EDGES = 10000
        IN_DIM = 256
        OUT_DIM = 256
        N_HEADS = 4
        D_K = OUT_DIM // N_HEADS
        N_NTYPES = 4
        N_RELS = 8
        SQRT_DK = float(np.sqrt(D_K))

        def _typed_matmul(x, W, node_type):
            all_t = jnp.einsum('ni,tio->tno', x, W)
            return all_t[node_type, jnp.arange(x.shape[0])]
        key = jax.random.key(seed)
        ks = jax.random.split(key, 12)
        xav = lambda k, shape, fan: jax.random.normal(k, shape, jnp.float32) * (1.0 / np.sqrt(fan))
        return {'h': jax.random.normal(ks[0], (N_NODES, IN_DIM), jnp.float32), 'k_linears': xav(ks[1], (N_NTYPES, IN_DIM, OUT_DIM), IN_DIM), 'q_linears': xav(ks[2], (N_NTYPES, IN_DIM, OUT_DIM), IN_DIM), 'v_linears': xav(ks[3], (N_NTYPES, IN_DIM, OUT_DIM), IN_DIM), 'a_linears': xav(ks[4], (N_NTYPES, OUT_DIM, OUT_DIM), OUT_DIM), 'relation_att': xav(ks[5], (N_RELS, N_HEADS, D_K, D_K), D_K), 'relation_msg': xav(ks[6], (N_RELS, N_HEADS, D_K, D_K), D_K), 'relation_pri': jnp.ones((N_RELS, N_HEADS), jnp.float32), 'skip': jnp.ones((N_NTYPES,), jnp.float32), 'node_type': jax.random.randint(ks[7], (N_NODES,), 0, N_NTYPES), 'etype': jnp.sort(jax.random.randint(ks[8], (N_EDGES,), 0, N_RELS)), 'row_idx': jax.random.randint(ks[9], (N_EDGES,), 0, N_NODES), 'col_idx': jax.random.randint(ks[10], (N_EDGES,), 0, N_NODES)}
    _L3_gnn_all = _L3_gnn_setup()
    _L3_gnn_in = {k: v for k, v in _L3_gnn_all.items() if k in ('k_linears', 'q_linears', 'v_linears', 'a_linears', 'relation_att', 'relation_msg', 'relation_pri', 'skip')}
    del _L3_gnn_all
    return {'x': x, 'src': src, 'dst': dst, 'edge_type_8': edge_type_8, 'edge_weight': edge_weight, 'node_type_4': node_type_4, 'L0_gnn_W': _L0_gnn_in['W'], 'L1_gnn_W1': _L1_gnn_in['W1'], 'L1_gnn_b1': _L1_gnn_in['b1'], 'L1_gnn_W2': _L1_gnn_in['W2'], 'L1_gnn_b2': _L1_gnn_in['b2'], 'L1_gnn_eps': _L1_gnn_in['eps'], 'L1_gnn_offset': _L1_gnn_in['offset'], 'L1_gnn_scale': _L1_gnn_in['scale'], 'L2_gnn_Wq': _L2_gnn_in['Wq'], 'L2_gnn_bq': _L2_gnn_in['bq'], 'L2_gnn_Wk': _L2_gnn_in['Wk'], 'L2_gnn_bk': _L2_gnn_in['bk'], 'L2_gnn_Wv': _L2_gnn_in['Wv'], 'L2_gnn_bv': _L2_gnn_in['bv'], 'L3_gnn_k_linears': _L3_gnn_in['k_linears'], 'L3_gnn_q_linears': _L3_gnn_in['q_linears'], 'L3_gnn_v_linears': _L3_gnn_in['v_linears'], 'L3_gnn_a_linears': _L3_gnn_in['a_linears'], 'L3_gnn_relation_att': _L3_gnn_in['relation_att'], 'L3_gnn_relation_msg': _L3_gnn_in['relation_msg'], 'L3_gnn_relation_pri': _L3_gnn_in['relation_pri'], 'L3_gnn_skip': _L3_gnn_in['skip']}

def reference(x, src, dst, edge_type_8, edge_weight, node_type_4, L0_gnn_W, L1_gnn_W1, L1_gnn_b1, L1_gnn_W2, L1_gnn_b2, L1_gnn_eps, L1_gnn_offset, L1_gnn_scale, L2_gnn_Wq, L2_gnn_bq, L2_gnn_Wk, L2_gnn_bk, L2_gnn_Wv, L2_gnn_bv, L3_gnn_k_linears, L3_gnn_q_linears, L3_gnn_v_linears, L3_gnn_a_linears, L3_gnn_relation_att, L3_gnn_relation_msg, L3_gnn_relation_pri, L3_gnn_skip):
    import jax
    import jax.numpy as jnp

    def _L0_gnn_ref(x, W, edge_index):
        import jax, jax.numpy as jnp
        import numpy as np
        N_NODES = 50000
        N = x.shape[0]
        src, dst = (edge_index[0], edge_index[1])
        h = x @ W
        deg = jax.ops.segment_sum(jnp.ones_like(dst, dtype=h.dtype), dst, num_segments=N)
        deg_inv_sqrt = jnp.where(deg > 0, jax.lax.rsqrt(jnp.maximum(deg, 1)), 0.0)
        norm = deg_inv_sqrt[src] * deg_inv_sqrt[dst]
        msgs = h[src] * norm[:, None]
        out = jax.ops.segment_sum(msgs, dst, num_segments=N)
        return out

    def _L1_gnn_ref(feat_in, edge_row, edge_col, edge_val, W1, b1, W2, b2, eps, offset, scale):
        import jax, jax.numpy as jnp
        import numpy as np
        N_NODES = 3125
        N_EDGES = 100000
        DIM_IN = 256
        DIM_OUT = 256
        msg = edge_val[:, None] * feat_in[edge_col]
        aggr = jax.ops.segment_sum(msg, edge_row, num_segments=feat_in.shape[0])
        aggr = aggr + (1.0 + eps) * feat_in
        h = jnp.maximum(aggr @ W1 + b1, 0.0) @ W2 + b2
        h = jnp.maximum(h, 0.0)
        mean = jnp.mean(h, axis=1, keepdims=True)
        var = jnp.var(h, axis=1, keepdims=True) + 1e-10
        return (h - mean) * scale * jax.lax.rsqrt(var) + offset

    def _L2_gnn_ref(x, Wq, bq, Wk, bk, Wv, bv, src, dst):
        import jax, jax.numpy as jnp
        import numpy as np
        N_NODES = 50000
        N_EDGES = 25000
        DIM = 256
        HEADS = 8
        DIM_OUT = 32
        n = x.shape[0]
        q = (x @ Wq + bq).reshape(n, HEADS, DIM_OUT)
        k = (x @ Wk + bk).reshape(n, HEADS, DIM_OUT)
        v = (x @ Wv + bv).reshape(n, HEADS, DIM_OUT)
        scores = jnp.einsum('ehd,ehd->eh', q[src], k[dst]) / jnp.sqrt(jnp.asarray(DIM_OUT, dtype=x.dtype))
        m = jax.ops.segment_max(scores, dst, num_segments=n)
        m = jnp.where(jnp.isfinite(m), m, 0.0)
        e = jnp.exp(scores - m[dst])
        z = jax.ops.segment_sum(e, dst, num_segments=n)
        p = e / jnp.maximum(z[dst], 1e-16)
        out = jax.ops.segment_sum(v[src] * p[:, :, None], dst, num_segments=n)
        return out.reshape(n, HEADS * DIM_OUT)

    def _L3_gnn_ref(h, k_linears, q_linears, v_linears, a_linears, relation_att, relation_msg, relation_pri, skip, node_type, etype, row_idx, col_idx):
        import jax, jax.numpy as jnp
        import numpy as np
        N_NODES = 625
        N_EDGES = 10000
        IN_DIM = 256
        OUT_DIM = 256
        N_HEADS = 4
        D_K = OUT_DIM // N_HEADS
        N_NTYPES = 4
        N_RELS = 8
        SQRT_DK = float(np.sqrt(D_K))

        def _typed_matmul(x, W, node_type):
            all_t = jnp.einsum('ni,tio->tno', x, W)
            return all_t[node_type, jnp.arange(x.shape[0])]
        n = h.shape[0]
        k = _typed_matmul(h, k_linears, node_type).reshape(n, N_HEADS, D_K)
        q = _typed_matmul(h, q_linears, node_type).reshape(n, N_HEADS, D_K)
        v = _typed_matmul(h, v_linears, node_type).reshape(n, N_HEADS, D_K)
        q_att = jnp.einsum('nhd,rhde->rnhe', q, relation_att)
        v_msg = jnp.einsum('nhd,rhde->rnhe', v, relation_msg)
        aw_q_edge = q_att[etype, col_idx]
        msg_edge = v_msg[etype, row_idx]
        attn_score = jnp.sum(aw_q_edge * k[row_idx], axis=-1)
        score = attn_score * (relation_pri[etype] / SQRT_DK)
        m = jax.ops.segment_max(score, col_idx, num_segments=n)
        ex = jnp.exp(score - m[col_idx])
        denom = jax.ops.segment_sum(ex, col_idx, num_segments=n)
        alpha = ex / denom[col_idx]
        agg = jax.ops.segment_sum(alpha[..., None] * msg_edge, col_idx, num_segments=n)
        agg = agg.reshape(n, OUT_DIM)
        out = _typed_matmul(agg, a_linears, node_type)
        out = jax.nn.sigmoid(skip)[node_type][:, None] * out
        return out
    edge_index = jnp.stack([src, dst])
    x = _layernorm(x + _L0_gnn_ref(x, L0_gnn_W, edge_index), axis=-1)
    x = _layernorm(x + _L1_gnn_ref(x, src, dst, edge_weight, L1_gnn_W1, L1_gnn_b1, L1_gnn_W2, L1_gnn_b2, L1_gnn_eps, L1_gnn_offset, L1_gnn_scale), axis=-1)
    x = _layernorm(x + _L2_gnn_ref(x, L2_gnn_Wq, L2_gnn_bq, L2_gnn_Wk, L2_gnn_bk, L2_gnn_Wv, L2_gnn_bv, src, dst), axis=-1)
    x = _layernorm(x + _L3_gnn_ref(x, L3_gnn_k_linears, L3_gnn_q_linears, L3_gnn_v_linears, L3_gnn_a_linears, L3_gnn_relation_att, L3_gnn_relation_msg, L3_gnn_relation_pri, L3_gnn_skip, node_type_4, edge_type_8, src, dst), axis=-1)
    return x

_drawn_inputs = setup_inputs


def setup_inputs(seed=0):
    import zlib

    import numpy as np

    out = dict(_drawn_inputs(seed))
    spreads = {'L1_gnn_b1': (0.0, 0.1),
     'L1_gnn_b2': (0.0, 0.1),
     'L1_gnn_offset': (0.0, 0.1),
     'L1_gnn_scale': (1.0, 0.2),
     'L3_gnn_relation_pri': (1.0, 0.2),
     'L3_gnn_skip': (1.0, 0.6)}
    factors = {'L2_gnn_bq': 8.0, 'L2_gnn_bk': 8.0}
    for name, (base, spread) in spreads.items():
        noise = np.random.default_rng([zlib.crc32(name.encode()), seed]).standard_normal(out[name].shape)
        drawn = base * np.exp(spread * noise) if base else spread * noise
        out[name] = jnp.asarray(drawn.astype(out[name].dtype))
    for name, factor in factors.items():
        out[name] = (out[name] * factor).astype(out[name].dtype)
    return out
```

```python
import concourse.bass as bass
from concourse import mybir
from contextlib import ExitStack

F32 = mybir.dt.float32
BF16 = mybir.dt.bfloat16
F16 = mybir.dt.float16
I32 = mybir.dt.int32
ALU = mybir.AluOpType
ACT = mybir.ActivationFunctionType
AX = mybir.AxisListType

P = 128
D = 256
N_NODES, N_EDGES = 3125, 50000
NT = -(-N_NODES // P)
NP = NT * P
PAD_NODE = NP - 1
GT = 7
HALVES = 2
BODY = GT * HALVES
NB = -(-N_EDGES // (P * BODY))
TILES = NB * BODY
EP = TILES * P
CH = 4
ROWS = TILES // CH
NBR = 2 * TILES
BC = 7
BR = NBR // BC
MERGED = EP
ZERO_ROW = EP + NBR
PROWS = ZERO_ROW + 1
NL = 5
BIG = 1.0e30
RELS, TYPES = 8, 4
assert ROWS * CH == TILES and BR * BC == NBR and NT % NL == 0


class Chain:

    def __init__(self, eng, sem, base=0):
        self.eng, self.sem, self.base, self.n = eng, sem, base, 0

    def __call__(self, ins):
        self.n += 1
        ins.then_inc(self.sem, 1)
        self.eng.wait_ge(self.sem, self.base + self.n)


def wait(eng, sem, value):
    if isinstance(value, int) and value <= 0:
        return
    eng.wait_ge(sem, value)


def hold(eng, seen, sem, value):
    wait(eng, sem, value)
    eng.sem_inc(seen, 1)


def repeat(eng, count, body):
    body(0)
    if count > 1:
        with eng.Fori(1, count) as b:
            body(b)


class Names:

    def __init__(self, nc, stack):
        self.nc, self.stack = nc, stack

    def sb(self, name, shape, dt=F32):
        return self.stack.enter_context(self.nc.sbuf_tensor(name, shape, dt))

    def ps(self, name, shape, dt=F32):
        return self.stack.enter_context(self.nc.psum_tensor(name, shape, dt))

    def sem(self, name):
        handle = self.nc.alloc_semaphore(name=name)
        self.stack.callback(self.nc.release_semaphore, handle)
        self.stack.callback(self.nc.gpsimd.sem_clear, handle)
        return handle


    def dma_sem(self, name):
        return self.nc.alloc_semaphore(name=name)


def bcast(ap, count):
    return ap.unsqueeze(2).to_broadcast([ap.shape[0], ap.shape[1], count])


def mid(ap, count):
    return ap.unsqueeze(1).to_broadcast([ap.shape[0], count, ap.shape[1]])


def constants(nc, k):
    with ExitStack() as st:
        a = Names(nc, st)
        s_fill = a.sem("c_fill")
        with nc.Block() as block:
            @block.gpsimd
            def _(pool):
                done = Chain(pool, s_fill)
                nc.gpsimd.iota(k.iota[:, :], [[1, P]], base=0, channel_multiplier=0,
                               allow_small_or_imprecise_dtypes=True)
                pool.memset(k.ident[:, :], 0.0)
                pool.memset(k.tri[:, :], 1.0)
                pool.memset(k.zeros_bf[:, :], 0.0)
                pool.memset(k.ones[:, :], 1.0)
                done(pool.memset(k.tri_hi[:, :], 1.0))
                pool.affine_select(out=k.ident[:, :], in_=k.ident[:, :], compare_op=ALU.not_equal, fill=1.0,
                                   base=0, pattern=[[-1, P]], channel_multiplier=1)
                pool.affine_select(out=k.tri[:, :], in_=k.tri[:, :], compare_op=ALU.is_gt, fill=0.0,
                                   base=0, pattern=[[-1, P]], channel_multiplier=1)
                done(pool.affine_select(out=k.tri_hi[:, :], in_=k.tri_hi[:, :], compare_op=ALU.is_gt, fill=0.0,
                                        base=0, pattern=[[1, NT]], channel_multiplier=-1))
                done(nc.gpsimd.tensor_copy(k.ident_bf[:, :], k.ident[:, :]))


def load_rows(sp, rows, source, sem, pad_tile_free):
    full = N_EDGES // P
    c, r = full // ROWS, full % ROWS
    sp.dma_start(rows[:, 0:c, :], source[0:c * ROWS * P].rearrange("(c t e) -> t c e", t=ROWS, e=P)).then_inc(sem, 16)
    sp.dma_start(rows[0:r, c, :], source[c * ROWS * P:full * P].rearrange("(t e) -> t e", e=P)).then_inc(sem, 16)
    sp.dma_start(rows[r:r + 1, c, 0:N_EDGES - full * P],
                 source[full * P:N_EDGES].rearrange("(t e) -> t e", t=1)).then_inc(sem, 16)


def edge_columns(nc, k, other, key, etype, weight):
    with ExitStack() as st:
        a = Names(nc, st)
        rows_i = a.sb(k.tag + "ec_rows_i", [ROWS, 3, CH, P], I32)
        rows_w = a.sb(k.tag + "ec_rows_w", [ROWS, CH, P])
        rows_f = a.sb(k.tag + "ec_rows_f", [ROWS, 3, CH, P])
        key_i = a.sb(k.tag + "ec_key_i", [P, 3, TILES], I32)
        rec_rows = a.sb(k.tag + "ec_rec_rows", [ROWS, CH, P, 4])
        following = a.sb(k.tag + "ec_following", [ROWS, CH, P])
        falls = a.sb(k.tag + "ec_falls", [ROWS, CH, P])
        fall_sum = a.sb(k.tag + "ec_fall_sum", [ROWS, 1])
        turned = a.ps(k.tag + "ec_turned", [P, 4, CH, P])
        total = a.ps(k.tag + "ec_total", [P, 1])
        s_pad, s_load, s_row, s_turn, s_col, s_store, s_next, s_rec, s_fall, s_total = (
            a.sem(k.tag + "ec_" + n) for n in ("pad", "load", "row", "turn", "col", "store", "next", "rec", "fall", "stotal"))
        with nc.Block() as block:
            @block.gpsimd
            def _(pool):
                pool.memset(rows_i[:, 0, :, :], 0).then_inc(s_pad, 1)
                pool.memset(rows_i[:, 1, :, :], PAD_NODE).then_inc(s_pad, 1)
                pool.memset(rows_i[:, 2, :, :], 0).then_inc(s_pad, 1)
                pool.memset(rows_w[:, :, :], 0.0).then_inc(s_pad, 1)

            @block.sync
            def _(sp):
                sp.wait_ge(s_pad, 4)
                load_rows(sp, rows_i[:, 0, :, :], other, s_load, None)
                load_rows(sp, rows_i[:, 1, :, :], key, s_load, None)
                load_rows(sp, rows_i[:, 2, :, :], etype, s_load, None)
                load_rows(sp, rows_w[:, :, :], weight, s_load, None)
                sp.wait_ge(s_row, 1)
                sp.dma_start(k.key_pad.rearrange("(c t e) -> t c e", t=ROWS, e=P), rows_f[:, 1, :, :]).then_inc(s_store, 16)
                sp.wait_ge(s_store, 16)
                first = k.key_pad[P:EP].rearrange("(t e) -> t e", e=P)[:, 0:1]
                for c in range(CH):
                    n = min(ROWS, TILES - 1 - c * ROWS)
                    with nc.allow_non_contiguous_dma("a value of each tile"):
                        sp.dma_start(following[0:n, c, P - 1:P], first[c * ROWS:c * ROWS + n, :]).then_inc(s_next, 16)
                sp.wait_ge(s_rec, 4)
                sp.dma_start(k.rec_sorted.rearrange("(c t e) q -> t c (e q)", t=ROWS, e=P),
                             rec_rows[:, :, :, :].rearrange("t c e q -> t c (e q)")).then_inc(s_store, 16)
                sp.wait_ge(s_store, 32)

            @block.vector
            def _(dve):
                dve.wait_ge(s_load, 16 * 12)
                nc.vector.memset(following[:, :, P - 1:P], float(PAD_NODE))
                nc.vector.tensor_copy(rows_f[:, :, :, :], rows_i[:, :, :, :]).then_inc(s_row, 1)
                dve.wait_ge(s_row, 1)
                for n in range(4):
                    nc.vector.tensor_copy(rec_rows[:, :, :, n], rows_w[:, :, :] if n == 3 else rows_f[:, n, :, :]).then_inc(s_rec, 1)
                nc.vector.tensor_copy(following[:, :, 0:P - 1], rows_f[:, 1, :, 1:P]).then_inc(s_fall, 1)
                dve.wait_ge(s_fall, 1)
                dve.wait_ge(s_next, 16 * CH)
                nc.vector.tensor_tensor(falls[:, :, :], rows_f[:, 1, :, :], following[:, :, :], ALU.is_gt).then_inc(s_fall, 1)
                dve.wait_ge(s_fall, 2)
                nc.vector.tensor_reduce(fall_sum[:, :], falls[:, :, :], AX.XY, ALU.add).then_inc(s_fall, 1)
                dve.wait_ge(s_total, 1)
                nc.vector.tensor_copy(k.unsorted[:, :], total[:, :]).then_inc(s_fall, 1)
                dve.wait_ge(s_turn, 1)
                done = Chain(dve, s_col)
                for n in range(4):
                    last = nc.vector.tensor_copy(k.rec[:, :, n].rearrange("p (c t) -> p c t", c=CH), turned[:, n, :, 0:ROWS])
                    done(last)
                done(nc.vector.tensor_copy(k.key_col[:, 0:TILES], k.rec[:, :, 1]))
                done(nc.vector.tensor_copy(key_i[:, 0, :], k.rec[:, :, 1]))
                done(nc.vector.tensor_scalar(key_i[:, 1, :], key_i[:, 0, :], 7, None, ALU.logical_shift_right))
                done(nc.vector.tensor_scalar(key_i[:, 2, :], key_i[:, 0, :], P - 1, None, ALU.bitwise_and))
                done(nc.vector.tensor_copy(k.hi_col[:, 0:TILES], key_i[:, 1, :]))
                done(nc.vector.tensor_copy(k.lo_col[:, 0:TILES], key_i[:, 2, :]))
                for pad in (k.hi_col, k.lo_col):
                    done(nc.vector.memset(pad[:, TILES:TILES + GT], 0.0))

            @block.tensor
            def _(pe):
                pe.wait_ge(s_row, 1)
                for n in range(4):
                    for c in range(CH):
                        source = rows_w[:, c, :] if n == 3 else rows_f[:, n, c, :]
                        last = nc.tensor.transpose(turned[:, n, c, 0:ROWS], source, k.ident[0:ROWS, 0:ROWS])
                last.then_inc(s_turn, 1)
                pe.wait_ge(s_fall, 3)
                nc.tensor.matmul(total[:, :], k.ones[0:ROWS, :], fall_sum[:, :], start=True, stop=True).then_inc(s_total, 1)


def degrees(nc, k):
    with ExitStack() as st:
        a = Names(nc, st)
        hot_hi = a.sb(k.tag + "dg_hot_hi", [P, 2, GT, NT], BF16)
        hot_lo = a.sb(k.tag + "dg_hot_lo", [P, 2, GT, P], BF16)
        hist = a.ps(k.tag + "dg_hist", [NT, P])
        s_hot, s_used, s_free, s_tot, s_pre, s_v, s_t, s_tt = (a.sem(k.tag + "dg_" + n) for n in
                                                 ("hot", "used", "free", "tot", "pre", "v", "t", "tt"))
        deg = a.sb(k.tag + "dg_deg", [NT, P])
        incl = a.sb(k.tag + "dg_incl", [NT, P])
        before = a.ps(k.tag + "dg_before", [NT, 1])
        ends = a.sb(k.tag + "dg_ends", [NT, 4, P])
        ei = a.sb(k.tag + "dg_ei", [NT, 8, P], I32)
        ef = a.sb(k.tag + "dg_ef", [NT, 8, P])
        turned = a.ps(k.tag + "dg_turned", [P, 2, 32])
        with nc.Block() as block:
            @block.vector
            def _(dve):
                def body(b):
                    for h in range(HALVES):
                        cols = bass.ds(b * BODY + h * GT, GT)
                        wait(dve, s_free, b * 2 + (h - 1))
                        nc.vector.tensor_tensor(hot_hi[:, h, :, :], mid(k.iota[:, 0:NT], GT), bcast(k.hi_col[:, cols], NT), ALU.is_equal)
                        nc.vector.tensor_tensor(hot_lo[:, h, :, :], mid(k.iota[:, :], GT), bcast(k.lo_col[:, cols], P), ALU.is_equal).then_inc(s_hot, 1)
                repeat(dve, NB, body)
                dve.wait_ge(s_used, 1)
                done = Chain(dve, s_v)
                done(nc.vector.tensor_copy(deg[:, :], hist[:, :]))
                done(nc.vector.memset(ef[:, 0, :], 0.0))
                done(nc.vector.tensor_tensor_scan(incl[:, :], ef[:, 0, :], deg[:, :], 0.0, ALU.add, ALU.add))
                dve.sem_inc(s_tot, 1)
                dve.wait_ge(s_pre, 1)
                e0, e1 = ends[:, 0, :], ends[:, 1, :]
                done(nc.vector.tensor_scalar(e1, incl[:, :], before[:, 0:1], None, ALU.add))
                done(nc.vector.tensor_tensor(e0, e1, deg[:, :], ALU.subtract))
                done(nc.vector.tensor_copy(k.first_pos[:, :], e0))
                done(nc.vector.tensor_scalar(ends[:, 2, :], e1, 1.0, 0.0, ALU.subtract, ALU.max))
                done(nc.vector.tensor_copy(ei[:, 0, :], e0))
                done(nc.vector.tensor_copy(ei[:, 1, :], e1))
                done(nc.vector.tensor_copy(ei[:, 2, :], ends[:, 2, :]))
                done(nc.vector.tensor_scalar(ei[:, 3, :], ei[:, 0, :], 7, None, ALU.logical_shift_right))
                done(nc.vector.tensor_scalar(ei[:, 4, :], ei[:, 2, :], 7, None, ALU.logical_shift_right))
                done(nc.vector.tensor_scalar(ei[:, 5, :], ei[:, 1, :], P - 1, None, ALU.bitwise_and))
                done(nc.vector.tensor_copy(ef[:, 3:6, :], ei[:, 3:6, :]))
                t0, t1, tail = ef[:, 3, :], ef[:, 4, :], ef[:, 5, :]
                last, same, none, inside, across = (ef[:, n, :] for n in (6, 7, 0, 1, 2))
                done(nc.vector.tensor_scalar(last, tail, 0.0, None, ALU.is_equal))
                done(nc.vector.tensor_tensor(same, t0, t1, ALU.is_equal))
                done(nc.vector.tensor_scalar(inside, t0, float(P), float(P - 1), ALU.mult, ALU.add))
                done(nc.vector.tensor_tensor(inside, inside, e0, ALU.subtract))
                done(nc.vector.tensor_tensor(inside, inside, last, ALU.mult))
                done(nc.vector.tensor_tensor(inside, inside, e0, ALU.add))
                done(nc.vector.tensor_scalar(across, t1, 2.0, float(MERGED), ALU.mult, ALU.add))
                done(nc.vector.tensor_tensor(across, across, last, ALU.add))
                done(nc.vector.tensor_tensor(inside, inside, across, ALU.subtract))
                done(nc.vector.tensor_tensor(inside, inside, same, ALU.mult))
                done(nc.vector.tensor_tensor(inside, inside, across, ALU.add))
                done(nc.vector.tensor_scalar(none, deg[:, :], 0.0, None, ALU.is_equal))
                done(nc.vector.tensor_scalar(across, inside, -1.0, float(ZERO_ROW), ALU.mult, ALU.add))
                done(nc.vector.tensor_tensor(across, across, none, ALU.mult))
                done(nc.vector.tensor_tensor(inside, inside, across, ALU.add))
                dve.sem_inc(s_t, 1)
                dve.wait_ge(s_tt, 1)
                done(nc.vector.tensor_copy(k.sum_row[:, :], turned[:, 0, 0:NT]))
                done(nc.vector.tensor_copy(k.deg[:, :], turned[:, 1, 0:NT]))

            @block.tensor
            def _(pe):
                nc.tensor.matmul(hist[:, :], k.zeros_bf[:, 0:NT], k.zeros_bf[:, :], start=True, stop=False)
                def body(b):
                    for h in range(HALVES):
                        pe.wait_ge(s_hot, b * 2 + (h + 1))
                        for j in range(GT):
                            last = nc.tensor.matmul(hist[:, :], hot_hi[:, h, j, :], hot_lo[:, h, j, :],
                                                    start=False, stop=False)
                        last.then_inc(s_free, 1)
                repeat(pe, NB, body)
                nc.tensor.matmul(hist[:, :], k.zeros_bf[:, 0:NT], k.zeros_bf[:, :], start=False, stop=True).then_inc(s_used, 1)
                pe.wait_ge(s_tot, 1)
                nc.tensor.matmul(before[:, :], k.tri_hi[0:NT, 0:NT], incl[:, P - 1:P], start=True, stop=True).then_inc(s_pre, 1)
                pe.wait_ge(s_t, 1)
                nc.tensor.transpose(turned[:, 0, 0:NT], ef[:, 1, :], k.ident[0:NT, 0:NT])
                nc.tensor.transpose(turned[:, 1, 0:NT], deg[:, :], k.ident[0:NT, 0:NT]).then_inc(s_tt, 1)



def key_falls(nc, k, eng, kind):
    return eng.to_reg(nc.values_load(k.unsorted[0:1, 0:1], engines=(mybir.EngineType[kind],), min_val=0, max_val=EP))


def ranks(nc, k):
    with ExitStack() as st:
        a = Names(nc, st)
        hot_hi = a.sb(k.tag + "rk_hot_hi", [P, 2, GT, NT], BF16)
        hot_lo = a.sb(k.tag + "rk_hot_lo", [P, 2, GT, P], BF16)
        hot_hi_t = a.sb(k.tag + "rk_hot_hi_t", [NT, 2, GT, P], F16)
        snap = a.sb(k.tag + "rk_snap", [NT, 2, GT, P], F16)
        base = a.sb(k.tag + "rk_base", [NT, P])
        base_i = a.sb(k.tag + "rk_base_i", [NT, 2, P], I32)
        parts = a.sb(k.tag + "rk_parts", [NT, 2, 2, P], F16)
        key_row = a.sb(k.tag + "rk_key_row", [P, 2, GT * P])
        key_ring = a.sb(k.tag + "rk_key_ring", [P, 2, GT])
        junk = a.sb(k.tag + "rk_junk", [P, GT, P])
        part = a.sb(k.tag + "rk_part", [P, 2, 2 * GT])
        index = a.sb(k.tag + "rk_index", [P, 2, GT], I32)
        rec_ring = a.sb(k.tag + "rk_rec_ring", [P, 2, GT, 4])
        table = a.ps(k.tag + "rk_table", [NT, GT + 1, P])
        picked = [a.ps(k.tag + f"rk_picked{h}", [P, 8, P]) for h in range(2)]
        turned = [a.ps(k.tag + f"rk_turned{h}", [NT, 8, P], BF16) for h in range(2)]
        s_row = [a.sem(k.tag + f"rk_row{h}") for h in range(2)]
        s_scat = [a.dma_sem(k.tag + f"rk_scat{h}") for h in range(2)]
        s_hot, s_turn, s_turned, s_snap, s_table, s_pick, s_index, s_v, s_seen, s_free, s_taken, s_base = (
            a.sem(k.tag + "rk_" + n) for n in ("hot", "turn", "turned", "snap", "stable", "pick", "index", "v", "seen", "free", "taken", "sbase"))
        with nc.Block() as block:
            @block.sync
            def _(sp):
                with sp.If_ne(key_falls(nc, k, sp, "SP"), 0):
                    def body(b):
                        for h in range(HALVES):
                            wait(sp, s_free, b * 2 + (h - 1))
                            sp.dma_start(key_row[:, h, :], k.key_pad[bass.ds(b * (BODY * P) + h * GT * P, GT * P)]
                                         .partition_broadcast(P)).then_inc(s_row[h], 16)
                    repeat(sp, NB, body)

            @block.vector
            def _(dve):
                with dve.If_ne(key_falls(nc, k, dve, "DVE"), 0):
                    PER = 2 * (9 + 2 * GT)

                    def one_hots(h, tile):
                        cols = bass.ds(tile, GT)
                        nc.vector.tensor_tensor(hot_hi[:, h, :, :], mid(k.iota[:, 0:NT], GT), bcast(k.hi_col[:, cols], NT), ALU.is_equal)
                        return nc.vector.tensor_tensor(hot_lo[:, h, :, :], mid(k.iota[:, :], GT), bcast(k.lo_col[:, cols], P), ALU.is_equal)

                    def split_base(done, h):
                        done(nc.vector.tensor_copy(base_i[:, 0, :], base[:, :]))
                        done(nc.vector.tensor_scalar(base_i[:, 1, :], base_i[:, 0, :], 255, None, ALU.bitwise_and))
                        done(nc.vector.tensor_copy(parts[:, h, 0, :], base_i[:, 1, :]))
                        done(nc.vector.tensor_tensor(parts[:, h, 1, :], base[:, :], base_i[:, 1, :], ALU.subtract))
                        dve.sem_inc(s_base, 1)

                    start = Chain(dve, s_v)
                    start(one_hots(0, 0))
                    dve.sem_inc(s_hot, 1)
                    start(nc.vector.tensor_copy(base[:, :], k.first_pos[:, :]))
                    split_base(start, 0)

                    def body(b):
                        done = Chain(dve, s_v, b * PER + start.n)
                        for h in range(HALVES):
                            cols = bass.ds(b * BODY + h * GT, GT)
                            done(one_hots((h + 1) % 2, b * BODY + (h + 1) * GT))
                            dve.sem_inc(s_hot, 1)
                            done(nc.vector.tensor_copy(key_ring[:, h, :], k.key_col[:, cols]))
                            dve.wait_ge(s_row[h], b * 16 + 16)
                            for j in range(GT):
                                done(nc.vector.scalar_tensor_tensor(
                                    out=junk[:, j, :], in0=key_row[:, h, j * P:(j + 1) * P], scalar=key_ring[:, h, j:j + 1],
                                    in1=k.tri[:, :], op0=ALU.is_equal, op1=ALU.mult, accum_out=part[:, h, j:j + 1]))
                            dve.sem_inc(s_free, 1)
                            dve.wait_ge(s_snap, b * 2 + (h + 1))
                            done(nc.vector.tensor_tensor(base[:, :], base[:, :], snap[:, h, GT - 1, :], ALU.add))
                            split_base(done, (h + 1) % 2)
                            dve.wait_ge(s_pick, b * 2 + (h + 1))
                            for j in range(GT):
                                done(nc.vector.scalar_tensor_tensor(
                                    out=junk[:, j, :], in0=picked[h][:, j, :], scalar=1.0, in1=hot_lo[:, h, j, :],
                                    op0=ALU.mult, op1=ALU.mult, accum_out=part[:, h, GT + j:GT + j + 1]))
                            wait(dve, s_scat[h], b * (16 * GT))
                            done(nc.vector.tensor_copy(rec_ring[:, h, :, :], k.rec[:, cols, :]))
                            done(nc.vector.tensor_tensor(index[:, h, :], part[:, h, 0:GT], part[:, h, GT:2 * GT], ALU.add))
                            dve.sem_inc(s_index, 1)
                        assert done.n == PER
                    repeat(dve, NB, body)

            @block.scalar
            def _(act):
                with act.If_ne(key_falls(nc, k, act, "Activation"), 0):
                    def body(b):
                        for h in range(HALVES):
                            act.wait_ge(s_table, b * 2 + (h + 1))
                            nc.scalar.copy(snap[:, h, :, :], table[:, 0:GT, :]).then_inc(s_snap, 1)
                            act.wait_ge(s_turn, b * 2 + (h + 1))
                            nc.scalar.copy(hot_hi_t[:, h, :, :], turned[h][:, 0:GT, :]).then_inc(s_turned, 1)
                    repeat(act, NB, body)

            @block.tensor
            def _(pe):
                with pe.If_ne(key_falls(nc, k, pe, "PE"), 0):
                    def body(b):
                        for h in range(HALVES):
                            pe.wait_ge(s_hot, b * 2 + (h + 1))
                            for j in range(GT):
                                last = nc.tensor.transpose(turned[h][:, j, :], hot_hi[:, h, j, :], k.ident_bf[:, :])
                            last.then_inc(s_turn, 1)
                            hold(pe, s_taken, s_snap, b * 2 + h)
                            for lo, hi in ((0, 4), (4, GT)):
                                for j in range(hi):
                                    lo_j = max(lo, j)
                                    last = nc.tensor.matmul(table[:, lo_j:hi, :], hot_hi[:, h, j, :], mid(hot_lo[:, h, j, :], hi - lo_j),
                                                            start=(j == 0), stop=True, skip_group_check=(j > 0))
                            last.then_inc(s_table, 1)
                            hold(pe, s_taken, s_turned, b * 2 + (h + 1))
                            hold(pe, s_taken, s_snap, b * 2 + (h + 1))
                            hold(pe, s_taken, s_base, b * 2 + (h + 1))
                            hold(pe, s_taken, s_index, b * 2 + (h - 1))
                            for j in range(GT):
                                terms = [parts[:, h, 0, :], parts[:, h, 1, :]] + ([snap[:, h, j - 1, :]] if j else [])
                                for n, term in enumerate(terms):
                                    last = nc.tensor.matmul(picked[h][:, j, :], hot_hi_t[:, h, j, :], term, start=(n == 0), stop=(n == len(terms) - 1))
                            last.then_inc(s_pick, 1)
                    repeat(pe, NB, body)

            @block.gpsimd
            def _(pool):
                with pool.If_ne(key_falls(nc, k, pool, "Pool"), 0):
                    limit = pool.snap(pool.to_reg(EP - 1))
                    def body(b):
                        for h in range(HALVES):
                            pool.wait_ge(s_index, b * 2 + (h + 1))
                            pool.sem_inc(s_seen, 1)
                            for j in range(GT):
                                pool.indirect_dma_start(k.rec_sorted, bass.IndirectOffsetOnAxis(ap=index[:, h, j:j + 1], axis=0),
                                                        rec_ring[:, h, j, :], None, bounds_check=limit, oob_is_err=False).then_inc(s_scat[h], 16)
                    repeat(pool, NB, body)
                    for h in range(HALVES):
                        pool.wait_ge(s_scat[h], 16 * GT * NB)


def edge_meta(nc, k):
    with ExitStack() as st:
        a = Names(nc, st)
        rows = a.sb(k.tag + "em_rows", [ROWS, CH, P, 4])
        start = a.sb(k.tag + "em_start", [ROWS, CH, P])
        pos = a.sb(k.tag + "em_pos", [ROWS, CH, P])
        slot = a.sb(k.tag + "em_slot", [ROWS, CH, P])
        last = a.sb(k.tag + "em_last", [ROWS, CH, P])
        reset = a.sb(k.tag + "em_reset", [ROWS, 2, CH, P])
        rel = a.sb(k.tag + "em_rel", [ROWS, CH, P])
        ends = a.sb(k.tag + "em_ends", [ROWS, CH, 2])
        zero = a.sb(k.tag + "em_zero", [ROWS, P])
        key = a.sb(k.tag + "em_key", [P, NBR])
        turned = [a.ps(k.tag + f"em_turned{n}", [P, CH, P]) for n in range(6)]
        s_load, s_v, s_rows, s_turn, s_store, s_key = (a.sem(k.tag + "em_" + n) for n in ("load", "v", "rows", "turn", "store", "key"))
        src, dst, typ, wgt = (rows[:, :, :, n] for n in range(4))
        with nc.Block() as block:
            @block.sync
            def _(sp):
                sp.dma_start(rows[:, :, :, :].rearrange("t c e q -> t c (e q)"),
                             k.rec_sorted.rearrange("(c t e) q -> t c (e q)", t=ROWS, e=P)).then_inc(s_load, 16)
                sp.wait_ge(s_rows, 1)
                for n in range(2 if k.attention else 0):
                    for heads in (8, 4):
                        for c in range(CH):
                            sp.dma_start(k.resets[n][heads][c * ROWS:(c + 1) * ROWS, :, :], mid(reset[:, n, c, :], heads)).then_inc(s_store, 16)
                sp.dma_start(k.ends.rearrange("(c t w) -> t c w", t=ROWS, w=2), ends[:, :, :]).then_inc(s_store, 16)
                sp.wait_ge(s_store, 16 * ((4 * CH if k.attention else 0) + 1))
                sp.dma_start(key[:, :], k.ends.partition_broadcast(P)).then_inc(s_key, 16)

            @block.vector
            def _(dve):
                done = Chain(dve, s_v)
                dve.wait_ge(s_load, 16)
                nc.vector.memset(zero[:, :], 0.0)
                nc.vector.memset(start[:, :, 0:1], 1.0)
                done(nc.vector.tensor_tensor(start[:, :, 1:P], dst[:, :, 1:P], dst[:, :, 0:P - 1], ALU.not_equal))
                done(nc.vector.tensor_tensor(last[:, :, :], start[:, :, :], mid(k.iota[0:ROWS, :], CH), ALU.mult))
                for c in range(CH):
                    done(nc.vector.tensor_tensor_scan(pos[:, c, :], zero[:, :], last[:, c, :], 0.0, ALU.add, ALU.max))
                done(nc.vector.tensor_tensor(last[:, :, :], dst, dst[:, :, P - 1:P].to_broadcast([ROWS, CH, P]), ALU.is_equal))
                done(nc.vector.tensor_scalar(slot[:, :, :], pos[:, :, :], -1.0, float(P - 1), ALU.mult, ALU.add))
                done(nc.vector.tensor_tensor(slot[:, :, :], slot[:, :, :], last[:, :, :], ALU.mult))
                done(nc.vector.tensor_tensor(slot[:, :, :], slot[:, :, :], pos[:, :, :], ALU.add))
                nc.vector.tensor_scalar(reset[:, 0, :, :], start[:, :, :], -BIG, None, ALU.mult)
                nc.vector.tensor_scalar(reset[:, 1, :, 0:P - 1], start[:, :, 1:P], -BIG, None, ALU.mult)
                nc.vector.memset(reset[:, 1, :, P - 1:P], -BIG)
                nc.vector.tensor_copy(ends[:, :, 0:1], dst[:, :, 0:1])
                nc.vector.tensor_copy(ends[:, :, 1:2], dst[:, :, P - 1:P])
                done(nc.vector.tensor_scalar(rel[:, :, :], typ, float(NP), None, ALU.mult))
                done(nc.vector.tensor_tensor(rel[:, :, :], rel[:, :, :], src, ALU.add))
                dve.sem_inc(s_rows, 1)
                dve.wait_ge(s_turn, 1)
                for out, n in ((k.slot, 0), (k.weight, 1), (k.other_idx, 2)) + (((k.start, 3), (k.key_idx, 4), (k.rel_idx, 5)) if k.attention else ()):
                    done(nc.vector.tensor_copy(out[:, :].rearrange("p (c t) -> p c t", c=CH), turned[n][:, :, 0:ROWS]))
                dve.wait_ge(s_key, 16)
                nc.vector.memset(k.keep[:, 0:1], 0.0)
                done(nc.vector.tensor_tensor(k.keep[:, 1:NBR], key[:, 1:NBR], key[:, 0:NBR - 1], ALU.is_equal))
                if k.attention:
                    nc.vector.tensor_scalar(k.cut[:, 0, :], k.keep[0:8, :], 1.0, BIG, ALU.subtract, ALU.mult)
                    nc.vector.memset(k.cut[:, 1, NBR - 1:NBR], -BIG)
                    done(nc.vector.tensor_scalar(k.cut[:, 1, 0:NBR - 1], k.keep[0:8, 1:NBR], 1.0, BIG, ALU.subtract, ALU.mult))

            @block.tensor
            def _(pe):
                pe.wait_ge(s_rows, 1)
                for n, q in enumerate((slot[:, :, :], wgt, src, start[:, :, :], dst, rel[:, :, :])):
                    for c in range(CH):
                        ins = nc.tensor.transpose(turned[n][:, c, 0:ROWS], q[:, c, :], k.ident[0:ROWS, 0:ROWS])
                ins.then_inc(s_turn, 1)

class Shared:

    def __init__(self, a):
        self.iota, self.ident, self.tri, self.tri_hi = (
            a.sb(n, [P, w]) for n, w in (("iota", P), ("ident", P), ("tri", P), ("tri_hi", NT)))
        self.ident_bf, self.zeros_bf = a.sb("ident_bf", [P, P], BF16), a.sb("zeros_bf", [P, P], BF16)
        self.ones = a.sb("ones", [P, P])
        self.mask, self.gate, self.inv_root = a.sb("mask", [P, NT * TYPES]), a.sb("gate", [P, NT]), a.sb("inv_root", [P, NT])


class Order:

    def __init__(self, k):
        self.iota, self.ident, self.tri, self.tri_hi = k.iota, k.ident, k.tri, k.tri_hi
        self.ident_bf, self.zeros_bf, self.ones = k.ident_bf, k.zeros_bf, k.ones
        self.mask, self.gate, self.inv_root = k.mask, k.gate, k.inv_root


def edge_order(nc, k, a, ins, tag, key, other, attention):
    o = Order(k)
    o.tag, o.attention = tag, attention
    o.slot, o.weight, o.other_idx = a.sb(tag + "slot", [P, TILES]), a.sb(tag + "weight", [P, TILES]), a.sb(tag + "other_idx", [P, TILES], I32)
    o.deg, o.sum_row = a.sb(tag + "deg", [P, NT]), a.sb(tag + "sum_row", [P, NT], I32)
    o.keep = a.sb(tag + "keep", [P, NBR])
    if attention:
        o.start = a.sb(tag + "start", [P, TILES])
        o.key_idx, o.rel_idx = (a.sb(tag + n, [P, TILES], I32) for n in ("key_idx", "rel_idx"))
        o.cut = a.sb(tag + "cut", [8, 2, NBR])
        o.resets = [{heads: nc.dram_tensor(f"{tag}resets{n}_{heads}", (TILES, heads, P), F32, kind="Internal").ap()
                     for heads in (8, 4)} for n in range(2)]
    o.key_pad = nc.dram_tensor(tag + "key_pad", (EP,), F32, kind="Internal").ap()
    o.rec_sorted = nc.dram_tensor(tag + "rec_sorted", (EP, 4), F32, kind="Internal").ap()
    o.ends = nc.dram_tensor(tag + "ends", (NBR,), F32, kind="Internal").ap()
    with ExitStack() as st:
        t = Names(nc, st)
        o.rec = t.sb(tag + "rec", [P, TILES, 4])
        o.key_col, o.hi_col, o.lo_col = (t.sb(tag + n, [P, TILES + GT]) for n in ("key_col", "hi_col", "lo_col"))
        o.first_pos = t.sb(tag + "first_pos", [NT, P])
        o.unsorted = t.sb(tag + "unsorted", [P, 1], I32)
        edge_columns(nc, o, other, key, ins["etype"], ins["weight"])
        degrees(nc, o)
        ranks(nc, o)
    edge_meta(nc, o)
    return o


def sum_edges(nc, k, tag, table, partial, weighted):
    with ExitStack() as st:
        a = Names(nc, st)
        got = a.sb(tag + "got", [P, 2, GT, D])
        hot = a.sb(tag + "hot", [P, 2, GT, P])
        sums = a.sb(tag + "sums", [P, 2, GT, D])
        idx = a.sb(tag + "idx", [P, 2, GT], I32)
        acc = [a.ps(f"{tag}acc{j}", [P, 512]) for j in range(GT)]
        s_got = [a.dma_sem(f"{tag}s_got{h}") for h in range(2)]
        s_out = [a.sem(f"{tag}s_out{h}") for h in range(2)]
        s_idx, s_seen, s_hot, s_v, s_acc, s_sums = (a.sem(tag + n) for n in ("s_idx", "s_seen", "s_hot", "s_v", "s_acc", "s_sums"))
        with nc.Block() as block:
            @block.gpsimd
            def _(pool):
                limit = pool.snap(pool.to_reg(NP - 1))

                def body(b):
                    for h in range(HALVES):
                        hold(pool, s_seen, s_acc, b * BODY + (h - 1) * GT)
                        nc.gpsimd.tensor_copy(idx[:, h, :], k.other_idx[:, bass.ds(b * BODY + h * GT, GT)]).then_inc(s_idx, 1)
                        hold(pool, s_seen, s_idx, b * 2 + (h + 1))
                        for j in range(GT):
                            pool.indirect_dma_start(got[:, h, j, :], None, table, bass.IndirectOffsetOnAxis(ap=idx[:, h, j:j + 1], axis=0),
                                                    bounds_check=limit, oob_is_err=False).then_inc(s_got[h], 16)
                repeat(pool, NB, body)

            @block.vector
            def _(dve):
                def body(b):
                    for h in range(HALVES):
                        cols = bass.ds(b * BODY + h * GT, GT)
                        wait(dve, s_acc, b * BODY + (h - 1) * GT)
                        ins = nc.vector.tensor_tensor(hot[:, h, :, :], mid(k.iota[:, :], GT), bcast(k.slot[:, cols], P), ALU.is_equal)
                        if weighted:
                            ins.then_inc(s_v, 1)
                            dve.wait_ge(s_v, b * 2 + (h + 1))
                            ins = nc.vector.tensor_tensor(hot[:, h, :, :], hot[:, h, :, :], bcast(k.weight[:, cols], P), ALU.mult)
                        ins.then_inc(s_hot, 1)
                repeat(dve, NB, body)

            @block.tensor
            def _(pe):
                def body(b):
                    for h in range(HALVES):
                        pe.wait_ge(s_hot, b * 2 + (h + 1))
                        pe.wait_ge(s_got[h], b * (16 * GT) + 16 * GT)
                        for j in range(GT):
                            wait(pe, s_sums, b * BODY + ((h - 1) * GT + j + 1))
                            nc.tensor.matmul(acc[j][:, 0:D], hot[:, h, j, :], got[:, h, j, :], start=True, stop=True).then_inc(s_acc, 1)
                repeat(pe, NB, body)

            @block.scalar
            def _(act):
                def body(b):
                    for h in range(HALVES):
                        wait(act, s_out[h], b * 16)
                        for j in range(GT):
                            act.wait_ge(s_acc, b * BODY + (h * GT + j + 1))
                            nc.scalar.copy(sums[:, h, j, :], acc[j][:, 0:D]).then_inc(s_sums, 1)
                repeat(act, NB, body)

            @block.sync
            def _(sp):
                def body(b):
                    for h in range(HALVES):
                        sp.wait_ge(s_sums, b * BODY + (h + 1) * GT)
                        sp.dma_start(partial[bass.ds(b * (BODY * P) + h * GT * P, GT * P), :].rearrange("(t s) w -> s t w", s=P),
                                     sums[:, h, :, :]).then_inc(s_out[h], 16)
                repeat(sp, NB, body)
                for h in range(HALVES):
                    sp.wait_ge(s_out[h], 16 * NB)


def attend_edges(nc, k, tag, table, main_idx, limit_rows, own, heads, scale, partial):
    W = D + 2 * heads
    dk = D // heads
    HT = GT * heads
    with ExitStack() as st:
        a = Names(nc, st)
        got = a.sb(tag + "got", [P, 2, GT, 2 * D])
        mine = a.sb(tag + "mine", [P, 2, GT, D])
        hot = a.sb(tag + "hot", [P, 2, GT, P])
        val = a.sb(tag + "val", [P, 2, GT, W])
        sums = a.sb(tag + "sums", [P, 2, GT, W])
        idx = a.sb(tag + "idx", [P, 2, 2, GT], I32)
        cuts = a.sb(tag + "cuts", [HT, 2, 2, P])
        score = a.sb(tag + "score", [P, 2, HT])
        diff = a.sb(tag + "diff", [P, 2, HT])
        run = a.sb(tag + "run", [HT, 2, P])
        segmax = a.sb(tag + "segmax", [HT, 2, P])
        acc = [a.ps(f"{tag}acc{j}", [P, 512]) for j in range(GT)]
        flip = a.ps(tag + "flip", [P, 4, P])
        s_got = [a.dma_sem(f"{tag}s_got{h}") for h in range(2)]
        s_out = [a.sem(f"{tag}s_out{h}") for h in range(2)]
        s_cut = [a.sem(f"{tag}s_cut{h}") for h in range(2)]
        s_idx, s_seen, s_v, s_read, s_score, s_flip, s_segmax, s_back, s_diff, s_exp, s_val, s_acc, s_sums = (
            a.sem(tag + "s_" + n) for n in ("idx", "seen", "v", "read", "score", "flip", "segmax", "back", "diff", "exp",
                                            "val", "acc", "sums"))
        with nc.Block() as block:
            @block.gpsimd
            def _(pool):
                limit = pool.snap(pool.to_reg(limit_rows - 1))
                own_limit = pool.snap(pool.to_reg(NP - 1))

                def body(b):
                    for h in range(HALVES):
                        cols = bass.ds(b * BODY + h * GT, GT)
                        hold(pool, s_seen, s_val, b * 2 + (h - 1))
                        nc.gpsimd.tensor_copy(idx[:, h, 0, :], main_idx[:, cols]).then_inc(s_idx, 1)
                        nc.gpsimd.tensor_copy(idx[:, h, 1, :], k.key_idx[:, cols]).then_inc(s_idx, 1)
                        hold(pool, s_seen, s_idx, b * 4 + (2 * h + 2))
                        for j in range(GT):
                            pool.indirect_dma_start(got[:, h, j, :], None, table, bass.IndirectOffsetOnAxis(ap=idx[:, h, 0, j:j + 1], axis=0),
                                                    bounds_check=limit, oob_is_err=False).then_inc(s_got[h], 16)
                            pool.indirect_dma_start(mine[:, h, j, :], None, own, bass.IndirectOffsetOnAxis(ap=idx[:, h, 1, j:j + 1], axis=0),
                                                    bounds_check=own_limit, oob_is_err=False).then_inc(s_got[h], 16)
                repeat(pool, NB, body)

            @block.sync
            def _(sp):
                def body(b):
                    for h in range(HALVES):
                        wait(sp, s_segmax, b * 2 + (h - 1))
                        for n in range(2):
                            sp.dma_start(cuts[:, h, n, :], k.resets[n][heads].rearrange("t h e -> (t h) e")[bass.ds(b * (BODY * heads) + h * GT * heads, HT), :]).then_inc(s_cut[h], 16)
                repeat(sp, NB, body)

            @block.vector
            def _(dve):
                PER = 2 * 8

                def body(b):
                    done = Chain(dve, s_v, b * PER)
                    for h in range(HALVES):
                        cols = bass.ds(b * BODY + h * GT, GT)
                        dve.wait_ge(s_got[h], b * (32 * GT) + 32 * GT)
                        done(nc.vector.tensor_tensor(mine[:, h, :, :], got[:, h, :, 0:D], mine[:, h, :, :], ALU.mult))
                        done(nc.vector.tensor_reduce(score[:, h, :], mine[:, h, :, :].rearrange("p t (h d) -> p (t h) d", d=dk), AX.X, ALU.add))
                        dve.sem_inc(s_score, 1)
                        wait(dve, s_acc, b * BODY + (h - 1) * GT)
                        done(nc.vector.tensor_tensor(hot[:, h, :, :], mid(k.iota[:, :], GT), bcast(k.slot[:, cols], P), ALU.is_equal))
                        dve.wait_ge(s_cut[h], b * 32 + 32)
                        dve.wait_ge(s_flip, b * 2 + (h + 1))
                        done(nc.vector.tensor_tensor_scan(run[:, h, :], cuts[:, h, 0, :], flip[0:HT, h, :], -BIG, ALU.add, ALU.max))
                        done(nc.vector.tensor_tensor_scan(segmax[:, h, ::-1], cuts[:, h, 1, ::-1], run[:, h, ::-1], -BIG, ALU.add, ALU.max))
                        dve.sem_inc(s_segmax, 1)
                        dve.wait_ge(s_back, b * 2 + (h + 1))
                        done(nc.vector.tensor_tensor(diff[:, h, :], score[:, h, :], flip[:, 2 + h, 0:HT], ALU.subtract))
                        dve.sem_inc(s_diff, 1)
                        done(nc.vector.tensor_tensor(val[:, h, :, D + heads:W], flip[:, 2 + h, 0:HT].rearrange("p (t h) -> p t h", h=heads),
                                                     bcast(k.start[:, cols], heads), ALU.mult))
                        dve.wait_ge(s_exp, b * 2 + (h + 1))
                        done(nc.vector.tensor_tensor(val[:, h, :, 0:D].rearrange("p t (h d) -> p t h d", d=dk),
                                                     got[:, h, :, D:2 * D].rearrange("p t (h d) -> p t h d", d=dk),
                                                     val[:, h, :, D:D + heads].unsqueeze(3).to_broadcast([P, GT, heads, dk]), ALU.mult))
                        dve.sem_inc(s_val, 1)
                    assert done.n == PER
                repeat(dve, NB, body)

            @block.tensor
            def _(pe):
                def products(b, h):
                    pe.wait_ge(s_val, b * 2 + (h + 1))
                    for j in range(GT):
                        wait(pe, s_sums, b * BODY + ((h - 1) * GT + j + 1))
                        nc.tensor.matmul(acc[j][:, 0:W], hot[:, h, j, :], val[:, h, j, :], start=True, stop=True).then_inc(s_acc, 1)

                def body(b):
                    for h in range(HALVES):
                        hold(pe, s_read, s_score, b * 2 + (h + 1))
                        nc.tensor.transpose(flip[0:HT, h, :], score[:, h, :], k.ident[:, :]).then_inc(s_flip, 1)
                        hold(pe, s_read, s_segmax, b * 2 + (h + 1))
                        nc.tensor.transpose(flip[:, 2 + h, 0:HT], segmax[:, h, :], k.ident[0:HT, 0:HT]).then_inc(s_back, 1)
                        products(b, h)
                repeat(pe, NB, body)

            @block.scalar
            def _(act):
                def body(b):
                    for h in range(HALVES):
                        act.wait_ge(s_diff, b * 2 + (h + 1))
                        nc.scalar.activation(val[:, h, :, D:D + heads], diff[:, h, :].rearrange("p (t h) -> p t h", h=heads),
                                             ACT.Exp, scale=scale).then_inc(s_exp, 1)
                        wait(act, s_out[h], b * 16)
                        for j in range(GT):
                            act.wait_ge(s_acc, b * BODY + (h * GT + j + 1))
                            nc.scalar.copy(sums[:, h, j, :], acc[j][:, 0:W]).then_inc(s_sums, 1)
                        act.wait_ge(s_sums, b * BODY + (h + 1) * GT)
                        act.dma_start(partial[bass.ds(b * (BODY * P) + h * GT * P, GT * P), :].rearrange("(t s) w -> s t w", s=P),
                                      sums[:, h, :, :]).then_inc(s_out[h], 16)
                repeat(act, NB, body)
                for h in range(HALVES):
                    act.wait_ge(s_out[h], 16 * NB)


def merge(nc, k, tag, partial, heads, scale):
    W = D + 2 * heads
    with ExitStack() as st:
        a = Names(nc, st)
        rows = a.sb(tag + "rows", [BR, BC, W])
        cols = a.sb(tag + "cols", [P, 2, NBR])
        total = a.sb(tag + "total", [P, 2, NBR])
        small = a.sb(tag + "small", [8, 6, NBR]) if heads else None
        pick = a.sb(tag + "pick", [8, 2, P]) if heads else None
        back = a.sb(tag + "back", [BR, BC, W])
        zero = a.sb(tag + "zero", [1, W])
        SPLIT = (4, BC - 4)
        turn = [a.ps(f"{tag}turn{n}", [P, 2, 512]) for n in range(4 if heads else 2)]
        s_load, s_zero, s_turn, s_cols, s_v, s_f, s_scaled, s_total, s_back, s_rows, s_store, s_pick, s_exp, s_fac = (
            a.sem(tag + n) for n in ("load", "zero", "turn", "cols", "v", "f", "scaled", "total", "back", "rows", "store", "pick", "exp", "fac"))

        def parts(n):
            return ((0, 0, SPLIT[0] * BR), (1, SPLIT[0] * BR, NBR))

        with nc.Block() as block:
            @block.gpsimd
            def _(pool):
                pool.memset(zero[:, :], 0.0).then_inc(s_zero, 1)
                if heads:
                    dk = D // heads
                    done = Chain(pool, s_pick)
                    done(pool.memset(pick[:, :, :], 1.0))
                    flat = pick[0:heads, :, :].rearrange("h f p -> h (f p)")
                    done(pool.affine_select(out=flat, in_=flat, compare_op=ALU.is_ge, fill=0.0, base=0,
                                            pattern=[[1, D]], channel_multiplier=-dk))
                    done(pool.affine_select(out=flat, in_=flat, compare_op=ALU.is_ge, fill=0.0, base=dk - 1,
                                            pattern=[[-1, D]], channel_multiplier=dk))

            @block.sync
            def _(sp):
                view = partial[0:EP, :].rearrange("(c t s) w -> t c s w", t=BR // 2, s=P)
                for n in range(2):
                    sp.dma_start(rows[n:BR:2, :, :], view[:, :, n * (P - 1), :]).then_inc(s_load, 16)
                sp.wait_ge(s_zero, 1)
                sp.dma_start(partial[ZERO_ROW:ZERO_ROW + 1, :], zero[:, :]).then_inc(s_store, 16)
                sp.wait_ge(s_rows, 1)
                sp.dma_start(partial[MERGED:MERGED + NBR, :].rearrange("(c p) w -> p c w", p=BR), back[:, :, :]).then_inc(s_store, 16)
                sp.wait_ge(s_store, 32)

            @block.tensor
            def _(pe):
                pe.wait_ge(s_load, 32)
                for n, (lo, hi) in enumerate(((0, P), (P, D)) + (((D, D + heads), (D + heads, W)) if heads else ())):
                    for c in range(BC):
                        col = (c % 4) * BR
                        ins = nc.tensor.transpose(turn[n][0:hi - lo, c // 4, col:col + BR], rows[:, c, lo:hi], k.ident[0:BR, 0:BR])
                ins.then_inc(s_turn, 1)
                if heads:
                    pe.wait_ge(s_pick, 3)
                    pe.wait_ge(s_exp, 1)
                    pe.wait_ge(s_cols, 1)
                    for f in range(2):
                        for bank, lo, hi in parts(f):
                            ins = nc.tensor.matmul(turn[f][:, bank, 0:hi - lo], pick[0:heads, f, :], small[0:heads, 5, lo:hi], start=True, stop=True)
                    ins.then_inc(s_fac, 1)
                pe.wait_ge(s_total, 1)
                for c in range(BC):
                    for f in range(2):
                        ins = nc.tensor.transpose(turn[f][0:BR, c // 4, (c % 4) * P:(c % 4 + 1) * P], total[:, f, c * BR:(c + 1) * BR], k.ident[:, :])
                    if heads:
                        ins = nc.tensor.transpose(turn[2][0:BR, c // 4, (c % 4) * P:(c % 4) * P + heads],
                                                  small[0:heads, 4, c * BR:(c + 1) * BR], k.ident[0:heads, 0:heads])
                ins.then_inc(s_back, 1)

            @block.scalar
            def _(act):
                if heads:
                    act.wait_ge(s_f, 1)
                    nc.scalar.activation(small[0:heads, 5, :], small[0:heads, 3, :], ACT.Exp, scale=scale).then_inc(s_exp, 1)

            @block.vector
            def _(dve):
                done = Chain(dve, s_v)
                dve.wait_ge(s_turn, 1)
                for f in range(2):
                    for bank, lo, hi in parts(f):
                        done(nc.vector.tensor_copy(cols[:, f, lo:hi], turn[f][:, bank, 0:hi - lo]))
                if heads:
                    z, m, run, top, zsum = (small[0:heads, n, :] for n in range(5))
                    for n, q in ((2, 0), (3, 1)):
                        for bank, lo, hi in parts(n):
                            done(nc.vector.tensor_copy(small[0:heads, q, lo:hi], turn[n][0:heads, bank, 0:hi - lo]))
                    dve.sem_inc(s_cols, 1)
                    done(nc.vector.tensor_scalar(run, z, 0.0, -BIG, ALU.is_equal, ALU.mult))
                    done(nc.vector.tensor_tensor(m, m, run, ALU.add))
                    done(nc.vector.tensor_tensor_scan(run, k.cut[0:heads, 0, :], m, -BIG, ALU.add, ALU.max))
                    done(nc.vector.tensor_tensor_scan(small[0:heads, 3, ::-1], k.cut[0:heads, 1, ::-1], small[0:heads, 2, ::-1], -BIG, ALU.add, ALU.max))
                    done(nc.vector.tensor_tensor(top, m, top, ALU.subtract))
                    dve.sem_inc(s_f, 1)
                    dve.wait_ge(s_exp, 1)
                    done(nc.vector.tensor_tensor(z, z, small[0:heads, 5, :], ALU.mult))
                    done(nc.vector.tensor_tensor_scan(zsum, k.keep[0:heads, :], z, 0.0, ALU.mult, ALU.add))
                    dve.wait_ge(s_fac, 1)
                    for f in range(2):
                        for bank, lo, hi in parts(f):
                            done(nc.vector.tensor_tensor(cols[:, f, lo:hi], cols[:, f, lo:hi], turn[f][:, bank, 0:hi - lo], ALU.mult))
                for f in range(2):
                    done(nc.vector.tensor_tensor_scan(total[:, f, :], k.keep[:, :], cols[:, f, :], 0.0, ALU.mult, ALU.add))
                dve.sem_inc(s_total, 1)
                if heads:
                    done(nc.vector.memset(back[:, :, D:W], 0.0))
                dve.wait_ge(s_back, 1)
                for bank in range(2):
                    c0, c1 = bank * 4, min(bank * 4 + 4, BC)
                    for f in range(2):
                        done(nc.vector.tensor_copy(back[:, c0:c1, f * P:(f + 1) * P],
                                                   turn[f][0:BR, bank, 0:(c1 - c0) * P].rearrange("p (c w) -> p c w", w=P)))
                    if heads:
                        done(nc.vector.tensor_copy(back[:, c0:c1, D:D + heads],
                                                   turn[2][0:BR, bank, 0:(c1 - c0) * P].rearrange("p (c w) -> p c w", w=P)[:, :, 0:heads]))
                dve.sem_inc(s_rows, 1)


def gather_sums(nc, k, tag, partial, W, sums):
    with ExitStack() as st:
        a = Names(nc, st)
        s_in = a.dma_sem(tag + "in")
        with nc.Block() as block:
            @block.gpsimd
            def _(pool):
                limit = pool.snap(pool.to_reg(PROWS - 1))
                for c in range(NT):
                    pool.indirect_dma_start(sums[:, c, 0:W], None, partial, bass.IndirectOffsetOnAxis(ap=k.sum_row[:, c:c + 1], axis=0),
                                            bounds_check=limit, oob_is_err=False).then_inc(s_in, 16)
                pool.wait_ge(s_in, 16 * NT)


def linear(nc, k, tag, source, chunks, weights, width, dest=None, relu=False, bias=None, types=1, stores=()):
    KC = chunks * types
    banks = -(-width // 512)
    with ExitStack() as st:
        a = Names(nc, st)
        turned = a.sb(tag + "turned", [P, 2, KC, P])
        masked = a.sb(tag + "masked", [P, 2, types, chunks * P])
        ring = a.sb(tag + "ring", [P, 2, width]) if dest is None else None
        flip = [a.ps(f"{tag}flip{n}", [P, max(KC * P, 512)]) for n in range(2)]
        acc = [a.ps(f"{tag}acc{n}", [P, 512 * banks]) for n in range(2)]
        s_mask, s_flip, s_turned, s_acc, s_out, s_seen = (a.sem(tag + n) for n in ("mask", "flip", "turned", "acc", "out", "seen"))
        s_store = [a.sem(f"{tag}store{n}") for n in range(2)]
        spans = [(lo, min(lo + 512, width)) for lo in range(0, width, 512)]
        def buf(j):
            return j % 2

        def before(j):
            return 1 if j == 0 else 2
        with nc.Block() as block:
            @block.tensor
            def _(pe):
                def body(b):
                    for j in range(NL):
                        n = buf(j)
                        c = b * NL + j
                        pe.wait_ge(s_mask, b * NL + (j + 1))
                        hold_at = b * NL + (j + 1 - before(j))
                        hold(pe, s_seen, s_turned, hold_at)
                        for q in range(KC):
                            last = nc.tensor.transpose(flip[n][:, q * P:(q + 1) * P],
                                                       masked[:, n, q // chunks, (q % chunks) * P:(q % chunks + 1) * P], k.ident[:, :])
                        last.then_inc(s_flip, 1)
                        pe.wait_ge(s_turned, b * NL + (j + 1))
                        wait(pe, s_out, b * NL + (j + 1 - before(j)))
                        for lo, hi in spans:
                            for q in range(KC):
                                last = nc.tensor.matmul(acc[n][:, lo:hi], turned[:, n, q, :], weights[:, q, lo:hi],
                                                        start=(q == 0), stop=(q == KC - 1 and bias is None))
                            if bias is not None:
                                last = nc.tensor.matmul(acc[n][:, lo:hi], k.ones[:, :], bias[:, lo:hi], start=False, stop=True)
                        last.then_inc(s_acc, 1)
                repeat(pe, NT // NL, body)

            @block.vector
            def _(dve):
                def body(b):
                    for j in range(NL):
                        c = b * NL + j
                        wait(dve, s_flip, b * NL + (j + 1 - before(j)))
                        if types > 1:
                            ins = nc.vector.tensor_tensor(masked[:, buf(j), :, :],
                                                          source[:, bass.ds(c, 1), :].to_broadcast([P, types, chunks * P]),
                                                          bcast(k.mask[:, bass.ds(c * types, types)], chunks * P), ALU.mult)
                        else:
                            ins = nc.vector.tensor_copy(masked[:, buf(j), :, :], source[:, bass.ds(c, 1), :])
                        ins.then_inc(s_mask, 1)
                repeat(dve, NT // NL, body)

            @block.scalar
            def _(act):
                def body(b):
                    for j in range(NL):
                        n = buf(j)
                        c = b * NL + j
                        act.wait_ge(s_flip, b * NL + (j + 1))
                        wait(act, s_acc, b * NL + (j + 1 - before(j)))
                        nc.scalar.copy(turned[:, n, :, :].rearrange("p q w -> p (q w)"), flip[n][:, 0:KC * P]).then_inc(s_turned, 1)
                        act.wait_ge(s_acc, b * NL + (j + 1))
                        if dest is None:
                            used = 3 if n == 0 else 2
                            wait(act, s_store[n], (b * used + j // 2) * (16 * len(stores)))
                            out = ring[:, n, :]
                        else:
                            out = dest[:, bass.ds(c, 1), 0:width].rearrange("p o w -> p (o w)")
                        nc.scalar.activation(out, acc[n][:, 0:width], ACT.Relu if relu else ACT.Copy).then_inc(s_out, 1)
                repeat(act, NT // NL, body)

            @block.sync
            def _(sp):
                def body(b):
                    for j in range(NL):
                        if stores:
                            sp.wait_ge(s_out, b * NL + (j + 1))
                        for table, col, lo, w in stores:
                            if dest is None:
                                data = ring[:, buf(j), lo:lo + w]
                            else:
                                data = dest[:, bass.ds(b * NL + j, 1), lo:lo + w].rearrange("p o w -> p (o w)")
                            sp.dma_start(table[bass.ds(b * (NL * P) + j * P, P), col:col + w], data).then_inc(s_store[buf(j)], 16)
                if stores:
                    repeat(sp, NT // NL, body)
                    for n in range(2):
                        sp.wait_ge(s_store[n], 16 * len(stores) * (NT // NL) * (3 if n == 0 else 2))


def normalise(nc, k, tag, y, tmp, eps, scale=None, offset=None, add=None):
    with ExitStack() as st:
        a = Names(nc, st)
        mean, var = a.sb(tag + "mean", [P, NT]), a.sb(tag + "var", [P, NT])
        s_v, s_var, s_std = (a.sem(tag + n) for n in ("v", "sv", "std"))
        with nc.Block() as block:
            @block.vector
            def _(dve):
                done = Chain(dve, s_v)
                done(nc.vector.tensor_reduce(mean[:, :], y, AX.X, ALU.add))
                done(nc.vector.tensor_scalar(mean[:, :], mean[:, :], 1.0 / D, None, ALU.mult))
                done(nc.vector.tensor_tensor(y, y, bcast(mean[:, :], D), ALU.subtract))
                done(nc.vector.tensor_tensor(tmp, y, y, ALU.mult))
                done(nc.vector.tensor_reduce(var[:, :], tmp, AX.X, ALU.add))
                done(nc.vector.tensor_scalar(var[:, :], var[:, :], 1.0 / D, eps, ALU.mult, ALU.add))
                dve.sem_inc(s_var, 1)
                dve.wait_ge(s_std, 1)
                done(nc.vector.reciprocal(var[:, :], mean[:, :]))
                done(nc.vector.tensor_tensor(y, y, bcast(var[:, :], D), ALU.mult))
                if scale is not None:
                    done(nc.vector.tensor_tensor(y, y, mid(scale, NT), ALU.mult))
                    done(nc.vector.tensor_tensor(y, y, mid(offset, NT), ALU.add))
                if add is not None:
                    done(nc.vector.tensor_tensor(y, y, add, ALU.add))

            @block.scalar
            def _(act):
                act.wait_ge(s_var, 1)
                nc.scalar.activation(mean[:, :], var[:, :], ACT.Sqrt).then_inc(s_std, 1)


def vector_steps(nc, k, tag, steps):
    with ExitStack() as st:
        a = Names(nc, st)
        s_v = a.sem(tag + "v")
        with nc.Block() as block:
            @block.vector
            def _(dve):
                done = Chain(dve, s_v)
                for step in steps:
                    done(step())


def zero_fill(nc, k, tag, *tensors):
    with ExitStack() as st:
        s_fill = Names(nc, st).sem(tag + "fill")
        with nc.Block() as block:
            @block.vector
            def _(dve):
                for t in tensors:
                    nc.vector.memset(t[:, :], 0.0).then_inc(s_fill, 1)


def copies(nc, k, tag, moves):
    with ExitStack() as st:
        a = Names(nc, st)
        s_dma = a.sem(tag + "dma")
        with nc.Block() as block:
            @block.sync
            def _(sp):
                for out, src in moves:
                    sp.dma_start(out, src).then_inc(s_dma, 16)
                sp.wait_ge(s_dma, 16 * len(moves))


def relate(nc, k, tag, kv, weights, table):
    with ExitStack() as st:
        a = Names(nc, st)
        rows = a.sb(tag + "rows", [P, 2, 2 * D])
        turned = a.sb(tag + "turned", [P, 2, 4 * P])
        ring = a.sb(tag + "ring", [P, 2, RELS, 2 * D])
        flip = [a.ps(f"{tag}flip{n}", [P, 512]) for n in range(2)]
        acc = [a.ps(f"{tag}acc{n}", [P, RELS * P]) for n in range(2)]
        s_load = [a.sem(f"{tag}load{n}") for n in range(2)]
        s_store = [a.dma_sem(f"{tag}store{n}") for n in range(2)]
        s_flip, s_turned, s_seen, s_seen2 = (a.sem(tag + n) for n in ("s_flip", "s_turned", "seen", "seen2"))
        s_acc = [a.sem(f"{tag}acc_s{n}") for n in range(2)]
        s_out = [a.sem(f"{tag}out{n}") for n in range(2)]

        def before(j):
            return 1 if j == 0 else 2

        def copied(eng, copy, b, side):
            for j in range(NL):
                n = j % 2
                used = 3 if n == 0 else 2
                wait(eng, s_store[n], (b * used + j // 2) * 16)
                for q in (side, side + 2):
                    eng.wait_ge(s_acc[side], b * (2 * NL) + (2 * j + q // 2 + 1))
                    copy(ring[:, n, :, q * P:(q + 1) * P], acc[side][:, :].rearrange("p (r w) -> p r w", w=P)).then_inc(s_out[side], 1)

        with nc.Block() as block:
            @block.sync
            def _(sp):
                def body(b):
                    for j in range(NL):
                        wait(sp, s_flip, b * NL + (j + 1 - before(j)))
                        sp.dma_start(rows[:, j % 2, :], kv[bass.ds(b * (NL * P) + j * P, P), :]).then_inc(s_load[j % 2], 16)
                repeat(sp, NT // NL, body)

            @block.gpsimd
            def _(pool):
                def body(b):
                    for j in range(NL):
                        for side in range(2):
                            hold(pool, s_seen, s_out[side], b * (2 * NL) + 2 * (j + 1))
                        pool.dma_start(table.rearrange("(r n) w -> n r w", r=RELS)[bass.ds(b * (NL * P) + j * P, P), :, :],
                                       ring[:, j % 2, :, :]).then_inc(s_store[j % 2], 16)
                repeat(pool, NT // NL, body)
                for n in range(2):
                    pool.wait_ge(s_store[n], 16 * (NT // NL) * (3 if n == 0 else 2))

            @block.tensor
            def _(pe):
                def body(b):
                    for j in range(NL):
                        n = j % 2
                        used = 3 if n == 0 else 2
                        wait(pe, s_turned, b * NL + (j + 1 - before(j)))
                        hold(pe, s_seen2, s_load[n], (b * used + j // 2) * 16 + 16)
                        for q in range(4):
                            last = nc.tensor.transpose(flip[n][:, q * P:(q + 1) * P], rows[:, n, q * P:(q + 1) * P], k.ident[:, :])
                        last.then_inc(s_flip, 1)
                        pe.wait_ge(s_turned, b * NL + (j + 1))
                        for q in range(4):
                            wait(pe, s_out[q % 2], b * (2 * NL) + (2 * j + q // 2))
                            for lo in range(0, RELS * P, 512):
                                last = nc.tensor.matmul(acc[q % 2][:, lo:lo + 512], turned[:, n, q * P:(q + 1) * P],
                                                        weights[:, q, lo:lo + 512], start=True, stop=True)
                            last.then_inc(s_acc[q % 2], 1)
                repeat(pe, NT // NL, body)

            @block.scalar
            def _(act):
                def body(b):
                    for j in range(NL):
                        act.wait_ge(s_flip, b * NL + (j + 1))
                        wait(act, s_acc[1], b * (2 * NL) + 2 * (j + 1 - before(j)))
                        nc.scalar.copy(turned[:, j % 2, :], flip[j % 2][:, :]).then_inc(s_turned, 1)
                        n = j % 2
                        wait(act, s_store[n], (b * (3 if n == 0 else 2) + j // 2) * 16)
                        for q in (0, 2):
                            act.wait_ge(s_acc[0], b * (2 * NL) + (2 * j + q // 2 + 1))
                            nc.scalar.copy(ring[:, n, :, q * P:(q + 1) * P], acc[0][:, :].rearrange("p (r w) -> p r w", w=P)).then_inc(s_out[0], 1)
                repeat(act, NT // NL, body)

            @block.vector
            def _(dve):
                repeat(dve, NT // NL, lambda b: copied(dve, nc.vector.tensor_copy, b, 1))


def relation_weights(nc, k, a, ins, out):
    dk = D // 4
    with ExitStack() as st:
        t = Names(nc, st)
        att = t.sb("rw_att", [P, 2, RELS, P])
        pri = t.sb("rw_pri", [P, 2 * RELS])
        flip = t.ps("rw_flip", [P, 2 * RELS, P])
        s_zero, s_load, s_flip, s_v = (t.sem("rw_" + n) for n in ("zero", "load", "flip", "v"))
        with nc.Block() as block:
            @block.gpsimd
            def _(pool):
                pool.memset(att[:, :, :, :], 0.0).then_inc(s_zero, 1)
                pool.memset(out[:, 2:4, :], 0.0).then_inc(s_zero, 1)

            @block.sync
            def _(sp):
                sp.wait_ge(s_zero, 2)
                for kc in range(2):
                    for h2 in range(2):
                        lo, hi = h2 * dk, (h2 + 1) * dk
                        sp.dma_start(att[lo:hi, kc, :, lo:hi], ins["relation_att"][:, 2 * kc + h2].rearrange("r d e -> d r e")).then_inc(s_load, 16)
                        sp.dma_start(out[lo:hi, 2 + kc, :].rearrange("p (r e) -> p r e", e=P)[:, :, lo:hi],
                                     ins["relation_msg"][:, 2 * kc + h2].rearrange("r d e -> d r e")).then_inc(s_load, 16)
                        with nc.allow_non_contiguous_dma("32 values"):
                            sp.dma_start(pri[lo:hi, kc * RELS:(kc + 1) * RELS],
                                         ins["relation_pri"][:, 2 * kc + h2].partition_broadcast(dk)).then_inc(s_load, 16)
                sp.wait_ge(s_load, 16 * 12)

            @block.tensor
            def _(pe):
                pe.wait_ge(s_load, 16 * 12)
                for kc in range(2):
                    for r in range(RELS):
                        last = nc.tensor.transpose(flip[:, kc * RELS + r, :], att[:, kc, r, :], k.ident[:, :])
                last.then_inc(s_flip, 1)

            @block.vector
            def _(dve):
                done = Chain(dve, s_v)
                dve.wait_ge(s_load, 16 * 12)
                done(nc.vector.tensor_scalar(pri[:, :], pri[:, :], float(dk) ** -0.5, None, ALU.mult))
                dve.wait_ge(s_flip, 1)
                done(nc.vector.tensor_tensor(out[:, 0:2, :].rearrange("p c (r w) -> p (c r) w", w=P), flip[:, :, :],
                                             bcast(pri[:, :], P), ALU.mult))


def node_constants(nc, k, ins):
    with ExitStack() as st:
        a = Names(nc, st)
        rows = a.sb("nc_rows", [NT, P], I32)
        rows_f = a.sb("nc_rows_f", [NT, P])
        kind = a.ps("nc_kind", [P, 512])
        gate = a.sb("nc_gate", [P, NT, TYPES])
        skip = a.sb("nc_skip", [P, TYPES])
        root = a.sb("nc_root", [P, NT])
        some = a.sb("nc_some", [P, NT])
        s_pad, s_load, s_v, s_row, s_kind, s_deg, s_root, s_exp = (a.sem("nc_" + n) for n in ("pad", "load", "v", "row", "skind", "deg", "sroot", "exp"))
        full = N_NODES // P
        with nc.Block() as block:
            @block.gpsimd
            def _(pool):
                pool.memset(rows[:, :], 0).then_inc(s_pad, 1)

            @block.sync
            def _(sp):
                sp.wait_ge(s_pad, 1)
                sp.dma_start(rows[0:full, :], ins["node_type"][0:full * P].rearrange("(t n) -> t n", n=P)).then_inc(s_load, 16)
                sp.dma_start(rows[full:full + 1, 0:N_NODES - full * P], ins["node_type"][full * P:N_NODES].rearrange("(t n) -> t n", t=1)).then_inc(s_load, 16)
                sp.dma_start(skip[:, :], ins["skip"].partition_broadcast(P)).then_inc(s_load, 16)

            @block.tensor
            def _(pe):
                pe.wait_ge(s_row, 1)
                nc.tensor.transpose(kind[:, 0:NT], rows_f[:, :], k.ident[0:NT, 0:NT]).then_inc(s_kind, 1)

            @block.scalar
            def _(act):
                act.wait_ge(s_load, 48)
                nc.scalar.activation(skip[:, :], skip[:, :], ACT.Exp, scale=-1.0).then_inc(s_exp, 1)
                act.wait_ge(s_deg, 1)
                nc.scalar.activation(root[:, :], some[:, :], ACT.Sqrt).then_inc(s_root, 1)

            @block.vector
            def _(dve):
                done = Chain(dve, s_v)
                dve.wait_ge(s_load, 48)
                done(nc.vector.tensor_copy(rows_f[:, :], rows[:, :]))
                dve.sem_inc(s_row, 1)
                done(nc.vector.tensor_scalar(some[:, :], k.deg[:, :], 1.0, None, ALU.max))
                dve.sem_inc(s_deg, 1)
                dve.wait_ge(s_exp, 1)
                done(nc.vector.tensor_scalar(skip[:, :], skip[:, :], 1.0, None, ALU.add))
                done(nc.vector.reciprocal(skip[:, :], skip[:, :]))
                dve.wait_ge(s_kind, 1)
                mask = k.mask[:, :].rearrange("p (c t) -> p c t", t=TYPES)
                for t in range(TYPES):
                    done(nc.vector.tensor_scalar(mask[:, :, t], kind[:, 0:NT], float(t), None, ALU.is_equal))
                done(nc.vector.tensor_tensor(gate[:, :, :], mask, mid(skip[:, :], NT), ALU.mult))
                done(nc.vector.tensor_reduce(k.gate[:, :], gate[:, :, :], AX.X, ALU.add))
                dve.wait_ge(s_root, 1)
                done(nc.vector.reciprocal(k.inv_root[:, :], root[:, :]))
                done(nc.vector.tensor_scalar(some[:, :], k.deg[:, :], 0.0, None, ALU.is_gt))
                done(nc.vector.tensor_tensor(k.inv_root[:, :], k.inv_root[:, :], some[:, :], ALU.mult))


def head_average(nc, k, tag, sums, out, heads):
    dk = D // heads

    def per_head(ap):
        return ap.rearrange("p c (h d) -> p c h d", d=dk)
    z = sums[:, :, D:D + heads]
    vector_steps(nc, k, tag, [
        lambda: nc.vector.tensor_scalar(z, z, 1e-16, None, ALU.max),
        lambda: nc.vector.reciprocal(z, z),
        lambda: nc.vector.tensor_tensor(per_head(out[:, :, 0:D]), per_head(sums[:, :, 0:D]),
                                        z.unsqueeze(3).to_broadcast([P, NT, heads, dk]), ALU.mult)])


def program(nc, ins, out):
    WMAX = D + 16
    full = N_NODES // P
    with ExitStack() as st:
        a = Names(nc, st)
        k = Shared(a)
        constants(nc, k)
        into = edge_order(nc, k, a, ins, "into_", ins["dst"], ins["src"], True)
        outof = edge_order(nc, k, a, ins, "outof_", ins["src"], ins["dst"], False)
        node_constants(nc, into, ins)
        bufs = [a.sb(f"nodes{n}", [P, NT, WMAX]) for n in range(3)]
        X, H, S = (b[:, :, 0:D] for b in bufs)

        def table(name, rows, width):
            return nc.dram_tensor(name, (rows, width), F32, kind="Internal").ap()

        def node_rows(t):
            return t.rearrange("(c p) w -> p c w", p=P)

        vector_steps(nc, k, "x0", [lambda: nc.vector.memset(X[:, full, :], 0.0)])
        copies(nc, k, "xl", [(X[:, 0:full, :], node_rows(ins["x"][0:full * P, :])),
                             (X[0:N_NODES - full * P, full, :], ins["x"][full * P:N_NODES, :])])

        t0, p0 = table("t0", NP, D), table("p0", PROWS, D)
        vector_steps(nc, k, "l0a", [lambda: nc.vector.tensor_tensor(H, X, bcast(k.inv_root[:, :], D), ALU.mult)])
        copies(nc, k, "l0b", [(node_rows(t0), H)])
        sum_edges(nc, into, "l0c", t0, p0, False)
        merge(nc, into, "l0d", p0, 0, None)
        gather_sums(nc, into, "l0e", p0, D, bufs[2])
        vector_steps(nc, k, "l0f", [lambda: nc.vector.tensor_tensor(S, S, bcast(k.inv_root[:, :], D), ALU.mult)])
        with ExitStack() as ws:
            w = Names(nc, ws).sb("l0w", [P, 2, D])
            copies(nc, k, "l0g", [(w[:, :, :], ins["W0"].rearrange("(q p) n -> p q n", p=P))])
            linear(nc, k, "l0h", S, 2, w, D, dest=H)
        vector_steps(nc, k, "l0i", [lambda: nc.vector.tensor_tensor(X, X, H, ALU.add)])
        normalise(nc, k, "l0j", X, H, 1e-5)

        t1, p1 = table("t1", NP, D), table("p1", PROWS, D)
        copies(nc, k, "l1a", [(node_rows(t1), X)])
        sum_edges(nc, outof, "l1b", t1, p1, True)
        merge(nc, outof, "l1c", p1, 0, None)
        gather_sums(nc, outof, "l1d", p1, D, bufs[2])
        with ExitStack() as ws:
            w = Names(nc, ws)
            w1, w2 = w.sb("l1w1", [P, 2, D]), w.sb("l1w2", [P, 2, D])
            b1, b2 = w.sb("l1b1", [P, D]), w.sb("l1b2", [P, D])
            eps, scale, offset = w.sb("l1eps", [P, 1]), w.sb("l1scale", [P, D]), w.sb("l1offset", [P, D])
            zero_fill(nc, k, "l1z", b1, b2)
            copies(nc, k, "l1e", [(w1[:, :, :], ins["W1"].rearrange("(q p) n -> p q n", p=P)),
                                  (w2[:, :, :], ins["W2"].rearrange("(q p) n -> p q n", p=P)),
                                  (b1[0:1, :], ins["b1"].rearrange("(a n) -> a n", a=1)), (b2[0:1, :], ins["b2"].rearrange("(a n) -> a n", a=1)),
                                  (eps[:, :], ins["eps"].partition_broadcast(P)), (scale[:, :], ins["scale"].partition_broadcast(P)),
                                  (offset[:, :], ins["offset"].partition_broadcast(P))])
            vector_steps(nc, k, "l1f", [
                lambda: nc.vector.tensor_scalar(eps[:, :], eps[:, :], 1.0, None, ALU.add),
                lambda: nc.vector.scalar_tensor_tensor(out=S, in0=X, scalar=eps[:, 0:1], in1=S, op0=ALU.mult, op1=ALU.add)])
            linear(nc, k, "l1g", S, 2, w1, D, dest=H, relu=True, bias=b1)
            linear(nc, k, "l1h", H, 2, w2, D, dest=S, relu=True, bias=b2)
            normalise(nc, k, "l1i", S, H, 1e-10, scale=scale[:, :], offset=offset[:, :], add=X)
        normalise(nc, k, "l1j", S, H, 1e-5)
        bufs = [bufs[2], bufs[1], bufs[0]]
        X, H, S = (b[:, :, 0:D] for b in bufs)

        qv2, k2, p2 = table("qv2", NP, 2 * D), table("k2", NP, D), table("p2", PROWS, D + 16)
        with ExitStack() as ws:
            w = Names(nc, ws)
            wq, bq = w.sb("l2w", [P, 2, 3 * D]), w.sb("l2b", [P, 3 * D])
            zero_fill(nc, k, "l2z", bq)
            copies(nc, k, "l2a", [m for n, (wt, bt) in enumerate(((ins["Wq"], ins["bq"]), (ins["Wv"], ins["bv"]), (ins["Wk"], ins["bk"])))
                                  for m in ((wq[:, :, n * D:(n + 1) * D], wt.rearrange("(q p) n -> p q n", p=P)),
                                            (bq[0:1, n * D:(n + 1) * D], bt.rearrange("(a n) -> a n", a=1)))])
            linear(nc, k, "l2b", X, 2, wq, 3 * D, bias=bq, stores=((qv2, 0, 0, 2 * D), (k2, 0, 2 * D, D)))
        attend_edges(nc, into, "l2c", qv2, into.other_idx, NP, k2, 8, 32.0 ** -0.5, p2)
        merge(nc, into, "l2d", p2, 8, 32.0 ** -0.5)
        gather_sums(nc, into, "l2e", p2, D + 16, bufs[2])
        head_average(nc, k, "l2f", bufs[2], bufs[1], 8)
        vector_steps(nc, k, "l2g", [lambda: nc.vector.tensor_tensor(X, X, H, ALU.add)])
        normalise(nc, k, "l2h", X, H, 1e-5)

        kv3, q3 = table("kv3", NP, 2 * D), table("q3", NP, D)
        r3, p3 = table("r3", RELS * NP, 2 * D), table("p3", PROWS, D + 8)
        with ExitStack() as ws:
            w3 = Names(nc, ws).sb("l3w", [P, 2 * TYPES, 3 * D])
            copies(nc, k, "l3a", [(w3[:, 2 * t:2 * t + 2, n * D:(n + 1) * D], wt[t].rearrange("(q p) n -> p q n", p=P))
                                  for n, wt in enumerate((ins["k_linears"], ins["v_linears"], ins["q_linears"])) for t in range(TYPES)])
            linear(nc, k, "l3b", X, 2, w3, 3 * D, types=TYPES, stores=((kv3, 0, 0, 2 * D), (q3, 0, 2 * D, D)))
        with ExitStack() as ws:
            wr = Names(nc, ws).sb("l3r", [P, 4, RELS * P])
            relation_weights(nc, k, a, ins, wr)
            relate(nc, k, "l3c", kv3, wr, r3)
        attend_edges(nc, into, "l3d", r3, into.rel_idx, RELS * NP, q3, 4, 1.0, p3)
        merge(nc, into, "l3e", p3, 4, 1.0)
        gather_sums(nc, into, "l3f", p3, D + 8, bufs[2])
        head_average(nc, k, "l3g", bufs[2], bufs[1], 4)
        with ExitStack() as ws:
            wa = Names(nc, ws).sb("l3wa", [P, 2 * TYPES, D])
            copies(nc, k, "l3h", [(wa[:, 2 * t:2 * t + 2, :], ins["a_linears"][t].rearrange("(q p) n -> p q n", p=P)) for t in range(TYPES)])
            linear(nc, k, "l3i", H, 2, wa, D, dest=S, types=TYPES)
        vector_steps(nc, k, "l3j", [lambda: nc.vector.tensor_tensor(S, S, bcast(k.gate[:, :], D), ALU.mult),
                                    lambda: nc.vector.tensor_tensor(X, X, S, ALU.add)])
        normalise(nc, k, "l3k", X, H, 1e-5)
        copies(nc, k, "l3l", [(node_rows(out[0:full * P, :]), X[:, 0:full, :]),
                              (out[full * P:N_NODES, :], X[0:N_NODES - full * P, full, :])])


_INS = {"x": "x", "src": "src", "dst": "dst", "edge_type_8": "etype", "edge_weight": "weight", "node_type_4": "node_type",
        "L0_gnn_W": "W0", "L1_gnn_W1": "W1", "L1_gnn_b1": "b1", "L1_gnn_W2": "W2", "L1_gnn_b2": "b2", "L1_gnn_eps": "eps",
        "L1_gnn_offset": "offset", "L1_gnn_scale": "scale", "L2_gnn_Wq": "Wq", "L2_gnn_bq": "bq", "L2_gnn_Wk": "Wk",
        "L2_gnn_bk": "bk", "L2_gnn_Wv": "Wv", "L2_gnn_bv": "bv", "L3_gnn_k_linears": "k_linears",
        "L3_gnn_q_linears": "q_linears", "L3_gnn_v_linears": "v_linears", "L3_gnn_a_linears": "a_linears",
        "L3_gnn_relation_att": "relation_att", "L3_gnn_relation_msg": "relation_msg",
        "L3_gnn_relation_pri": "relation_pri", "L3_gnn_skip": "skip"}


def kernel(x, src, dst, edge_type_8, edge_weight, node_type_4, L0_gnn_W, L1_gnn_W1, L1_gnn_b1, L1_gnn_W2, L1_gnn_b2,
           L1_gnn_eps, L1_gnn_offset, L1_gnn_scale, L2_gnn_Wq, L2_gnn_bq, L2_gnn_Wk, L2_gnn_bk, L2_gnn_Wv, L2_gnn_bv,
           L3_gnn_k_linears, L3_gnn_q_linears, L3_gnn_v_linears, L3_gnn_a_linears, L3_gnn_relation_att,
           L3_gnn_relation_msg, L3_gnn_relation_pri, L3_gnn_skip):
    import numpy as _np
    import concourse.bacc as _bacc
    from concourse.bass_utils import run_bass_kernel_spmd as _run

    given = dict(x=x, src=src, dst=dst, edge_type_8=edge_type_8, edge_weight=edge_weight, node_type_4=node_type_4,
                 L0_gnn_W=L0_gnn_W, L1_gnn_W1=L1_gnn_W1, L1_gnn_b1=L1_gnn_b1, L1_gnn_W2=L1_gnn_W2, L1_gnn_b2=L1_gnn_b2,
                 L1_gnn_eps=L1_gnn_eps, L1_gnn_offset=L1_gnn_offset, L1_gnn_scale=L1_gnn_scale, L2_gnn_Wq=L2_gnn_Wq,
                 L2_gnn_bq=L2_gnn_bq, L2_gnn_Wk=L2_gnn_Wk, L2_gnn_bk=L2_gnn_bk, L2_gnn_Wv=L2_gnn_Wv, L2_gnn_bv=L2_gnn_bv,
                 L3_gnn_k_linears=L3_gnn_k_linears, L3_gnn_q_linears=L3_gnn_q_linears, L3_gnn_v_linears=L3_gnn_v_linears,
                 L3_gnn_a_linears=L3_gnn_a_linears, L3_gnn_relation_att=L3_gnn_relation_att,
                 L3_gnn_relation_msg=L3_gnn_relation_msg, L3_gnn_relation_pri=L3_gnn_relation_pri, L3_gnn_skip=L3_gnn_skip)
    nc = _bacc.Bacc("TRN2", target_bir_lowering=False, num_devices=1)
    arrays, aps = {}, {}
    for name, short in _INS.items():
        v = _np.ascontiguousarray(given[name])
        arrays["in_" + name] = v
        aps[short] = nc.dram_tensor("in_" + name, v.shape, mybir.dt.from_np(v.dtype), kind="ExternalInput").ap()
    out = nc.dram_tensor("out_0", (N_NODES, D), F32, kind="ExternalOutput").ap()
    program(nc, aps, out)
    r = _run(nc, [arrays], core_ids=[0])
    return r.results[0]["out_0"]
```

```python
import concourse.bass as bass
from concourse import mybir
from contextlib import ExitStack

F32 = mybir.dt.float32
BF16 = mybir.dt.bfloat16
F16 = mybir.dt.float16
I32 = mybir.dt.int32
ALU = mybir.AluOpType
ACT = mybir.ActivationFunctionType
AX = mybir.AxisListType

P = 128
D = 256
N_NODES, N_EDGES = 3125, 50000
NT = -(-N_NODES // P)
NP = NT * P
PAD_NODE = NP - 1
GT = 7
HALVES = 2
BODY = GT * HALVES
NB = -(-N_EDGES // (P * BODY))
TILES = NB * BODY
EP = TILES * P
CH = 4
ROWS = TILES // CH
NBR = 2 * TILES
BC = 7
BR = NBR // BC
MERGED = EP
ZERO_ROW = EP + NBR
PROWS = ZERO_ROW + 1
NL = 5
PAIR_BLOCKS = -(-(NP + TILES) // P) + 1
PAIRS = PAIR_BLOCKS * P
BIG = 1.0e30
RELS, TYPES = 8, 4
assert ROWS * CH == TILES and BR * BC == NBR and NT % NL == 0


class Chain:

    def __init__(self, eng, sem, base=0):
        self.eng, self.sem, self.base, self.n = eng, sem, base, 0

    def __call__(self, ins):
        self.n += 1
        ins.then_inc(self.sem, 1)
        self.eng.wait_ge(self.sem, self.base + self.n)


def wait(eng, sem, value):
    if isinstance(value, int) and value <= 0:
        return
    eng.wait_ge(sem, value)


def hold(eng, seen, sem, value):
    wait(eng, sem, value)
    eng.sem_inc(seen, 1)


def repeat(eng, count, body):
    body(0)
    if count > 1:
        with eng.Fori(1, count) as b:
            body(b)


class Names:

    def __init__(self, nc, stack):
        self.nc, self.stack = nc, stack

    def sb(self, name, shape, dt=F32):
        return self.stack.enter_context(self.nc.sbuf_tensor(name, shape, dt))

    def ps(self, name, shape, dt=F32):
        return self.stack.enter_context(self.nc.psum_tensor(name, shape, dt))

    def sem(self, name):
        handle = self.nc.alloc_semaphore(name=name)
        self.stack.callback(self.nc.release_semaphore, handle)
        self.stack.callback(self.nc.gpsimd.sem_clear, handle)
        return handle


    def dma_sem(self, name):
        return self.nc.alloc_semaphore(name=name)


def node_tiles(eng, step):
    def body(b):
        for n in range(2):
            step(b * 2 + n, n, b)
    repeat(eng, NT // 2, body)
    for c in range(NT // 2 * 2, NT):
        step(c, 0, NT // 2)


def repeat_between(eng, count, body):
    body(0)
    with eng.Fori(1, count - 1) as b:
        body(b)
    body(count - 1)


def bcast(ap, count):
    return ap.unsqueeze(2).to_broadcast([ap.shape[0], ap.shape[1], count])


def mid(ap, count):
    return ap.unsqueeze(1).to_broadcast([ap.shape[0], count, ap.shape[1]])


def constants(nc, k):
    with ExitStack() as st:
        a = Names(nc, st)
        s_fill = a.sem("c_fill")
        with nc.Block() as block:
            @block.gpsimd
            def _(pool):
                done = Chain(pool, s_fill)
                nc.gpsimd.iota(k.iota[:, :], [[1, P]], base=0, channel_multiplier=0,
                               allow_small_or_imprecise_dtypes=True)
                pool.memset(k.ident[:, :], 0.0)
                pool.memset(k.tri[:, :], 1.0)
                pool.memset(k.zeros_bf[:, :], 0.0)
                pool.memset(k.ones[:, :], 1.0)
                done(pool.memset(k.tri_hi[:, :], 1.0))
                pool.affine_select(out=k.ident[:, :], in_=k.ident[:, :], compare_op=ALU.not_equal, fill=1.0,
                                   base=0, pattern=[[-1, P]], channel_multiplier=1)
                pool.affine_select(out=k.tri[:, :], in_=k.tri[:, :], compare_op=ALU.is_gt, fill=0.0,
                                   base=0, pattern=[[-1, P]], channel_multiplier=1)
                done(pool.affine_select(out=k.tri_hi[:, :], in_=k.tri_hi[:, :], compare_op=ALU.is_gt, fill=0.0,
                                        base=0, pattern=[[1, P]], channel_multiplier=-1))
                nc.gpsimd.iota(k.minus_p[:, :], [[0, 1]], base=0, channel_multiplier=-1,
                               allow_small_or_imprecise_dtypes=True)
                done(nc.gpsimd.tensor_copy(k.ident_bf[:, :], k.ident[:, :]))


def load_rows(sp, rows, source, sem, pad_tile_free):
    full = N_EDGES // P
    c, r = full // ROWS, full % ROWS
    sp.dma_start(rows[:, 0:c, :], source[0:c * ROWS * P].rearrange("(c t e) -> t c e", t=ROWS, e=P)).then_inc(sem, 16)
    sp.dma_start(rows[0:r, c, :], source[c * ROWS * P:full * P].rearrange("(t e) -> t e", e=P)).then_inc(sem, 16)
    sp.dma_start(rows[r:r + 1, c, 0:N_EDGES - full * P],
                 source[full * P:N_EDGES].rearrange("(t e) -> t e", t=1)).then_inc(sem, 16)


def edge_columns(nc, k, other, key, etype, weight):
    with ExitStack() as st:
        a = Names(nc, st)
        rows_i = a.sb(k.tag + "ec_rows_i", [ROWS, 3, CH, P], I32)
        rows_w = a.sb(k.tag + "ec_rows_w", [ROWS, CH, P])
        rows_f = a.sb(k.tag + "ec_rows_f", [ROWS, 3, CH, P])
        key_i = a.sb(k.tag + "ec_key_i", [P, 3, TILES], I32)
        rec_rows = a.sb(k.tag + "ec_rec_rows", [ROWS, CH, P, 4])
        following = a.sb(k.tag + "ec_following", [ROWS, CH, P])
        falls = a.sb(k.tag + "ec_falls", [ROWS, CH, P])
        fall_sum = a.sb(k.tag + "ec_fall_sum", [ROWS, 1])
        turned = a.ps(k.tag + "ec_turned", [P, 4, CH, P])
        total = a.ps(k.tag + "ec_total", [P, 1])
        s_pad, s_load, s_row, s_turn, s_col, s_store, s_next, s_rec, s_fall, s_total = (
            a.sem(k.tag + "ec_" + n) for n in ("pad", "load", "row", "turn", "col", "store", "next", "rec", "fall", "stotal"))
        with nc.Block() as block:
            @block.gpsimd
            def _(pool):
                pool.memset(rows_i[:, 0, :, :], 0).then_inc(s_pad, 1)
                pool.memset(rows_i[:, 1, :, :], PAD_NODE).then_inc(s_pad, 1)
                pool.memset(rows_i[:, 2, :, :], 0).then_inc(s_pad, 1)
                pool.memset(rows_w[:, :, :], 0.0).then_inc(s_pad, 1)

            @block.sync
            def _(sp):
                sp.wait_ge(s_pad, 4)
                load_rows(sp, rows_i[:, 0, :, :], other, s_load, None)
                load_rows(sp, rows_i[:, 1, :, :], key, s_load, None)
                load_rows(sp, rows_i[:, 2, :, :], etype, s_load, None)
                load_rows(sp, rows_w[:, :, :], weight, s_load, None)
                sp.wait_ge(s_row, 1)
                sp.dma_start(k.key_pad.rearrange("(c t e) -> t c e", t=ROWS, e=P), rows_f[:, 1, :, :]).then_inc(s_store, 16)
                sp.wait_ge(s_store, 16)
                first = k.key_pad[P:EP].rearrange("(t e) -> t e", e=P)[:, 0:1]
                for c in range(CH):
                    n = min(ROWS, TILES - 1 - c * ROWS)
                    with nc.allow_non_contiguous_dma("a value of each tile"):
                        sp.dma_start(following[0:n, c, P - 1:P], first[c * ROWS:c * ROWS + n, :]).then_inc(s_next, 16)
                sp.wait_ge(s_rec, 4)
                sp.dma_start(k.rec_sorted.rearrange("(c t e) q -> t c (e q)", t=ROWS, e=P),
                             rec_rows[:, :, :, :].rearrange("t c e q -> t c (e q)")).then_inc(s_store, 16)
                sp.wait_ge(s_store, 32)

            @block.vector
            def _(dve):
                dve.wait_ge(s_load, 16 * 12)
                nc.vector.memset(following[:, :, P - 1:P], float(PAD_NODE))
                nc.vector.tensor_copy(rows_f[:, :, :, :], rows_i[:, :, :, :]).then_inc(s_row, 1)
                dve.wait_ge(s_row, 1)
                for n in range(4):
                    nc.vector.tensor_copy(rec_rows[:, :, :, n], rows_w[:, :, :] if n == 3 else rows_f[:, n, :, :]).then_inc(s_rec, 1)
                nc.vector.tensor_copy(following[:, :, 0:P - 1], rows_f[:, 1, :, 1:P]).then_inc(s_fall, 1)
                dve.wait_ge(s_fall, 1)
                dve.wait_ge(s_next, 16 * CH)
                nc.vector.tensor_tensor(falls[:, :, :], rows_f[:, 1, :, :], following[:, :, :], ALU.is_gt).then_inc(s_fall, 1)
                dve.wait_ge(s_fall, 2)
                nc.vector.tensor_reduce(fall_sum[:, :], falls[:, :, :], AX.XY, ALU.add).then_inc(s_fall, 1)
                dve.wait_ge(s_total, 1)
                nc.vector.tensor_copy(k.unsorted[:, :], total[:, :]).then_inc(s_fall, 1)
                dve.wait_ge(s_turn, 1)
                done = Chain(dve, s_col)
                for n in range(4):
                    last = nc.vector.tensor_copy(k.rec[:, :, n].rearrange("p (c t) -> p c t", c=CH), turned[:, n, :, 0:ROWS])
                    done(last)
                done(nc.vector.tensor_copy(k.key_col[:, 0:TILES], k.rec[:, :, 1]))
                done(nc.vector.tensor_copy(key_i[:, 0, :], k.rec[:, :, 1]))
                done(nc.vector.tensor_scalar(key_i[:, 1, :], key_i[:, 0, :], 7, None, ALU.logical_shift_right))
                done(nc.vector.tensor_scalar(key_i[:, 2, :], key_i[:, 0, :], P - 1, None, ALU.bitwise_and))
                done(nc.vector.tensor_copy(k.hi_col[:, 0:TILES], key_i[:, 1, :]))
                done(nc.vector.tensor_copy(k.lo_col[:, 0:TILES], key_i[:, 2, :]))
                for pad in (k.hi_col, k.lo_col):
                    done(nc.vector.memset(pad[:, TILES:TILES + GT], 0.0))

            @block.tensor
            def _(pe):
                pe.wait_ge(s_row, 1)
                for n in range(4):
                    for c in range(CH):
                        source = rows_w[:, c, :] if n == 3 else rows_f[:, n, c, :]
                        last = nc.tensor.transpose(turned[:, n, c, 0:ROWS], source, k.ident[0:ROWS, 0:ROWS])
                last.then_inc(s_turn, 1)
                pe.wait_ge(s_fall, 3)
                nc.tensor.matmul(total[:, :], k.ones[0:ROWS, :], fall_sum[:, :], start=True, stop=True).then_inc(s_total, 1)


def degrees(nc, k):
    with ExitStack() as st:
        a = Names(nc, st)
        hot_hi = a.sb(k.tag + "dg_hot_hi", [P, 2, GT, NT], BF16)
        hot_lo = a.sb(k.tag + "dg_hot_lo", [P, 2, GT, P], BF16)
        hist = a.ps(k.tag + "dg_hist", [NT, P])
        s_hot, s_used, s_free, s_tot, s_pre, s_v, s_t, s_tt = (a.sem(k.tag + "dg_" + n) for n in
                                                 ("hot", "used", "free", "tot", "pre", "v", "t", "tt"))
        deg = a.sb(k.tag + "dg_deg", [NT, P])
        incl = a.sb(k.tag + "dg_incl", [NT, P])
        before = a.ps(k.tag + "dg_before", [NT, 1])
        ends = a.sb(k.tag + "dg_ends", [NT, 4, P])
        ei = a.sb(k.tag + "dg_ei", [NT, 8, P], I32)
        ef = a.sb(k.tag + "dg_ef", [NT, 8, P])
        turned = a.ps(k.tag + "dg_turned", [P, 3, 32])
        pairs = a.sb(k.tag + "dg_pairs", [NT, 3, P])
        spare = a.sb(k.tag + "dg_spare", [NT, P])
        s_spare, s_count, s_shift = (a.sem(k.tag + "dg_" + n) for n in ("sspare", "count", "shift"))
        with nc.Block() as block:
            @block.vector
            def _(dve):
                def body(b):
                    for h in range(HALVES):
                        cols = bass.ds(b * BODY + h * GT, GT)
                        wait(dve, s_free, b * 2 + (h - 1))
                        nc.vector.tensor_tensor(hot_hi[:, h, :, :], mid(k.iota[:, 0:NT], GT), bcast(k.hi_col[:, cols], NT), ALU.is_equal)
                        nc.vector.tensor_tensor(hot_lo[:, h, :, :], mid(k.iota[:, :], GT), bcast(k.lo_col[:, cols], P), ALU.is_equal).then_inc(s_hot, 1)
                repeat(dve, NB, body)
                dve.wait_ge(s_used, 1)
                done = Chain(dve, s_v)
                done(nc.vector.tensor_copy(deg[:, :], hist[:, :]))
                done(nc.vector.memset(ef[:, 0, :], 0.0))
                done(nc.vector.tensor_tensor_scan(incl[:, :], ef[:, 0, :], deg[:, :], 0.0, ALU.add, ALU.add))
                dve.sem_inc(s_tot, 1)
                dve.wait_ge(s_pre, 1)
                e0, e1 = ends[:, 0, :], ends[:, 1, :]
                done(nc.vector.tensor_scalar(e1, incl[:, :], before[:, 0:1], None, ALU.add))
                done(nc.vector.tensor_tensor(e0, e1, deg[:, :], ALU.subtract))
                done(nc.vector.tensor_copy(k.first_pos[:, :], e0))
                done(nc.vector.tensor_scalar(ends[:, 2, :], e1, 1.0, 0.0, ALU.subtract, ALU.max))
                done(nc.vector.tensor_copy(ei[:, 0, :], e0))
                done(nc.vector.tensor_copy(ei[:, 1, :], e1))
                done(nc.vector.tensor_copy(ei[:, 2, :], ends[:, 2, :]))
                done(nc.vector.tensor_scalar(ei[:, 3, :], ei[:, 0, :], 7, None, ALU.logical_shift_right))
                done(nc.vector.tensor_scalar(ei[:, 4, :], ei[:, 2, :], 7, None, ALU.logical_shift_right))
                done(nc.vector.tensor_scalar(ei[:, 5, :], ei[:, 1, :], P - 1, None, ALU.bitwise_and))
                done(nc.vector.tensor_copy(ef[:, 3:6, :], ei[:, 3:6, :]))
                t0, t1, tail = ef[:, 3, :], ef[:, 4, :], ef[:, 5, :]
                if k.attention:
                    touched, upto, row = (pairs[:, n, :] for n in range(3))
                    done(nc.vector.tensor_scalar(row, deg[:, :], 0.0, None, ALU.is_gt))
                    done(nc.vector.scalar_tensor_tensor(out=touched, in0=t1, scalar=1.0, in1=t0, op0=ALU.add, op1=ALU.subtract))
                    done(nc.vector.tensor_tensor(touched, touched, row, ALU.mult))
                    done(nc.vector.tensor_tensor_scan(upto, ef[:, 0, :], touched, 0.0, ALU.add, ALU.add))
                    dve.sem_inc(s_count, 1)
                    dve.wait_ge(s_shift, 1)
                    dve.wait_ge(s_spare, 1)
                    done(nc.vector.tensor_scalar(upto, upto, before[:, 0:1], None, ALU.add))
                    done(nc.vector.tensor_tensor(upto, upto, touched, ALU.subtract))
                    done(nc.vector.tensor_tensor(upto, upto, spare[:, :], ALU.subtract))
                    done(nc.vector.tensor_tensor(upto, upto, row, ALU.mult))
                    done(nc.vector.tensor_tensor(row, upto, spare[:, :], ALU.add))
                last, same, none, inside, across = (ef[:, n, :] for n in (6, 7, 0, 1, 2))
                done(nc.vector.tensor_scalar(last, tail, 0.0, None, ALU.is_equal))
                done(nc.vector.tensor_tensor(same, t0, t1, ALU.is_equal))
                done(nc.vector.tensor_scalar(inside, t0, float(P), float(P - 1), ALU.mult, ALU.add))
                done(nc.vector.tensor_tensor(inside, inside, e0, ALU.subtract))
                done(nc.vector.tensor_tensor(inside, inside, last, ALU.mult))
                done(nc.vector.tensor_tensor(inside, inside, e0, ALU.add))
                done(nc.vector.tensor_scalar(across, t1, 2.0, float(MERGED), ALU.mult, ALU.add))
                done(nc.vector.tensor_tensor(across, across, last, ALU.add))
                done(nc.vector.tensor_tensor(inside, inside, across, ALU.subtract))
                done(nc.vector.tensor_tensor(inside, inside, same, ALU.mult))
                done(nc.vector.tensor_tensor(inside, inside, across, ALU.add))
                done(nc.vector.tensor_scalar(none, deg[:, :], 0.0, None, ALU.is_equal))
                done(nc.vector.tensor_scalar(across, inside, -1.0, float(ZERO_ROW), ALU.mult, ALU.add))
                done(nc.vector.tensor_tensor(across, across, none, ALU.mult))
                done(nc.vector.tensor_tensor(inside, inside, across, ALU.add))
                dve.sem_inc(s_t, 1)
                dve.wait_ge(s_tt, 1)
                done(nc.vector.tensor_copy(k.sum_row[:, :], turned[:, 0, 0:NT]))
                done(nc.vector.tensor_copy(k.deg[:, :], turned[:, 1, 0:NT]))
                if k.attention:
                    done(nc.vector.tensor_copy(k.pair_row[:, :], turned[:, 2, 0:NT]))

            @block.gpsimd
            def _(pool):
                nc.gpsimd.iota(spare[:, :], [[1, P]], base=PAIRS, channel_multiplier=P,
                               allow_small_or_imprecise_dtypes=True).then_inc(s_spare, 1)

            @block.tensor
            def _(pe):
                nc.tensor.matmul(hist[:, :], k.zeros_bf[:, 0:NT], k.zeros_bf[:, :], start=True, stop=False)
                def body(b):
                    for h in range(HALVES):
                        pe.wait_ge(s_hot, b * 2 + (h + 1))
                        for j in range(GT):
                            last = nc.tensor.matmul(hist[:, :], hot_hi[:, h, j, :], hot_lo[:, h, j, :],
                                                    start=False, stop=False)
                        last.then_inc(s_free, 1)
                repeat(pe, NB, body)
                nc.tensor.matmul(hist[:, :], k.zeros_bf[:, 0:NT], k.zeros_bf[:, :], start=False, stop=True).then_inc(s_used, 1)
                pe.wait_ge(s_tot, 1)
                nc.tensor.matmul(before[:, :], k.tri_hi[0:NT, 0:NT], incl[:, P - 1:P], start=True, stop=True).then_inc(s_pre, 1)
                if k.attention:
                    pe.wait_ge(s_count, 1)
                    nc.tensor.matmul(before[:, :], k.tri_hi[0:NT, 0:NT], pairs[:, 1, P - 1:P], start=True, stop=True).then_inc(s_shift, 1)
                pe.wait_ge(s_t, 1)
                if k.attention:
                    nc.tensor.transpose(turned[:, 2, 0:NT], pairs[:, 2, :], k.ident[0:NT, 0:NT])
                nc.tensor.transpose(turned[:, 0, 0:NT], ef[:, 1, :], k.ident[0:NT, 0:NT])
                nc.tensor.transpose(turned[:, 1, 0:NT], deg[:, :], k.ident[0:NT, 0:NT]).then_inc(s_tt, 1)



def key_falls(nc, k, eng, kind):
    return eng.to_reg(nc.values_load(k.unsorted[0:1, 0:1], engines=(mybir.EngineType[kind],), min_val=0, max_val=EP))


def ranks(nc, k):
    with ExitStack() as st:
        a = Names(nc, st)
        hot_hi = a.sb(k.tag + "rk_hot_hi", [P, 2, GT, NT], BF16)
        hot_lo = a.sb(k.tag + "rk_hot_lo", [P, 2, GT, P], BF16)
        hot_hi_t = a.sb(k.tag + "rk_hot_hi_t", [NT, 2, GT, P], F16)
        snap = a.sb(k.tag + "rk_snap", [NT, 2, GT, P], F16)
        base = a.sb(k.tag + "rk_base", [NT, P])
        parts = a.sb(k.tag + "rk_parts", [NT, 2, 2, P], F16)
        key_row = a.sb(k.tag + "rk_key_row", [P, 2, GT * P])
        key_ring = a.sb(k.tag + "rk_key_ring", [P, 2, GT])
        junk = a.sb(k.tag + "rk_junk", [P, 2 * GT, P])
        part = a.sb(k.tag + "rk_part", [P, 2, 2 * GT])
        index = a.sb(k.tag + "rk_index", [P, 2, GT], I32)
        rec_ring = a.sb(k.tag + "rk_rec_ring", [P, 2, GT, 4])
        table = a.ps(k.tag + "rk_table", [NT, GT + 1, P])
        picked = [a.ps(k.tag + f"rk_picked{h}", [P, 8, P]) for h in range(2)]
        turned = [a.ps(k.tag + f"rk_turned{h}", [NT, 8, P], BF16) for h in range(2)]
        s_row = [a.sem(k.tag + f"rk_row{h}") for h in range(2)]
        s_scat = [a.dma_sem(k.tag + f"rk_scat{h}") for h in range(2)]
        s_hot, s_turn, s_turned, s_snap, s_table, s_pick, s_index, s_v, s_seen, s_free, s_taken, s_base = (
            a.sem(k.tag + "rk_" + n) for n in ("hot", "turn", "turned", "snap", "stable", "pick", "index", "v", "seen", "free", "taken", "sbase"))
        with nc.Block() as block:
            @block.sync
            def _(sp):
                with sp.If_ne(key_falls(nc, k, sp, "SP"), 0):
                    def body(b):
                        for h in range(HALVES):
                            wait(sp, s_free, b * 2 + (h - 1))
                            sp.dma_start(key_row[:, h, :], k.key_pad[bass.ds(b * (BODY * P) + h * GT * P, GT * P)]
                                         .partition_broadcast(P)).then_inc(s_row[h], 16)
                    repeat(sp, NB, body)

            @block.vector
            def _(dve):
                with dve.If_ne(key_falls(nc, k, dve, "DVE"), 0):
                    PER = 2 * 6

                    def one_hots(h, tile):
                        cols = bass.ds(tile, GT)
                        nc.vector.tensor_tensor(hot_hi[:, h, :, :], mid(k.iota[:, 0:NT], GT), bcast(k.hi_col[:, cols], NT), ALU.is_equal)
                        return nc.vector.tensor_tensor(hot_lo[:, h, :, :], mid(k.iota[:, :], GT), bcast(k.lo_col[:, cols], P), ALU.is_equal)

                    def split_base(done, h):
                        done(nc.vector.tensor_copy(parts[:, h, 0, :], base[:, :]))
                        done(nc.vector.tensor_tensor(parts[:, h, 1, :], base[:, :], parts[:, h, 0, :], ALU.subtract))
                        dve.sem_inc(s_base, 1)

                    start = Chain(dve, s_v)
                    start(one_hots(0, 0))
                    dve.sem_inc(s_hot, 1)
                    start(nc.vector.tensor_copy(base[:, :], k.first_pos[:, :]))
                    split_base(start, 0)

                    def body(b):
                        done = Chain(dve, s_v, b * PER + start.n)
                        for h in range(HALVES):
                            cols = bass.ds(b * BODY + h * GT, GT)
                            nc.vector.tensor_copy(key_ring[:, h, :], k.key_col[:, cols])
                            done(one_hots((h + 1) % 2, b * BODY + (h + 1) * GT))
                            dve.sem_inc(s_hot, 1)
                            dve.wait_ge(s_row[h], b * 16 + 16)
                            for j in range(GT):
                                last = nc.vector.scalar_tensor_tensor(
                                    out=junk[:, j, :], in0=key_row[:, h, j * P:(j + 1) * P], scalar=key_ring[:, h, j:j + 1],
                                    in1=k.tri[:, :], op0=ALU.is_equal, op1=ALU.mult, accum_out=part[:, h, j:j + 1])
                            last.then_inc(s_free, 1)
                            dve.wait_ge(s_snap, b * 2 + (h + 1))
                            done(nc.vector.tensor_tensor(base[:, :], base[:, :], snap[:, h, GT - 1, :], ALU.add))
                            split_base(done, (h + 1) % 2)
                            dve.wait_ge(s_pick, b * 2 + (h + 1))
                            for j in range(GT):
                                last = nc.vector.scalar_tensor_tensor(
                                    out=junk[:, GT + j, :], in0=picked[h][:, j, :], scalar=1.0, in1=hot_lo[:, h, j, :],
                                    op0=ALU.mult, op1=ALU.mult, accum_out=part[:, h, GT + j:GT + j + 1])
                            done(last)
                            wait(dve, s_scat[h], b * (16 * GT))
                            nc.vector.tensor_copy(rec_ring[:, h, :, :], k.rec[:, cols, :])
                            done(nc.vector.tensor_tensor(index[:, h, :], part[:, h, 0:GT], part[:, h, GT:2 * GT], ALU.add))
                            dve.sem_inc(s_index, 1)
                        assert done.n == PER
                    repeat(dve, NB, body)

            @block.scalar
            def _(act):
                with act.If_ne(key_falls(nc, k, act, "Activation"), 0):
                    def body(b):
                        for h in range(HALVES):
                            act.wait_ge(s_turn, b * 2 + (h + 1))
                            nc.scalar.copy(hot_hi_t[:, h, :, :], turned[h][:, 0:GT, :]).then_inc(s_turned, 1)
                            act.wait_ge(s_table, b * 2 + (h + 1))
                            nc.scalar.copy(snap[:, h, :, :], table[:, 0:GT, :]).then_inc(s_snap, 1)
                    repeat(act, NB, body)

            @block.tensor
            def _(pe):
                with pe.If_ne(key_falls(nc, k, pe, "PE"), 0):
                    def body(b):
                        for h in range(HALVES):
                            pe.wait_ge(s_hot, b * 2 + (h + 1))
                            for j in range(GT):
                                last = nc.tensor.transpose(turned[h][:, j, :], hot_hi[:, h, j, :], k.ident_bf[:, :])
                            last.then_inc(s_turn, 1)
                            hold(pe, s_taken, s_snap, b * 2 + h)
                            for lo, hi in ((0, 4), (4, GT)):
                                for j in range(hi):
                                    lo_j = max(lo, j)
                                    last = nc.tensor.matmul(table[:, lo_j:hi, :], hot_hi[:, h, j, :], mid(hot_lo[:, h, j, :], hi - lo_j),
                                                            start=(j == 0), stop=True, skip_group_check=(j > 0))
                            last.then_inc(s_table, 1)
                            hold(pe, s_taken, s_turned, b * 2 + (h + 1))
                            hold(pe, s_taken, s_snap, b * 2 + (h + 1))
                            hold(pe, s_taken, s_base, b * 2 + (h + 1))
                            hold(pe, s_taken, s_index, b * 2 + (h - 1))
                            for j in range(GT):
                                terms = [parts[:, h, 0, :], parts[:, h, 1, :]] + ([snap[:, h, j - 1, :]] if j else [])
                                for n, term in enumerate(terms):
                                    last = nc.tensor.matmul(picked[h][:, j, :], hot_hi_t[:, h, j, :], term, start=(n == 0), stop=(n == len(terms) - 1))
                            last.then_inc(s_pick, 1)
                    repeat(pe, NB, body)

            @block.gpsimd
            def _(pool):
                with pool.If_ne(key_falls(nc, k, pool, "Pool"), 0):
                    limit = pool.snap(pool.to_reg(EP - 1))
                    def body(b):
                        for h in range(HALVES):
                            pool.wait_ge(s_index, b * 2 + (h + 1))
                            pool.sem_inc(s_seen, 1)
                            for j in range(GT):
                                pool.indirect_dma_start(k.rec_sorted, bass.IndirectOffsetOnAxis(ap=index[:, h, j:j + 1], axis=0),
                                                        rec_ring[:, h, j, :], None, bounds_check=limit, oob_is_err=False).then_inc(s_scat[h], 16)
                    repeat(pool, NB, body)
                    for h in range(HALVES):
                        pool.wait_ge(s_scat[h], 16 * GT * NB)


def edge_meta(nc, k):
    with ExitStack() as st:
        a = Names(nc, st)
        rows = a.sb(k.tag + "em_rows", [ROWS, CH, P, 4])
        start = a.sb(k.tag + "em_start", [ROWS, CH, P])
        pos = a.sb(k.tag + "em_pos", [ROWS, CH, P])
        slot = a.sb(k.tag + "em_slot", [ROWS, CH, P])
        last = a.sb(k.tag + "em_last", [ROWS, CH, P])
        reset = a.sb(k.tag + "em_reset", [ROWS, 2, CH, P])
        rel = a.sb(k.tag + "em_rel", [ROWS, CH, P])
        ends = a.sb(k.tag + "em_ends", [ROWS, CH, 2])
        zero = a.sb(k.tag + "em_zero", [ROWS, P])
        key = a.sb(k.tag + "em_key", [P, NBR])
        local = a.sb(k.tag + "em_local", [ROWS, CH, P], BF16)
        count = a.sb(k.tag + "em_count", [ROWS, CH, P])
        first = a.sb(k.tag + "em_first", [ROWS, CH])
        ints = a.sb(k.tag + "em_ints", [ROWS, 2, CH], I32)
        ids = a.sb(k.tag + "em_ids", [P, NT], I32)
        none = a.sb(k.tag + "em_none", [PAIR_BLOCKS, P], I32)
        turned = [a.ps(k.tag + f"em_turned{n}", [P, CH, P]) for n in range(5)]
        sums = a.ps(k.tag + "em_sums", [P, 2, CH])
        s_count, s_sums, s_first, s_ids, s_none, s_pair = (a.sem(k.tag + "em_" + n) for n in ("scount", "ssums", "sfirst", "ids", "none", "pair"))
        s_node, s_tile = (a.dma_sem(k.tag + "em_" + n) for n in ("node", "tile"))
        s_load, s_v, s_rows, s_turn, s_store, s_key = (a.sem(k.tag + "em_" + n) for n in ("load", "v", "rows", "turn", "store", "key"))
        src, dst, typ, wgt = (rows[:, :, :, n] for n in range(4))
        with nc.Block() as block:
            @block.sync
            def _(sp):
                sp.dma_start(rows[:, :, :, :].rearrange("t c e q -> t c (e q)"),
                             k.rec_sorted.rearrange("(c t e) q -> t c (e q)", t=ROWS, e=P)).then_inc(s_load, 16)
                if k.attention:
                    sp.wait_ge(s_ids, 2)
                    sp.dma_start(k.pair_table[0:PAIRS, :].rearrange("(b p) o -> b (p o)", p=P), none[:, :]).then_inc(s_none, 16)
                    sp.wait_ge(s_first, 1)
                    with nc.allow_non_contiguous_dma("a value of each tile"):
                        sp.dma_start(k.tile_pairs.rearrange("(c t) -> t c", t=ROWS), ints[:, 0, :]).then_inc(s_pair, 16)
                    sp.dma_start(k.local.rearrange("(c t e) -> t c e", t=ROWS, e=P), local[:, :, :]).then_inc(s_pair, 16)
                    sp.wait_ge(s_pair, 32)
                    sp.dma_start(k.tile_pair[:, :], k.tile_pairs.rearrange("(o t) -> o t", o=1)).then_inc(s_pair, 16)
                    sp.wait_ge(s_tile, 16 * CH)
                    with nc.allow_non_contiguous_dma("a value of each pair"):
                        sp.dma_start(k.pair_node[:, :], k.pair_table[0:PAIRS, :].rearrange("(b p) o -> p (b o)", p=P)).then_inc(s_pair, 16)
                    sp.wait_ge(s_pair, 64)
                sp.wait_ge(s_rows, 1)
                for n in range(2 if k.attention else 0):
                    for heads in (8, 4):
                        for c in range(CH):
                            sp.dma_start(k.resets[n][heads][c * ROWS:(c + 1) * ROWS, :, :], mid(reset[:, n, c, :], heads)).then_inc(s_store, 16)
                sp.dma_start(k.ends.rearrange("(c t w) -> t c w", t=ROWS, w=2), ends[:, :, :]).then_inc(s_store, 16)
                sp.wait_ge(s_store, 16 * ((4 * CH if k.attention else 0) + 1))
                sp.dma_start(key[:, :], k.ends.partition_broadcast(P)).then_inc(s_key, 16)

            @block.vector
            def _(dve):
                done = Chain(dve, s_v)
                dve.wait_ge(s_load, 16)
                nc.vector.memset(zero[:, :], 0.0)
                nc.vector.memset(start[:, :, 0:1], 1.0)
                done(nc.vector.tensor_tensor(start[:, :, 1:P], dst[:, :, 1:P], dst[:, :, 0:P - 1], ALU.not_equal))
                if k.attention:
                    for c in range(CH):
                        nc.vector.tensor_tensor_scan(count[:, c, :], zero[:, :], start[:, c, :], 0.0, ALU.add, ALU.add).then_inc(s_count, 1)
                    dve.wait_ge(s_count, CH)
                    done(nc.vector.tensor_scalar(local[:, :, :], count[:, :, :], 1.0, None, ALU.subtract))
                    done(nc.vector.tensor_copy(ints[:, 1, :], dst[:, :, 0]))
                    dve.wait_ge(s_sums, 1)
                    done(nc.vector.tensor_copy(first[:, :], sums[0:ROWS, 0, :]))
                    for c in range(1, CH):
                        for before in range(c):
                            done(nc.vector.tensor_tensor(first[:, c:c + 1], first[:, c:c + 1], sums[0:ROWS, 1, before:before + 1], ALU.add))
                    done(nc.vector.tensor_copy(ints[:, 0, :], first[:, :]))
                    dve.sem_inc(s_first, 1)
                done(nc.vector.tensor_tensor(last[:, :, :], start[:, :, :], mid(k.iota[0:ROWS, :], CH), ALU.mult))
                for c in range(CH):
                    done(nc.vector.tensor_tensor_scan(pos[:, c, :], zero[:, :], last[:, c, :], 0.0, ALU.add, ALU.max))
                done(nc.vector.tensor_tensor(last[:, :, :], dst, dst[:, :, P - 1:P].to_broadcast([ROWS, CH, P]), ALU.is_equal))
                done(nc.vector.tensor_scalar(slot[:, :, :], pos[:, :, :], -1.0, float(P - 1), ALU.mult, ALU.add))
                done(nc.vector.tensor_tensor(slot[:, :, :], slot[:, :, :], last[:, :, :], ALU.mult))
                done(nc.vector.tensor_tensor(slot[:, :, :], slot[:, :, :], pos[:, :, :], ALU.add))
                nc.vector.tensor_scalar(reset[:, 0, :, :], start[:, :, :], -BIG, None, ALU.mult)
                nc.vector.tensor_scalar(reset[:, 1, :, 0:P - 1], start[:, :, 1:P], -BIG, None, ALU.mult)
                nc.vector.memset(reset[:, 1, :, P - 1:P], -BIG)
                nc.vector.tensor_copy(ends[:, :, 0:1], dst[:, :, 0:1])
                nc.vector.tensor_copy(ends[:, :, 1:2], dst[:, :, P - 1:P])
                done(nc.vector.tensor_scalar(rel[:, :, :], typ, float(NP), None, ALU.mult))
                done(nc.vector.tensor_tensor(rel[:, :, :], rel[:, :, :], src, ALU.add))
                dve.sem_inc(s_rows, 1)
                dve.wait_ge(s_turn, 1)
                for out, n in ((k.slot, 0), (k.weight, 1), (k.other_idx, 2)) + (((k.start, 3), (k.rel_idx, 4)) if k.attention else ()):
                    done(nc.vector.tensor_copy(out[:, :].rearrange("p (c t) -> p c t", c=CH), turned[n][:, :, 0:ROWS]))
                dve.wait_ge(s_key, 16)
                nc.vector.memset(k.keep[:, 0:1], 0.0)
                done(nc.vector.tensor_tensor(k.keep[:, 1:NBR], key[:, 1:NBR], key[:, 0:NBR - 1], ALU.is_equal))
                if k.attention:
                    nc.vector.tensor_scalar(k.cut[:, 0, :], k.keep[0:8, :], 1.0, BIG, ALU.subtract, ALU.mult)
                    nc.vector.memset(k.cut[:, 1, NBR - 1:NBR], -BIG)
                    done(nc.vector.tensor_scalar(k.cut[:, 1, 0:NBR - 1], k.keep[0:8, 1:NBR], 1.0, BIG, ALU.subtract, ALU.mult))

            @block.gpsimd
            def _(pool):
                if k.attention:
                    nc.gpsimd.iota(ids[:, :], [[P, NT]], base=0, channel_multiplier=1).then_inc(s_ids, 1)
                    pool.memset(none[:, :], 0).then_inc(s_ids, 1)
                    pool.wait_ge(s_ids, 2)
                    limit = pool.snap(pool.to_reg(PAIRS + NP - 1))
                    pool.wait_ge(s_none, 16)
                    for c in range(NT):
                        pool.indirect_dma_start(k.pair_table, bass.IndirectOffsetOnAxis(ap=k.pair_row[:, c:c + 1], axis=0),
                                                ids[:, c:c + 1], None, bounds_check=limit, oob_is_err=False).then_inc(s_node, 16)
                    pool.wait_ge(s_node, 16 * NT)
                    pool.wait_ge(s_first, 1)
                    for c in range(CH):
                        pool.indirect_dma_start(k.pair_table, bass.IndirectOffsetOnAxis(ap=ints[:, 0, c:c + 1], axis=0),
                                                ints[:, 1, c:c + 1], None, bounds_check=limit, oob_is_err=False).then_inc(s_tile, 16)
                    pool.wait_ge(s_tile, 16 * CH)

            @block.tensor
            def _(pe):
                if k.attention:
                    pe.wait_ge(s_count, CH)
                    nc.tensor.matmul(sums[0:ROWS, 0, :], k.tri_hi[0:ROWS, 0:ROWS], count[:, :, P - 1], start=True, stop=True)
                    nc.tensor.matmul(sums[:, 1, :], k.ones[0:ROWS, :], count[:, :, P - 1], start=True, stop=True).then_inc(s_sums, 1)
                pe.wait_ge(s_rows, 1)
                for n, q in enumerate((slot[:, :, :], wgt, src, start[:, :, :], rel[:, :, :])):
                    for c in range(CH):
                        ins = nc.tensor.transpose(turned[n][:, c, 0:ROWS], q[:, c, :], k.ident[0:ROWS, 0:ROWS])
                ins.then_inc(s_turn, 1)

class Shared:

    def __init__(self, a):
        self.iota, self.ident, self.tri, self.tri_hi = (
            a.sb(n, [P, w]) for n, w in (("iota", P), ("ident", P), ("tri", P), ("tri_hi", P)))
        self.ident_bf, self.zeros_bf = a.sb("ident_bf", [P, P], BF16), a.sb("zeros_bf", [P, P], BF16)
        self.ones, self.minus_p = a.sb("ones", [P, P]), a.sb("minus_p", [P, 1])
        self.mask, self.gate, self.inv_root = a.sb("mask", [P, NT * TYPES]), a.sb("gate", [P, NT]), a.sb("inv_root", [P, NT])


class Order:

    def __init__(self, k):
        self.iota, self.ident, self.tri, self.tri_hi = k.iota, k.ident, k.tri, k.tri_hi
        self.ident_bf, self.zeros_bf, self.ones = k.ident_bf, k.zeros_bf, k.ones
        self.mask, self.gate, self.inv_root, self.minus_p = k.mask, k.gate, k.inv_root, k.minus_p


def edge_order(nc, k, a, ins, tag, key, other, attention):
    o = Order(k)
    o.tag, o.attention = tag, attention
    o.slot, o.weight, o.other_idx = a.sb(tag + "slot", [P, TILES]), a.sb(tag + "weight", [P, TILES]), a.sb(tag + "other_idx", [P, TILES], I32)
    o.deg, o.sum_row = a.sb(tag + "deg", [P, NT]), a.sb(tag + "sum_row", [P, NT], I32)
    o.keep = a.sb(tag + "keep", [P, NBR])
    if attention:
        o.start = a.sb(tag + "start", [P, TILES])
        o.rel_idx = a.sb(tag + "rel_idx", [P, TILES], I32)
        o.pair_row, o.pair_node = a.sb(tag + "pair_row", [P, NT], I32), a.sb(tag + "pair_node", [P, PAIR_BLOCKS], I32)
        o.tile_pair = a.sb(tag + "tile_pair", [1, TILES], I32)
        o.pair_table = nc.dram_tensor(tag + "pair_table", (PAIRS + NP, 1), I32, kind="Internal").ap()
        o.local = nc.dram_tensor(tag + "local", (EP,), BF16, kind="Internal").ap()
        o.tile_pairs = nc.dram_tensor(tag + "tile_pairs", (TILES,), I32, kind="Internal").ap()
        o.cut = a.sb(tag + "cut", [8, 2, NBR])
        o.resets = [{heads: nc.dram_tensor(f"{tag}resets{n}_{heads}", (TILES, heads, P), F32, kind="Internal").ap()
                     for heads in (8, 4)} for n in range(2)]
    o.key_pad = nc.dram_tensor(tag + "key_pad", (EP,), F32, kind="Internal").ap()
    o.rec_sorted = nc.dram_tensor(tag + "rec_sorted", (EP, 4), F32, kind="Internal").ap()
    o.ends = nc.dram_tensor(tag + "ends", (NBR,), F32, kind="Internal").ap()
    with ExitStack() as st:
        t = Names(nc, st)
        o.rec = t.sb(tag + "rec", [P, TILES, 4])
        o.key_col, o.hi_col, o.lo_col = (t.sb(tag + n, [P, TILES + GT]) for n in ("key_col", "hi_col", "lo_col"))
        o.first_pos = t.sb(tag + "first_pos", [NT, P])
        o.unsorted = t.sb(tag + "unsorted", [P, 1], I32)
        edge_columns(nc, o, other, key, ins["etype"], ins["weight"])
        degrees(nc, o)
        ranks(nc, o)
    edge_meta(nc, o)
    return o


def sum_edges(nc, k, tag, table, partial, weighted):
    with ExitStack() as st:
        a = Names(nc, st)
        got = a.sb(tag + "got", [P, 2, GT, D])
        hot = a.sb(tag + "hot", [P, 2, GT, P])
        sums = a.sb(tag + "sums", [P, 2, GT, D])
        idx = a.sb(tag + "idx", [P, 2, GT], I32)
        acc = [a.ps(f"{tag}acc{j}", [P, 512]) for j in range(GT)]
        s_got = [a.dma_sem(f"{tag}s_got{h}") for h in range(2)]
        s_out = [a.sem(f"{tag}s_out{h}") for h in range(2)]
        s_idx, s_seen, s_hot, s_v, s_acc, s_sums = (a.sem(tag + n) for n in ("s_idx", "s_seen", "s_hot", "s_v", "s_acc", "s_sums"))
        with nc.Block() as block:
            @block.gpsimd
            def _(pool):
                limit = pool.snap(pool.to_reg(NP - 1))

                def body(b):
                    for h in range(HALVES):
                        hold(pool, s_seen, s_acc, b * BODY + (h - 1) * GT)
                        nc.gpsimd.tensor_copy(idx[:, h, :], k.other_idx[:, bass.ds(b * BODY + h * GT, GT)]).then_inc(s_idx, 1)
                        hold(pool, s_seen, s_idx, b * 2 + (h + 1))
                        for j in range(GT):
                            pool.indirect_dma_start(got[:, h, j, :], None, table, bass.IndirectOffsetOnAxis(ap=idx[:, h, j:j + 1], axis=0),
                                                    bounds_check=limit, oob_is_err=False).then_inc(s_got[h], 16)
                repeat(pool, NB, body)

            @block.vector
            def _(dve):
                def body(b):
                    for h in range(HALVES):
                        cols = bass.ds(b * BODY + h * GT, GT)
                        wait(dve, s_acc, b * BODY + (h - 1) * GT)
                        ins = nc.vector.tensor_tensor(hot[:, h, :, :], mid(k.iota[:, :], GT), bcast(k.slot[:, cols], P), ALU.is_equal)
                        if weighted:
                            ins.then_inc(s_v, 1)
                            dve.wait_ge(s_v, b * 2 + (h + 1))
                            ins = nc.vector.tensor_tensor(hot[:, h, :, :], hot[:, h, :, :], bcast(k.weight[:, cols], P), ALU.mult)
                        ins.then_inc(s_hot, 1)
                repeat(dve, NB, body)

            @block.tensor
            def _(pe):
                def body(b):
                    for h in range(HALVES):
                        pe.wait_ge(s_hot, b * 2 + (h + 1))
                        pe.wait_ge(s_got[h], b * (16 * GT) + 16 * GT)
                        for j in range(GT):
                            wait(pe, s_sums, b * BODY + ((h - 1) * GT + j + 1))
                            nc.tensor.matmul(acc[j][:, 0:D], hot[:, h, j, :], got[:, h, j, :], start=True, stop=True).then_inc(s_acc, 1)
                repeat(pe, NB, body)

            @block.scalar
            def _(act):
                def body(b):
                    for h in range(HALVES):
                        wait(act, s_out[h], b * 16)
                        for j in range(GT):
                            act.wait_ge(s_acc, b * BODY + (h * GT + j + 1))
                            nc.scalar.copy(sums[:, h, j, :], acc[j][:, 0:D]).then_inc(s_sums, 1)
                repeat(act, NB, body)

            @block.sync
            def _(sp):
                def body(b):
                    for h in range(HALVES):
                        sp.wait_ge(s_sums, b * BODY + (h + 1) * GT)
                        sp.dma_start(partial[bass.ds(b * (BODY * P) + h * GT * P, GT * P), :].rearrange("(t s) w -> s t w", s=P),
                                     sums[:, h, :, :]).then_inc(s_out[h], 16)
                repeat(sp, NB, body)
                for h in range(HALVES):
                    sp.wait_ge(s_out[h], 16 * NB)


def spread_rows(nc, k, tag, own, pair_rows):
    with ExitStack() as st:
        a = Names(nc, st)
        rows = a.sb(tag + "rows", [P, PAIR_BLOCKS, D])
        parts = [(lo, min(lo + GT, PAIR_BLOCKS)) for lo in range(0, PAIR_BLOCKS, GT)]
        s_in = [a.dma_sem(f"{tag}in{n}") for n in range(len(parts))]
        s_out = a.sem(tag + "out")
        with nc.Block() as block:
            @block.gpsimd
            def _(pool):
                limit = pool.snap(pool.to_reg(NP - 1))
                for n, (lo, hi) in enumerate(parts):
                    for c in range(lo, hi):
                        pool.indirect_dma_start(rows[:, c, :], None, own, bass.IndirectOffsetOnAxis(ap=k.pair_node[:, c:c + 1], axis=0),
                                                bounds_check=limit, oob_is_err=False).then_inc(s_in[n], 16)

            @block.sync
            def _(sp):
                for n, (lo, hi) in enumerate(parts):
                    sp.wait_ge(s_in[n], 16 * (hi - lo))
                    sp.dma_start(pair_rows[lo * P:hi * P, :].rearrange("(c p) w -> p c w", p=P), rows[:, lo:hi, :]).then_inc(s_out, 16)
                sp.wait_ge(s_out, 16 * len(parts))


def attend_edges(nc, k, tag, table, main_idx, limit_rows, pair_rows, heads, scale, partial, free):
    W = D + 2 * heads
    dk = D // heads
    HT = GT * heads
    with ExitStack() as st:
        a = Names(nc, st)
        got = a.sb(tag + "got", [P, 2, GT, 2 * D])
        window = a.sb(tag + "window", [P, 2, GT, D])
        local = a.sb(tag + "local", [P, 2, GT * P], BF16)
        apart = a.sb(tag + "apart", [P, GT * P])
        spread = a.sb(tag + "spread", [P, 2, GT * P])
        prod = a.sb(tag + "prod", [P, GT, D])
        hot = a.sb(tag + "hot", [P, 2, GT, P])
        val, sums = (t[:, 0:2 * GT, 0:W].rearrange("p (h t) w -> p h t w", h=2) for t in free)
        idx = a.sb(tag + "idx", [P, 2, GT], I32)
        cuts = a.sb(tag + "cuts", [HT, 2, 2, P])
        score = a.sb(tag + "score", [P, 2, HT])
        diff = a.sb(tag + "diff", [P, 2, HT])
        run = a.sb(tag + "run", [HT, 2, P])
        segmax = a.sb(tag + "segmax", [HT, 2, P])
        own = a.ps(tag + "own", [P, 8, D])
        BANKS = 3
        acc = [a.ps(f"{tag}acc{j}", [P, 512]) for j in range(BANKS)]
        flip = a.ps(tag + "flip", [P, 4, P])
        s_got = [a.dma_sem(f"{tag}s_got{h}") for h in range(2)]
        s_out = [a.sem(f"{tag}s_out{h}") for h in range(2)]
        s_cut = [a.sem(f"{tag}s_cut{h}") for h in range(2)]
        s_window = [a.sem(f"{tag}s_window{h}") for h in range(2)]
        s_local = [a.sem(f"{tag}s_local{h}") for h in range(2)]
        s_idx, s_seen, s_v, s_read, s_score, s_flip, s_segmax, s_back, s_diff, s_exp, s_val, s_acc, s_sums, s_apart, s_spread, s_own, s_mult = (
            a.sem(tag + "s_" + n) for n in ("idx", "seen", "v", "read", "score", "flip", "segmax", "back", "diff", "exp",
                                            "val", "acc", "sums", "apart", "spread", "own", "mult"))

        def bank(h, j):
            return (h * GT + j) % BANKS

        def bank_user(h, j):
            if h * GT + j >= BANKS:
                return BANKS
            return next(d for d in range(1, BODY) if (BODY + j - d) % BANKS == bank(0, j) and d > j)

        def group(b, h, ahead):
            body, half = b + (h + ahead) // HALVES, (h + ahead) % HALVES
            if isinstance(b, int) and not 0 <= body < NB:
                return None
            return body, half

        with nc.Block() as block:
            @block.gpsimd
            def _(pool):
                limit = pool.snap(pool.to_reg(limit_rows - 1))

                def body(b):
                    for h in range(HALVES):
                        cols = bass.ds(b * BODY + h * GT, GT)
                        hold(pool, s_seen, s_val, b * 2 + (h - 1))
                        nc.gpsimd.tensor_copy(idx[:, h, :], main_idx[:, cols]).then_inc(s_idx, 1)
                        hold(pool, s_seen, s_idx, b * 2 + (h + 1))
                        for j in range(GT):
                            pool.indirect_dma_start(got[:, h, j, :], None, table, bass.IndirectOffsetOnAxis(ap=idx[:, h, j:j + 1], axis=0),
                                                    bounds_check=limit, oob_is_err=False).then_inc(s_got[h], 16)
                repeat(pool, NB, body)

            @block.sync
            def _(sp):
                def body(b):
                    for h in range(HALVES):
                        wait(sp, s_spread, b * 2 + (h - 1))
                        sp.dma_start(local[:, h, :], k.local[bass.ds(b * (BODY * P) + h * GT * P, GT * P)].partition_broadcast(P)).then_inc(s_local[h], 16)
                        wait(sp, s_own, b * 2 + (h - 1))
                        for j in range(GT):
                            row = nc.values_load(k.tile_pair[0:1, bass.ds(b * BODY + h * GT + j, 1)], engines=(mybir.EngineType.SP,),
                                                 min_val=0, max_val=PAIRS - P)
                            sp.dma_start(window[:, h, j, :], pair_rows[bass.ds(row, P), :]).then_inc(s_window[h], 16)
                        wait(sp, s_segmax, b * 2 + (h - 1))
                        for n in range(2):
                            sp.dma_start(cuts[:, h, n, :], k.resets[n][heads].rearrange("t h e -> (t h) e")[bass.ds(b * (BODY * heads) + h * GT * heads, HT), :]).then_inc(s_cut[h], 16)
                repeat(sp, NB, body)

            @block.vector
            def _(dve):
                PER = 2 * 8

                def body(b):
                    done = Chain(dve, s_v, b * PER)
                    for h in range(HALVES):
                        cols = bass.ds(b * BODY + h * GT, GT)
                        dve.wait_ge(s_got[h], b * (16 * GT) + 16 * GT)
                        dve.wait_ge(s_own, b * 2 + (h + 1))
                        done(nc.vector.tensor_tensor(prod[:, :, :], got[:, h, :, 0:D], own[:, 0:GT, :], ALU.mult))
                        dve.sem_inc(s_mult, 1)
                        done(nc.vector.tensor_reduce(score[:, h, :], prod[:, :, :].rearrange("p t (h d) -> p (t h) d", d=dk), AX.X, ALU.add))
                        dve.sem_inc(s_score, 1)
                        wait(dve, s_acc, b * BODY + (h - 1) * GT)
                        done(nc.vector.tensor_tensor(hot[:, h, :, :], mid(k.iota[:, :], GT), bcast(k.slot[:, cols], P), ALU.is_equal))
                        dve.wait_ge(s_cut[h], b * 32 + 32)
                        dve.wait_ge(s_flip, b * 2 + (h + 1))
                        done(nc.vector.tensor_tensor_scan(run[:, h, :], cuts[:, h, 0, :], flip[0:HT, h, :], -BIG, ALU.add, ALU.max))
                        done(nc.vector.tensor_tensor_scan(segmax[:, h, ::-1], cuts[:, h, 1, ::-1], run[:, h, ::-1], -BIG, ALU.add, ALU.max))
                        dve.sem_inc(s_segmax, 1)
                        dve.wait_ge(s_back, b * 2 + (h + 1))
                        done(nc.vector.tensor_tensor(diff[:, h, :], score[:, h, :], flip[:, 2 + h, 0:HT], ALU.subtract))
                        dve.sem_inc(s_diff, 1)
                        done(nc.vector.tensor_tensor(val[:, h, :, D + heads:W], flip[:, 2 + h, 0:HT].rearrange("p (t h) -> p t h", h=heads),
                                                     bcast(k.start[:, cols], heads), ALU.mult))
                        dve.wait_ge(s_exp, b * 2 + (h + 1))
                        done(nc.vector.tensor_tensor(val[:, h, :, 0:D].rearrange("p t (h d) -> p t h d", d=dk),
                                                     got[:, h, :, D:2 * D].rearrange("p t (h d) -> p t h d", d=dk),
                                                     val[:, h, :, D:D + heads].unsqueeze(3).to_broadcast([P, GT, heads, dk]), ALU.mult))
                        dve.sem_inc(s_val, 1)
                    assert done.n == PER
                repeat(dve, NB, body)

            @block.tensor
            def _(pe):
                def spread_group(b, h):
                    pe.wait_ge(s_spread, b * 2 + (h + 1))
                    hold(pe, s_read, s_mult, b * 2 + h)
                    pe.wait_ge(s_window[h], b * (16 * GT) + 16 * GT)
                    for j in range(GT):
                        last = nc.tensor.matmul(own[:, j, :], spread[:, h, j * P:(j + 1) * P], window[:, h, j, :], start=True, stop=True)
                    last.then_inc(s_own, 1)

                def products(b, h):
                    pe.wait_ge(s_val, b * 2 + (h + 1))
                    for j in range(GT):
                        wait(pe, s_sums, b * BODY + (h * GT + j + 1 - bank_user(h, j)))
                        nc.tensor.matmul(acc[bank(h, j)][:, 0:W], hot[:, h, j, :], val[:, h, j, :], start=True, stop=True).then_inc(s_acc, 1)

                def body(b):
                    for h in range(HALVES):
                        following, previous = group(b, h, 1), group(b, h, -1)
                        if following:
                            spread_group(*following)
                        hold(pe, s_read, s_score, b * 2 + (h + 1))
                        nc.tensor.transpose(flip[0:HT, h, :], score[:, h, :], k.ident[:, :]).then_inc(s_flip, 1)
                        hold(pe, s_read, s_segmax, b * 2 + (h + 1))
                        nc.tensor.transpose(flip[:, 2 + h, 0:HT], segmax[:, h, :], k.ident[0:HT, 0:HT]).then_inc(s_back, 1)
                        if previous:
                            products(*previous)
                spread_group(0, 0)
                repeat_between(pe, NB, body)
                products(NB - 1, HALVES - 1)

            @block.scalar
            def _(act):
                def spread_one_hots(b, h):
                    act.wait_ge(s_local[h], b * 16 + 16)
                    wait(act, s_own, b * 2 + (h - 1))
                    wait(act, s_spread, b * 2 + h)
                    nc.scalar.activation(apart[:, :], local[:, h, :], ACT.Abs, bias=k.minus_p[:, 0:1]).then_inc(s_apart, 1)
                    act.wait_ge(s_apart, b * 2 + (h + 1))
                    nc.scalar.activation(spread[:, h, :], apart[:, :], ACT.Relu, bias=k.ones[:, 0:1], scale=-1.0).then_inc(s_spread, 1)

                def copy_sums(b, h):
                    wait(act, s_out[h], b * 16)
                    for j in range(GT):
                        act.wait_ge(s_acc, b * BODY + (h * GT + j + 1))
                        nc.scalar.copy(sums[:, h, j, :], acc[bank(h, j)][:, 0:W]).then_inc(s_sums, 1)
                    act.wait_ge(s_sums, b * BODY + (h + 1) * GT)
                    act.dma_start(partial[bass.ds(b * (BODY * P) + h * GT * P, GT * P), :].rearrange("(t s) w -> s t w", s=P),
                                  sums[:, h, :, :]).then_inc(s_out[h], 16)

                def body(b):
                    for h in range(HALVES):
                        following, previous = group(b, h, 2), group(b, h, -1)
                        if following:
                            spread_one_hots(*following)
                        act.wait_ge(s_diff, b * 2 + (h + 1))
                        nc.scalar.activation(val[:, h, :, D:D + heads], diff[:, h, :].rearrange("p (t h) -> p t h", h=heads),
                                             ACT.Exp, scale=scale).then_inc(s_exp, 1)
                        if previous:
                            copy_sums(*previous)
                spread_one_hots(0, 0)
                spread_one_hots(0, 1)
                repeat_between(act, NB, body)
                copy_sums(NB - 1, HALVES - 1)
                for h in range(HALVES):
                    act.wait_ge(s_out[h], 16 * NB)


def merge(nc, k, tag, partial, heads, scale):
    W = D + 2 * heads
    with ExitStack() as st:
        a = Names(nc, st)
        rows = a.sb(tag + "rows", [BR, BC, W])
        cols = a.sb(tag + "cols", [P, 2, NBR])
        total = a.sb(tag + "total", [P, 2, NBR])
        small = a.sb(tag + "small", [8, 6, NBR]) if heads else None
        pick = a.sb(tag + "pick", [8, 2, P]) if heads else None
        back = a.sb(tag + "back", [BR, BC, W])
        zero = a.sb(tag + "zero", [1, W])
        SPLIT = (4, BC - 4)
        turn = [a.ps(f"{tag}turn{n}", [P, 2, 512]) for n in range(4 if heads else 2)]
        s_load, s_zero, s_turn, s_cols, s_v, s_f, s_scaled, s_total, s_back, s_rows, s_store, s_pick, s_exp, s_fac = (
            a.sem(tag + n) for n in ("load", "zero", "turn", "cols", "v", "f", "scaled", "total", "back", "rows", "store", "pick", "exp", "fac"))

        def parts(n):
            return ((0, 0, SPLIT[0] * BR), (1, SPLIT[0] * BR, NBR))

        with nc.Block() as block:
            @block.gpsimd
            def _(pool):
                pool.memset(zero[:, :], 0.0).then_inc(s_zero, 1)
                if heads:
                    dk = D // heads
                    done = Chain(pool, s_pick)
                    done(pool.memset(pick[:, :, :], 1.0))
                    flat = pick[0:heads, :, :].rearrange("h f p -> h (f p)")
                    done(pool.affine_select(out=flat, in_=flat, compare_op=ALU.is_ge, fill=0.0, base=0,
                                            pattern=[[1, D]], channel_multiplier=-dk))
                    done(pool.affine_select(out=flat, in_=flat, compare_op=ALU.is_ge, fill=0.0, base=dk - 1,
                                            pattern=[[-1, D]], channel_multiplier=dk))

            @block.sync
            def _(sp):
                view = partial[0:EP, :].rearrange("(c t s) w -> t c s w", t=BR // 2, s=P)
                for n in range(2):
                    sp.dma_start(rows[n:BR:2, :, :], view[:, :, n * (P - 1), :]).then_inc(s_load, 16)
                sp.wait_ge(s_zero, 1)
                sp.dma_start(partial[ZERO_ROW:ZERO_ROW + 1, :], zero[:, :]).then_inc(s_store, 16)
                sp.wait_ge(s_rows, 1)
                sp.dma_start(partial[MERGED:MERGED + NBR, :].rearrange("(c p) w -> p c w", p=BR), back[:, :, :]).then_inc(s_store, 16)
                sp.wait_ge(s_store, 32)

            @block.tensor
            def _(pe):
                pe.wait_ge(s_load, 32)
                for n, (lo, hi) in enumerate(((0, P), (P, D)) + (((D, D + heads), (D + heads, W)) if heads else ())):
                    for c in range(BC):
                        col = (c % 4) * BR
                        ins = nc.tensor.transpose(turn[n][0:hi - lo, c // 4, col:col + BR], rows[:, c, lo:hi], k.ident[0:BR, 0:BR])
                ins.then_inc(s_turn, 1)
                if heads:
                    pe.wait_ge(s_pick, 3)
                    pe.wait_ge(s_exp, 1)
                    pe.wait_ge(s_cols, 1)
                    for f in range(2):
                        for bank, lo, hi in parts(f):
                            ins = nc.tensor.matmul(turn[f][:, bank, 0:hi - lo], pick[0:heads, f, :], small[0:heads, 5, lo:hi], start=True, stop=True)
                    ins.then_inc(s_fac, 1)
                pe.wait_ge(s_total, 1)
                for c in range(BC):
                    for f in range(2):
                        ins = nc.tensor.transpose(turn[f][0:BR, c // 4, (c % 4) * P:(c % 4 + 1) * P], total[:, f, c * BR:(c + 1) * BR], k.ident[:, :])
                    if heads:
                        ins = nc.tensor.transpose(turn[2][0:BR, c // 4, (c % 4) * P:(c % 4) * P + heads],
                                                  small[0:heads, 4, c * BR:(c + 1) * BR], k.ident[0:heads, 0:heads])
                ins.then_inc(s_back, 1)

            @block.scalar
            def _(act):
                if heads:
                    act.wait_ge(s_f, 1)
                    nc.scalar.activation(small[0:heads, 5, :], small[0:heads, 3, :], ACT.Exp, scale=scale).then_inc(s_exp, 1)

            @block.vector
            def _(dve):
                done = Chain(dve, s_v)
                dve.wait_ge(s_turn, 1)
                for f in range(2):
                    for bank, lo, hi in parts(f):
                        done(nc.vector.tensor_copy(cols[:, f, lo:hi], turn[f][:, bank, 0:hi - lo]))
                if heads:
                    z, m, run, top, zsum = (small[0:heads, n, :] for n in range(5))
                    for n, q in ((2, 0), (3, 1)):
                        for bank, lo, hi in parts(n):
                            done(nc.vector.tensor_copy(small[0:heads, q, lo:hi], turn[n][0:heads, bank, 0:hi - lo]))
                    dve.sem_inc(s_cols, 1)
                    done(nc.vector.tensor_scalar(run, z, 0.0, -BIG, ALU.is_equal, ALU.mult))
                    done(nc.vector.tensor_tensor(m, m, run, ALU.add))
                    done(nc.vector.tensor_tensor_scan(run, k.cut[0:heads, 0, :], m, -BIG, ALU.add, ALU.max))
                    done(nc.vector.tensor_tensor_scan(small[0:heads, 3, ::-1], k.cut[0:heads, 1, ::-1], small[0:heads, 2, ::-1], -BIG, ALU.add, ALU.max))
                    done(nc.vector.tensor_tensor(top, m, top, ALU.subtract))
                    dve.sem_inc(s_f, 1)
                    dve.wait_ge(s_exp, 1)
                    done(nc.vector.tensor_tensor(z, z, small[0:heads, 5, :], ALU.mult))
                    done(nc.vector.tensor_tensor_scan(zsum, k.keep[0:heads, :], z, 0.0, ALU.mult, ALU.add))
                    dve.wait_ge(s_fac, 1)
                    for f in range(2):
                        for bank, lo, hi in parts(f):
                            done(nc.vector.tensor_tensor(cols[:, f, lo:hi], cols[:, f, lo:hi], turn[f][:, bank, 0:hi - lo], ALU.mult))
                for f in range(2):
                    done(nc.vector.tensor_tensor_scan(total[:, f, :], k.keep[:, :], cols[:, f, :], 0.0, ALU.mult, ALU.add))
                dve.sem_inc(s_total, 1)
                if heads:
                    done(nc.vector.memset(back[:, :, D:W], 0.0))
                dve.wait_ge(s_back, 1)
                for bank in range(2):
                    c0, c1 = bank * 4, min(bank * 4 + 4, BC)
                    for f in range(2):
                        done(nc.vector.tensor_copy(back[:, c0:c1, f * P:(f + 1) * P],
                                                   turn[f][0:BR, bank, 0:(c1 - c0) * P].rearrange("p (c w) -> p c w", w=P)))
                    if heads:
                        done(nc.vector.tensor_copy(back[:, c0:c1, D:D + heads],
                                                   turn[2][0:BR, bank, 0:(c1 - c0) * P].rearrange("p (c w) -> p c w", w=P)[:, :, 0:heads]))
                dve.sem_inc(s_rows, 1)


def gather_sums(nc, k, tag, partial, W, sums):
    with ExitStack() as st:
        a = Names(nc, st)
        s_in = a.dma_sem(tag + "in")
        with nc.Block() as block:
            @block.gpsimd
            def _(pool):
                limit = pool.snap(pool.to_reg(PROWS - 1))
                for c in range(NT):
                    pool.indirect_dma_start(sums[:, c, 0:W], None, partial, bass.IndirectOffsetOnAxis(ap=k.sum_row[:, c:c + 1], axis=0),
                                            bounds_check=limit, oob_is_err=False).then_inc(s_in, 16)
                pool.wait_ge(s_in, 16 * NT)


def linear(nc, k, tag, source, chunks, weights, width, dest=None, relu=False, bias=None, types=1, stores=()):
    KC = chunks * types
    banks = -(-width // 512)
    with ExitStack() as st:
        a = Names(nc, st)
        turned = a.sb(tag + "turned", [P, 2, KC, P])
        masked = a.sb(tag + "masked", [P, 2, types, chunks * P])
        ring = a.sb(tag + "ring", [P, 2, width]) if dest is None else None
        flip = [a.ps(f"{tag}flip{n}", [P, max(KC * P, 512)]) for n in range(2)]
        acc = [a.ps(f"{tag}acc{n}", [P, 512 * banks]) for n in range(2)]
        s_mask, s_flip, s_turned, s_acc, s_out, s_seen = (a.sem(tag + n) for n in ("mask", "flip", "turned", "acc", "out", "seen"))
        s_store = [a.sem(f"{tag}store{n}") for n in range(2)]
        spans = [(lo, min(lo + 512, width)) for lo in range(0, width, 512)]
        with nc.Block() as block:
            @block.tensor
            def _(pe):
                def flips(c, n):
                    pe.wait_ge(s_mask, c + 1)
                    hold(pe, s_seen, s_turned, c - 1)
                    for q in range(KC):
                        last = nc.tensor.transpose(flip[n][:, q * P:(q + 1) * P],
                                                   masked[:, n, q // chunks, (q % chunks) * P:(q % chunks + 1) * P], k.ident[:, :])
                    last.then_inc(s_flip, 1)

                def step(c, n, b):
                    if not (isinstance(c, int) and c == NT - 1):
                        flips(c + 1, 1 - n)
                    pe.wait_ge(s_turned, c + 1)
                    wait(pe, s_out, c - 1)
                    for lo, hi in spans:
                        for q in range(KC):
                            last = nc.tensor.matmul(acc[n][:, lo:hi], turned[:, n, q, :], weights[:, q, lo:hi],
                                                    start=(q == 0), stop=(q == KC - 1 and bias is None))
                        if bias is not None:
                            last = nc.tensor.matmul(acc[n][:, lo:hi], k.ones[:, :], bias[:, lo:hi], start=False, stop=True)
                    last.then_inc(s_acc, 1)
                flips(0, 0)
                node_tiles(pe, step)

            @block.vector
            def _(dve):
                def step(c, n, b):
                    wait(dve, s_flip, c - 1)
                    if types > 1:
                        ins = nc.vector.tensor_tensor(masked[:, n, :, :],
                                                      source[:, bass.ds(c, 1), :].to_broadcast([P, types, chunks * P]),
                                                      bcast(k.mask[:, bass.ds(c * types, types)], chunks * P), ALU.mult)
                    else:
                        ins = nc.vector.tensor_copy(masked[:, n, :, :], source[:, bass.ds(c, 1), :])
                    ins.then_inc(s_mask, 1)
                node_tiles(dve, step)

            @block.scalar
            def _(act):
                def copy_turned(c, n):
                    act.wait_ge(s_flip, c + 1)
                    wait(act, s_acc, c - 1)
                    nc.scalar.copy(turned[:, n, :, :].rearrange("p q w -> p (q w)"), flip[n][:, 0:KC * P]).then_inc(s_turned, 1)

                def step(c, n, b):
                    if not (isinstance(c, int) and c == NT - 1):
                        copy_turned(c + 1, 1 - n)
                    act.wait_ge(s_acc, c + 1)
                    if dest is None:
                        wait(act, s_store[n], b * (16 * len(stores)))
                        out = ring[:, n, :]
                    else:
                        out = dest[:, bass.ds(c, 1), 0:width].rearrange("p o w -> p (o w)")
                    nc.scalar.activation(out, acc[n][:, 0:width], ACT.Relu if relu else ACT.Copy).then_inc(s_out, 1)
                copy_turned(0, 0)
                node_tiles(act, step)

            @block.sync
            def _(sp):
                def step(c, n, b):
                    sp.wait_ge(s_out, c + 1)
                    for table, col, lo, w in stores:
                        sp.dma_start(table[bass.ds(c * P, P), col:col + w], ring[:, n, lo:lo + w]).then_inc(s_store[n], 16)
                if stores:
                    node_tiles(sp, step)
                    for n in range(2):
                        sp.wait_ge(s_store[n], 16 * len(stores) * ((NT + 1 - n) // 2))


def normalise(nc, k, tag, y, eps, scale=None, add=None):
    split = NL * 3 if add is None else NT

    def tile(t, c):
        return t[:, bass.ds(c, 1), :].rearrange("p o w -> p (o w)")
    with ExitStack() as st:
        a = Names(nc, st)
        stats, mv = a.sb(tag + "stats", [P, NT, 6]), a.sb(tag + "mv", [P, NT, 2])
        std, inv, shift = a.sb(tag + "std", [P, NT]), a.sb(tag + "inv", [P, NT]), a.sb(tag + "shift", [P, NT])
        s_v, s_std, s_stats, s_apply, s_shift, s_scaled = (a.sem(tag + n) for n in ("v", "sstd", "sstats", "apply", "sshift", "scaled"))
        with nc.Block() as block:
            @block.vector
            def _(dve):
                def measure(b):
                    for j in range(NL):
                        last = nc.vector.bn_stats(tile(stats, b * NL + j), tile(y, b * NL + j))
                    last.then_inc(s_stats, 1)
                repeat(dve, NT // NL, measure)
                dve.wait_ge(s_stats, NT // NL)
                for c in range(NT):
                    last = nc.vector.bn_aggr(mv[:, c, :], stats[:, c, :])
                done = Chain(dve, s_v)
                done(last)
                done(nc.vector.tensor_scalar(shift[:, :], mv[:, :, 1], eps, None, ALU.add))
                dve.wait_ge(s_std, 1)
                done(nc.vector.reciprocal(inv[:, :], std[:, :]))
                if add is None:
                    ins = nc.vector.scalar_tensor_tensor(out=shift[:, :], in0=mv[:, :, 0], scalar=-1.0, in1=inv[:, :],
                                                         op0=ALU.mult, op1=ALU.mult)
                else:
                    ins = nc.vector.tensor_scalar(shift[:, :], mv[:, :, 0], -1.0, None, ALU.mult)
                ins.then_inc(s_shift, 1)
                dve.wait_ge(s_shift, 1)

                def apply(b):
                    for j in range(NL):
                        c = b * NL + j
                        if add is None:
                            nc.vector.tensor_scalar(tile(y, c), tile(y, c), inv[:, bass.ds(c, 1)], shift[:, bass.ds(c, 1)],
                                                    ALU.mult, ALU.add).then_inc(s_apply, 1)
                        else:
                            nc.vector.scalar_tensor_tensor(out=tile(y, c), in0=tile(y, c), scalar=shift[:, bass.ds(c, 1)],
                                                           in1=scale, op0=ALU.add, op1=ALU.mult).then_inc(s_apply, 1)
                repeat(dve, split // NL, apply)
                if add is not None:
                    dve.wait_ge(s_apply, split)

                    def finish(b):
                        for j in range(NL):
                            c = b * NL + j
                            nc.vector.scalar_tensor_tensor(out=tile(y, c), in0=tile(y, c), scalar=inv[:, bass.ds(c, 1)],
                                                           in1=tile(add, c), op0=ALU.mult, op1=ALU.add)
                    repeat(dve, NT // NL, finish)

            @block.scalar
            def _(act):
                act.wait_ge(s_v, 2)
                nc.scalar.activation(std[:, :], shift[:, :], ACT.Sqrt).then_inc(s_std, 1)
                act.wait_ge(s_shift, 1)

                def apply(b):
                    for j in range(NL):
                        c = b * NL + (j + split)
                        nc.scalar.activation(tile(y, c), tile(y, c), ACT.Identity, bias=shift[:, bass.ds(c, 1)], scale=inv[:, bass.ds(c, 1)])
                if split < NT:
                    repeat(act, (NT - split) // NL, apply)


def vector_steps(nc, k, tag, steps):
    with ExitStack() as st:
        a = Names(nc, st)
        s_v = a.sem(tag + "v")
        with nc.Block() as block:
            @block.vector
            def _(dve):
                done = Chain(dve, s_v)
                for step in steps:
                    done(step())


def zero_fill(nc, k, tag, *tensors):
    with ExitStack() as st:
        s_fill = Names(nc, st).sem(tag + "fill")
        with nc.Block() as block:
            @block.vector
            def _(dve):
                for t in tensors:
                    nc.vector.memset(t[:, :], 0.0).then_inc(s_fill, 1)


def copies(nc, k, tag, moves):
    with ExitStack() as st:
        a = Names(nc, st)
        s_dma = a.sem(tag + "dma")
        with nc.Block() as block:
            @block.sync
            def _(sp):
                for out, src in moves:
                    sp.dma_start(out, src).then_inc(s_dma, 16)
                sp.wait_ge(s_dma, 16 * len(moves))


def relate(nc, k, tag, kv, weights, table):
    with ExitStack() as st:
        a = Names(nc, st)
        rows = a.sb(tag + "rows", [P, 2, 2 * D])
        turned = a.sb(tag + "turned", [P, 2, 4 * P])
        ring = a.sb(tag + "ring", [P, 2, RELS, 2 * D])
        flip = [a.ps(f"{tag}flip{n}", [P, 512]) for n in range(2)]
        acc = [a.ps(f"{tag}acc{n}", [P, RELS * P]) for n in range(2)]
        s_load = [a.sem(f"{tag}load{n}") for n in range(2)]
        s_store = [a.dma_sem(f"{tag}store{n}") for n in range(2)]
        s_flip, s_turned, s_seen, s_seen2 = (a.sem(tag + n) for n in ("s_flip", "s_turned", "seen", "seen2"))
        s_acc = [a.sem(f"{tag}acc_s{n}") for n in range(2)]
        s_out = [a.sem(f"{tag}out{n}") for n in range(2)]

        def copied(eng, copy, c, n, b, side):
            wait(eng, s_store[n], b * 16)
            for q in (side, side + 2):
                eng.wait_ge(s_acc[side], c * 2 + (q // 2 + 1))
                copy(ring[:, n, :, q * P:(q + 1) * P], acc[side][:, :].rearrange("p (r w) -> p r w", w=P)).then_inc(s_out[side], 1)

        with nc.Block() as block:
            @block.sync
            def _(sp):
                def step(c, n, b):
                    wait(sp, s_flip, c - 1)
                    sp.dma_start(rows[:, n, :], kv[bass.ds(c * P, P), :]).then_inc(s_load[n], 16)
                node_tiles(sp, step)

            @block.gpsimd
            def _(pool):
                def step(c, n, b):
                    for side in range(2):
                        hold(pool, s_seen, s_out[side], c * 2 + 2)
                    pool.dma_start(table.rearrange("(r n) w -> n r w", r=RELS)[bass.ds(c * P, P), :, :],
                                   ring[:, n, :, :]).then_inc(s_store[n], 16)
                node_tiles(pool, step)
                for n in range(2):
                    pool.wait_ge(s_store[n], 16 * ((NT + 1 - n) // 2))

            @block.tensor
            def _(pe):
                def flips(c, n, b):
                    wait(pe, s_turned, c - 1)
                    hold(pe, s_seen2, s_load[n], b * 16 + 16)
                    for q in range(4):
                        last = nc.tensor.transpose(flip[n][:, q * P:(q + 1) * P], rows[:, n, q * P:(q + 1) * P], k.ident[:, :])
                    last.then_inc(s_flip, 1)

                def step(c, n, b):
                    if not (isinstance(c, int) and c == NT - 1):
                        flips(c + 1, 1 - n, b + n)
                    pe.wait_ge(s_turned, c + 1)
                    for q in range(4):
                        wait(pe, s_out[q % 2], c * 2 + q // 2)
                        for lo in range(0, RELS * P, 512):
                            last = nc.tensor.matmul(acc[q % 2][:, lo:lo + 512], turned[:, n, q * P:(q + 1) * P],
                                                    weights[:, q, lo:lo + 512], start=True, stop=True)
                        last.then_inc(s_acc[q % 2], 1)
                flips(0, 0, 0)
                node_tiles(pe, step)

            @block.scalar
            def _(act):
                def copy_turned(c, n):
                    act.wait_ge(s_flip, c + 1)
                    wait(act, s_acc[1], (c - 1) * 2)
                    nc.scalar.copy(turned[:, n, :], flip[n][:, :]).then_inc(s_turned, 1)

                def step(c, n, b):
                    if not (isinstance(c, int) and c == NT - 1):
                        copy_turned(c + 1, 1 - n)
                    copied(act, nc.scalar.copy, c, n, b, 0)
                copy_turned(0, 0)
                node_tiles(act, step)

            @block.vector
            def _(dve):
                node_tiles(dve, lambda c, n, b: copied(dve, nc.vector.tensor_copy, c, n, b, 1))


def relation_weights(nc, k, a, ins, out):
    dk = D // 4
    with ExitStack() as st:
        t = Names(nc, st)
        att = t.sb("rw_att", [P, 2, RELS, P])
        pri = t.sb("rw_pri", [P, 2 * RELS])
        flip = t.ps("rw_flip", [P, 2 * RELS, P])
        s_zero, s_load, s_flip, s_v = (t.sem("rw_" + n) for n in ("zero", "load", "flip", "v"))
        with nc.Block() as block:
            @block.gpsimd
            def _(pool):
                pool.memset(att[:, :, :, :], 0.0).then_inc(s_zero, 1)
                pool.memset(out[:, 2:4, :], 0.0).then_inc(s_zero, 1)

            @block.sync
            def _(sp):
                sp.wait_ge(s_zero, 2)
                for kc in range(2):
                    for h2 in range(2):
                        lo, hi = h2 * dk, (h2 + 1) * dk
                        sp.dma_start(att[lo:hi, kc, :, lo:hi], ins["relation_att"][:, 2 * kc + h2].rearrange("r d e -> d r e")).then_inc(s_load, 16)
                        sp.dma_start(out[lo:hi, 2 + kc, :].rearrange("p (r e) -> p r e", e=P)[:, :, lo:hi],
                                     ins["relation_msg"][:, 2 * kc + h2].rearrange("r d e -> d r e")).then_inc(s_load, 16)
                        with nc.allow_non_contiguous_dma("32 values"):
                            sp.dma_start(pri[lo:hi, kc * RELS:(kc + 1) * RELS],
                                         ins["relation_pri"][:, 2 * kc + h2].partition_broadcast(dk)).then_inc(s_load, 16)
                sp.wait_ge(s_load, 16 * 12)

            @block.tensor
            def _(pe):
                pe.wait_ge(s_load, 16 * 12)
                for kc in range(2):
                    for r in range(RELS):
                        last = nc.tensor.transpose(flip[:, kc * RELS + r, :], att[:, kc, r, :], k.ident[:, :])
                last.then_inc(s_flip, 1)

            @block.vector
            def _(dve):
                done = Chain(dve, s_v)
                dve.wait_ge(s_load, 16 * 12)
                done(nc.vector.tensor_scalar(pri[:, :], pri[:, :], float(dk) ** -0.5, None, ALU.mult))
                dve.wait_ge(s_flip, 1)
                done(nc.vector.tensor_tensor(out[:, 0:2, :].rearrange("p c (r w) -> p (c r) w", w=P), flip[:, :, :],
                                             bcast(pri[:, :], P), ALU.mult))


def node_constants(nc, k, ins):
    with ExitStack() as st:
        a = Names(nc, st)
        rows = a.sb("nc_rows", [NT, P], I32)
        rows_f = a.sb("nc_rows_f", [NT, P])
        kind = a.ps("nc_kind", [P, 512])
        gate = a.sb("nc_gate", [P, NT, TYPES])
        skip = a.sb("nc_skip", [P, TYPES])
        root = a.sb("nc_root", [P, NT])
        some = a.sb("nc_some", [P, NT])
        s_pad, s_load, s_v, s_row, s_kind, s_deg, s_root, s_exp = (a.sem("nc_" + n) for n in ("pad", "load", "v", "row", "skind", "deg", "sroot", "exp"))
        full = N_NODES // P
        with nc.Block() as block:
            @block.gpsimd
            def _(pool):
                pool.memset(rows[:, :], 0).then_inc(s_pad, 1)

            @block.sync
            def _(sp):
                sp.wait_ge(s_pad, 1)
                sp.dma_start(rows[0:full, :], ins["node_type"][0:full * P].rearrange("(t n) -> t n", n=P)).then_inc(s_load, 16)
                sp.dma_start(rows[full:full + 1, 0:N_NODES - full * P], ins["node_type"][full * P:N_NODES].rearrange("(t n) -> t n", t=1)).then_inc(s_load, 16)
                sp.dma_start(skip[:, :], ins["skip"].partition_broadcast(P)).then_inc(s_load, 16)

            @block.tensor
            def _(pe):
                pe.wait_ge(s_row, 1)
                nc.tensor.transpose(kind[:, 0:NT], rows_f[:, :], k.ident[0:NT, 0:NT]).then_inc(s_kind, 1)

            @block.scalar
            def _(act):
                act.wait_ge(s_load, 48)
                nc.scalar.activation(skip[:, :], skip[:, :], ACT.Exp, scale=-1.0).then_inc(s_exp, 1)
                act.wait_ge(s_deg, 1)
                nc.scalar.activation(root[:, :], some[:, :], ACT.Sqrt).then_inc(s_root, 1)

            @block.vector
            def _(dve):
                done = Chain(dve, s_v)
                dve.wait_ge(s_load, 48)
                done(nc.vector.tensor_copy(rows_f[:, :], rows[:, :]))
                dve.sem_inc(s_row, 1)
                done(nc.vector.tensor_scalar(some[:, :], k.deg[:, :], 1.0, None, ALU.max))
                dve.sem_inc(s_deg, 1)
                dve.wait_ge(s_exp, 1)
                done(nc.vector.tensor_scalar(skip[:, :], skip[:, :], 1.0, None, ALU.add))
                done(nc.vector.reciprocal(skip[:, :], skip[:, :]))
                dve.wait_ge(s_kind, 1)
                mask = k.mask[:, :].rearrange("p (c t) -> p c t", t=TYPES)
                for t in range(TYPES):
                    done(nc.vector.tensor_scalar(mask[:, :, t], kind[:, 0:NT], float(t), None, ALU.is_equal))
                done(nc.vector.tensor_tensor(gate[:, :, :], mask, mid(skip[:, :], NT), ALU.mult))
                done(nc.vector.tensor_reduce(k.gate[:, :], gate[:, :, :], AX.X, ALU.add))
                dve.wait_ge(s_root, 1)
                done(nc.vector.reciprocal(k.inv_root[:, :], root[:, :]))
                done(nc.vector.tensor_scalar(some[:, :], k.deg[:, :], 0.0, None, ALU.is_gt))
                done(nc.vector.tensor_tensor(k.inv_root[:, :], k.inv_root[:, :], some[:, :], ALU.mult))


def head_average(nc, k, tag, sums, out, heads):
    dk = D // heads

    def per_head(ap):
        return ap.rearrange("p c (h d) -> p c h d", d=dk)
    z = sums[:, :, D:D + heads]
    vector_steps(nc, k, tag, [
        lambda: nc.vector.tensor_scalar(z, z, 1e-16, None, ALU.max),
        lambda: nc.vector.reciprocal(z, z),
        lambda: nc.vector.tensor_tensor(per_head(out[:, :, 0:D]), per_head(sums[:, :, 0:D]),
                                        z.unsqueeze(3).to_broadcast([P, NT, heads, dk]), ALU.mult)])


def program(nc, ins, out):
    WMAX = D + 16
    full = N_NODES // P
    with ExitStack() as st:
        a = Names(nc, st)
        k = Shared(a)
        constants(nc, k)
        into = edge_order(nc, k, a, ins, "into_", ins["dst"], ins["src"], True)
        outof = edge_order(nc, k, a, ins, "outof_", ins["src"], ins["dst"], False)
        node_constants(nc, into, ins)
        bufs = [a.sb(f"nodes{n}", [P, NT, WMAX]) for n in range(3)]
        X, H, S = (b[:, :, 0:D] for b in bufs)

        def table(name, rows, width):
            return nc.dram_tensor(name, (rows, width), F32, kind="Internal").ap()

        def node_rows(t):
            return t.rearrange("(c p) w -> p c w", p=P)

        vector_steps(nc, k, "x0", [lambda: nc.vector.memset(X[:, full, :], 0.0)])
        copies(nc, k, "xl", [(X[:, 0:full, :], node_rows(ins["x"][0:full * P, :])),
                             (X[0:N_NODES - full * P, full, :], ins["x"][full * P:N_NODES, :])])

        t0, p0 = table("t0", NP, D), table("p0", PROWS, D)
        vector_steps(nc, k, "l0a", [lambda: nc.vector.tensor_tensor(H, X, bcast(k.inv_root[:, :], D), ALU.mult)])
        copies(nc, k, "l0b", [(node_rows(t0), H)])
        sum_edges(nc, into, "l0c", t0, p0, False)
        merge(nc, into, "l0d", p0, 0, None)
        gather_sums(nc, into, "l0e", p0, D, bufs[2])
        vector_steps(nc, k, "l0f", [lambda: nc.vector.tensor_tensor(S, S, bcast(k.inv_root[:, :], D), ALU.mult)])
        with ExitStack() as ws:
            w = Names(nc, ws).sb("l0w", [P, 2, D])
            copies(nc, k, "l0g", [(w[:, :, :], ins["W0"].rearrange("(q p) n -> p q n", p=P))])
            linear(nc, k, "l0h", S, 2, w, D, dest=H)
        vector_steps(nc, k, "l0i", [lambda: nc.vector.tensor_tensor(X, X, H, ALU.add)])
        normalise(nc, k, "l0j", X, 1e-5)

        t1, p1 = table("t1", NP, D), table("p1", PROWS, D)
        copies(nc, k, "l1a", [(node_rows(t1), X)])
        sum_edges(nc, outof, "l1b", t1, p1, True)
        merge(nc, outof, "l1c", p1, 0, None)
        gather_sums(nc, outof, "l1d", p1, D, bufs[2])
        with ExitStack() as ws:
            w = Names(nc, ws)
            w1, w2 = w.sb("l1w1", [P, 2, D]), w.sb("l1w2", [P, 2, D])
            b1, b2 = w.sb("l1b1", [P, D]), w.sb("l1b2", [P, D])
            eps, scale, offset = w.sb("l1eps", [P, 1]), w.sb("l1scale", [P, D]), w.sb("l1offset", [P, D])
            zero_fill(nc, k, "l1z", b1, b2)
            copies(nc, k, "l1e", [(w1[:, :, :], ins["W1"].rearrange("(q p) n -> p q n", p=P)),
                                  (w2[:, :, :], ins["W2"].rearrange("(q p) n -> p q n", p=P)),
                                  (b1[0:1, :], ins["b1"].rearrange("(a n) -> a n", a=1)), (b2[0:1, :], ins["b2"].rearrange("(a n) -> a n", a=1)),
                                  (eps[:, :], ins["eps"].partition_broadcast(P)), (scale[:, :], ins["scale"].partition_broadcast(P)),
                                  (offset[:, :], ins["offset"].partition_broadcast(P))])
            vector_steps(nc, k, "l1f", [
                lambda: nc.vector.tensor_scalar(eps[:, :], eps[:, :], 1.0, None, ALU.add),
                lambda: nc.vector.scalar_tensor_tensor(out=S, in0=X, scalar=eps[:, 0:1], in1=S, op0=ALU.mult, op1=ALU.add)])
            linear(nc, k, "l1g", S, 2, w1, D, dest=H, relu=True, bias=b1)
            linear(nc, k, "l1h", H, 2, w2, D, dest=S, relu=True, bias=b2)
            vector_steps(nc, k, "l1o", [lambda: nc.vector.tensor_tensor(X, X, mid(offset[:, :], NT), ALU.add)])
            normalise(nc, k, "l1i", S, 1e-10, scale=scale[:, :], add=X)
        normalise(nc, k, "l1j", S, 1e-5)
        bufs = [bufs[2], bufs[1], bufs[0]]
        X, H, S = (b[:, :, 0:D] for b in bufs)

        qv2, k2, p2 = table("qv2", NP, 2 * D), table("k2", NP, D), table("p2", PROWS, D + 16)
        with ExitStack() as ws:
            w = Names(nc, ws)
            wq, bq = w.sb("l2w", [P, 2, 3 * D]), w.sb("l2b", [P, 3 * D])
            zero_fill(nc, k, "l2z", bq)
            copies(nc, k, "l2a", [m for n, (wt, bt) in enumerate(((ins["Wq"], ins["bq"]), (ins["Wv"], ins["bv"]), (ins["Wk"], ins["bk"])))
                                  for m in ((wq[:, :, n * D:(n + 1) * D], wt.rearrange("(q p) n -> p q n", p=P)),
                                            (bq[0:1, n * D:(n + 1) * D], bt.rearrange("(a n) -> a n", a=1)))])
            linear(nc, k, "l2b", X, 2, wq, 3 * D, bias=bq, stores=((qv2, 0, 0, 2 * D), (k2, 0, 2 * D, D)))
        pair_rows = table("pair_rows", PAIRS, D)
        spread_rows(nc, into, "l2s", k2, pair_rows)
        attend_edges(nc, into, "l2c", qv2, into.other_idx, NP, pair_rows, 8, 32.0 ** -0.5, p2, bufs[1:])
        merge(nc, into, "l2d", p2, 8, 32.0 ** -0.5)
        gather_sums(nc, into, "l2e", p2, D + 16, bufs[2])
        head_average(nc, k, "l2f", bufs[2], bufs[1], 8)
        vector_steps(nc, k, "l2g", [lambda: nc.vector.tensor_tensor(X, X, H, ALU.add)])
        normalise(nc, k, "l2h", X, 1e-5)

        kv3, q3 = table("kv3", NP, 2 * D), table("q3", NP, D)
        r3, p3 = table("r3", RELS * NP, 2 * D), table("p3", PROWS, D + 8)
        with ExitStack() as ws:
            w3 = Names(nc, ws).sb("l3w", [P, 2 * TYPES, 3 * D])
            copies(nc, k, "l3a", [(w3[:, 2 * t:2 * t + 2, n * D:(n + 1) * D], wt[t].rearrange("(q p) n -> p q n", p=P))
                                  for n, wt in enumerate((ins["k_linears"], ins["v_linears"], ins["q_linears"])) for t in range(TYPES)])
            linear(nc, k, "l3b", X, 2, w3, 3 * D, types=TYPES, stores=((kv3, 0, 0, 2 * D), (q3, 0, 2 * D, D)))
        with ExitStack() as ws:
            wr = Names(nc, ws).sb("l3r", [P, 4, RELS * P])
            relation_weights(nc, k, a, ins, wr)
            relate(nc, k, "l3c", kv3, wr, r3)
        spread_rows(nc, into, "l3s", q3, pair_rows)
        attend_edges(nc, into, "l3d", r3, into.rel_idx, RELS * NP, pair_rows, 4, 1.0, p3, bufs[1:])
        merge(nc, into, "l3e", p3, 4, 1.0)
        gather_sums(nc, into, "l3f", p3, D + 8, bufs[2])
        head_average(nc, k, "l3g", bufs[2], bufs[1], 4)
        with ExitStack() as ws:
            wa = Names(nc, ws).sb("l3wa", [P, 2 * TYPES, D])
            copies(nc, k, "l3h", [(wa[:, 2 * t:2 * t + 2, :], ins["a_linears"][t].rearrange("(q p) n -> p q n", p=P)) for t in range(TYPES)])
            linear(nc, k, "l3i", H, 2, wa, D, dest=S, types=TYPES)
        vector_steps(nc, k, "l3j", [lambda: nc.vector.tensor_tensor(S, S, bcast(k.gate[:, :], D), ALU.mult),
                                    lambda: nc.vector.tensor_tensor(X, X, S, ALU.add)])
        normalise(nc, k, "l3k", X, 1e-5)
        copies(nc, k, "l3l", [(node_rows(out[0:full * P, :]), X[:, 0:full, :]),
                              (out[full * P:N_NODES, :], X[0:N_NODES - full * P, full, :])])


_INS = {"x": "x", "src": "src", "dst": "dst", "edge_type_8": "etype", "edge_weight": "weight", "node_type_4": "node_type",
        "L0_gnn_W": "W0", "L1_gnn_W1": "W1", "L1_gnn_b1": "b1", "L1_gnn_W2": "W2", "L1_gnn_b2": "b2", "L1_gnn_eps": "eps",
        "L1_gnn_offset": "offset", "L1_gnn_scale": "scale", "L2_gnn_Wq": "Wq", "L2_gnn_bq": "bq", "L2_gnn_Wk": "Wk",
        "L2_gnn_bk": "bk", "L2_gnn_Wv": "Wv", "L2_gnn_bv": "bv", "L3_gnn_k_linears": "k_linears",
        "L3_gnn_q_linears": "q_linears", "L3_gnn_v_linears": "v_linears", "L3_gnn_a_linears": "a_linears",
        "L3_gnn_relation_att": "relation_att", "L3_gnn_relation_msg": "relation_msg",
        "L3_gnn_relation_pri": "relation_pri", "L3_gnn_skip": "skip"}


def kernel(x, src, dst, edge_type_8, edge_weight, node_type_4, L0_gnn_W, L1_gnn_W1, L1_gnn_b1, L1_gnn_W2, L1_gnn_b2,
           L1_gnn_eps, L1_gnn_offset, L1_gnn_scale, L2_gnn_Wq, L2_gnn_bq, L2_gnn_Wk, L2_gnn_bk, L2_gnn_Wv, L2_gnn_bv,
           L3_gnn_k_linears, L3_gnn_q_linears, L3_gnn_v_linears, L3_gnn_a_linears, L3_gnn_relation_att,
           L3_gnn_relation_msg, L3_gnn_relation_pri, L3_gnn_skip):
    import numpy as _np
    import concourse.bacc as _bacc
    from concourse.bass_utils import run_bass_kernel_spmd as _run

    given = dict(x=x, src=src, dst=dst, edge_type_8=edge_type_8, edge_weight=edge_weight, node_type_4=node_type_4,
                 L0_gnn_W=L0_gnn_W, L1_gnn_W1=L1_gnn_W1, L1_gnn_b1=L1_gnn_b1, L1_gnn_W2=L1_gnn_W2, L1_gnn_b2=L1_gnn_b2,
                 L1_gnn_eps=L1_gnn_eps, L1_gnn_offset=L1_gnn_offset, L1_gnn_scale=L1_gnn_scale, L2_gnn_Wq=L2_gnn_Wq,
                 L2_gnn_bq=L2_gnn_bq, L2_gnn_Wk=L2_gnn_Wk, L2_gnn_bk=L2_gnn_bk, L2_gnn_Wv=L2_gnn_Wv, L2_gnn_bv=L2_gnn_bv,
                 L3_gnn_k_linears=L3_gnn_k_linears, L3_gnn_q_linears=L3_gnn_q_linears, L3_gnn_v_linears=L3_gnn_v_linears,
                 L3_gnn_a_linears=L3_gnn_a_linears, L3_gnn_relation_att=L3_gnn_relation_att,
                 L3_gnn_relation_msg=L3_gnn_relation_msg, L3_gnn_relation_pri=L3_gnn_relation_pri, L3_gnn_skip=L3_gnn_skip)
    nc = _bacc.Bacc("TRN2", target_bir_lowering=False, num_devices=1)
    arrays, aps = {}, {}
    for name, short in _INS.items():
        v = _np.ascontiguousarray(given[name])
        arrays["in_" + name] = v
        aps[short] = nc.dram_tensor("in_" + name, v.shape, mybir.dt.from_np(v.dtype), kind="ExternalInput").ap()
    out = nc.dram_tensor("out_0", (N_NODES, D), F32, kind="ExternalOutput").ap()
    program(nc, aps, out)
    r = _run(nc, [arrays], core_ids=[0])
    return r.results[0]["out_0"]
```

```python
import concourse.bass as bass
from concourse import mybir
from contextlib import ExitStack

F32 = mybir.dt.float32
BF16 = mybir.dt.bfloat16
F16 = mybir.dt.float16
I32 = mybir.dt.int32
ALU = mybir.AluOpType
ACT = mybir.ActivationFunctionType
AX = mybir.AxisListType

P = 128
D = 256
N_NODES, N_EDGES = 3125, 50000
NT = -(-N_NODES // P)
NP = NT * P
PAD_NODE = NP - 1
GT = 7
HALVES = 2
BODY = GT * HALVES
NB = -(-N_EDGES // (P * BODY))
TILES = NB * BODY
EP = TILES * P
CH = 4
ROWS = TILES // CH
NBR = 2 * TILES
BC = 7
BR = NBR // BC
MERGED = EP
ZERO_ROW = EP + NBR
PROWS = ZERO_ROW + 1
NL = 5
PAIR_BLOCKS = -(-(NP + TILES) // P) + 1
PAIRS = PAIR_BLOCKS * P
RELS, TYPES = 8, 4
KT = -(-(NP + (TYPES - 1) * (P - 1)) // P) | 1
BIG = 1.0e30
assert ROWS * CH == TILES and BR * BC == NBR and NT % NL == 0


class Chain:

    def __init__(self, eng, sem, base=0):
        self.eng, self.sem, self.base, self.n = eng, sem, base, 0

    def __call__(self, ins):
        self.n += 1
        ins.then_inc(self.sem, 1)
        self.eng.wait_ge(self.sem, self.base + self.n)


def wait(eng, sem, value):
    if isinstance(value, int) and value <= 0:
        return
    eng.wait_ge(sem, value)


def hold(eng, seen, sem, value):
    wait(eng, sem, value)
    eng.sem_inc(seen, 1)


def repeat(eng, count, body):
    body(0)
    if count > 1:
        with eng.Fori(1, count) as b:
            body(b)


class Names:

    def __init__(self, nc, stack):
        self.nc, self.stack = nc, stack

    def sb(self, name, shape, dt=F32):
        return self.stack.enter_context(self.nc.sbuf_tensor(name, shape, dt))

    def ps(self, name, shape, dt=F32):
        return self.stack.enter_context(self.nc.psum_tensor(name, shape, dt))

    def sem(self, name):
        handle = self.nc.alloc_semaphore(name=name)
        self.stack.callback(self.nc.release_semaphore, handle)
        self.stack.callback(self.nc.gpsimd.sem_clear, handle)
        return handle

    def dma_sem(self, name):
        return self.nc.alloc_semaphore(name=name)


def node_tiles(eng, step, tiles=NT):
    def body(b):
        for n in range(2):
            step(b * 2 + n, n, b)
    repeat(eng, tiles // 2, body)
    for c in range(tiles // 2 * 2, tiles):
        step(c, 0, tiles // 2)


def repeat_between(eng, count, body):
    body(0)
    with eng.Fori(1, count - 1) as b:
        body(b)
    body(count - 1)


def bcast(ap, count):
    return ap.unsqueeze(2).to_broadcast([ap.shape[0], ap.shape[1], count])


def mid(ap, count):
    return ap.unsqueeze(1).to_broadcast([ap.shape[0], count, ap.shape[1]])


def constants(nc, k):
    with ExitStack() as st:
        a = Names(nc, st)
        s_fill = a.sem("c_fill")
        with nc.Block() as block:
            @block.gpsimd
            def _(pool):
                done = Chain(pool, s_fill)
                nc.gpsimd.iota(k.iota[:, :], [[1, P]], base=0, channel_multiplier=0,
                               allow_small_or_imprecise_dtypes=True)
                pool.memset(k.ident[:, :], 0.0)
                pool.memset(k.tri[:, :], 1.0)
                pool.memset(k.zeros_bf[:, :], 0.0)
                pool.memset(k.ones[:, :], 1.0)
                done(pool.memset(k.tri_hi[:, :], 1.0))
                pool.affine_select(out=k.ident[:, :], in_=k.ident[:, :], compare_op=ALU.not_equal, fill=1.0,
                                   base=0, pattern=[[-1, P]], channel_multiplier=1)
                pool.affine_select(out=k.tri[:, :], in_=k.tri[:, :], compare_op=ALU.is_gt, fill=0.0,
                                   base=0, pattern=[[-1, P]], channel_multiplier=1)
                done(pool.affine_select(out=k.tri_hi[:, :], in_=k.tri_hi[:, :], compare_op=ALU.is_gt, fill=0.0,
                                        base=0, pattern=[[1, P]], channel_multiplier=-1))
                nc.gpsimd.iota(k.minus_p[:, :], [[0, 1]], base=0, channel_multiplier=-1,
                               allow_small_or_imprecise_dtypes=True)
                done(nc.gpsimd.tensor_copy(k.ident_bf[:, :], k.ident[:, :]))


def load_rows(sp, rows, source, sem):
    full = N_EDGES // P
    c, r = full // ROWS, full % ROWS
    sp.dma_start(rows[:, 0:c, :], source[0:c * ROWS * P].rearrange("(c t e) -> t c e", t=ROWS, e=P)).then_inc(sem, 16)
    sp.dma_start(rows[0:r, c, :], source[c * ROWS * P:full * P].rearrange("(t e) -> t e", e=P)).then_inc(sem, 16)
    sp.dma_start(rows[r:r + 1, c, 0:N_EDGES - full * P],
                 source[full * P:N_EDGES].rearrange("(t e) -> t e", t=1)).then_inc(sem, 16)


def edge_columns(nc, k, other, key, etype, weight):
    with ExitStack() as st:
        a = Names(nc, st)
        rows_i = a.sb(k.tag + "ec_rows_i", [ROWS, 3, CH, P], I32)
        rows_w = a.sb(k.tag + "ec_rows_w", [ROWS, CH, P])
        rows_f = a.sb(k.tag + "ec_rows_f", [ROWS, 3, CH, P])
        key_i = a.sb(k.tag + "ec_key_i", [P, 3, TILES], I32)
        rec_rows = a.sb(k.tag + "ec_rec_rows", [ROWS, CH, P, 4])
        following = a.sb(k.tag + "ec_following", [ROWS, CH, P])
        falls = a.sb(k.tag + "ec_falls", [ROWS, CH, P])
        fall_sum = a.sb(k.tag + "ec_fall_sum", [ROWS, 1])
        turned = a.ps(k.tag + "ec_turned", [P, 4, CH, P])
        total = a.ps(k.tag + "ec_total", [P, 1])
        s_pad, s_load, s_row, s_turn, s_col, s_store, s_next, s_rec, s_fall, s_total = (
            a.sem(k.tag + "ec_" + n) for n in ("pad", "load", "row", "turn", "col", "store", "next", "rec", "fall", "stotal"))
        with nc.Block() as block:
            @block.gpsimd
            def _(pool):
                pool.memset(rows_i[:, 0, :, :], 0).then_inc(s_pad, 1)
                pool.memset(rows_i[:, 1, :, :], PAD_NODE).then_inc(s_pad, 1)
                pool.memset(rows_i[:, 2, :, :], 0).then_inc(s_pad, 1)
                pool.memset(rows_w[:, :, :], 0.0).then_inc(s_pad, 1)

            @block.sync
            def _(sp):
                sp.wait_ge(s_pad, 4)
                load_rows(sp, rows_i[:, 0, :, :], other, s_load)
                load_rows(sp, rows_i[:, 1, :, :], key, s_load)
                load_rows(sp, rows_i[:, 2, :, :], etype, s_load)
                load_rows(sp, rows_w[:, :, :], weight, s_load)
                sp.wait_ge(s_row, 1)
                sp.dma_start(k.key_pad.rearrange("(c t e) -> t c e", t=ROWS, e=P), rows_f[:, 1, :, :]).then_inc(s_store, 16)
                sp.wait_ge(s_store, 16)
                first = k.key_pad[P:EP].rearrange("(t e) -> t e", e=P)[:, 0:1]
                for c in range(CH):
                    n = min(ROWS, TILES - 1 - c * ROWS)
                    with nc.allow_non_contiguous_dma("a value of each tile"):
                        sp.dma_start(following[0:n, c, P - 1:P], first[c * ROWS:c * ROWS + n, :]).then_inc(s_next, 16)
                sp.wait_ge(s_rec, 4)
                sp.dma_start(k.rec_sorted.rearrange("(c t e) q -> t c (e q)", t=ROWS, e=P),
                             rec_rows[:, :, :, :].rearrange("t c e q -> t c (e q)")).then_inc(s_store, 16)
                sp.wait_ge(s_store, 32)

            @block.vector
            def _(dve):
                dve.wait_ge(s_load, 16 * 12)
                nc.vector.memset(following[:, :, P - 1:P], float(PAD_NODE))
                nc.vector.tensor_copy(rows_f[:, :, :, :], rows_i[:, :, :, :]).then_inc(s_row, 1)
                dve.wait_ge(s_row, 1)
                for n in range(4):
                    nc.vector.tensor_copy(rec_rows[:, :, :, n], rows_w[:, :, :] if n == 3 else rows_f[:, n, :, :]).then_inc(s_rec, 1)
                nc.vector.tensor_copy(following[:, :, 0:P - 1], rows_f[:, 1, :, 1:P]).then_inc(s_fall, 1)
                dve.wait_ge(s_fall, 1)
                dve.wait_ge(s_next, 16 * CH)
                nc.vector.tensor_tensor(falls[:, :, :], rows_f[:, 1, :, :], following[:, :, :], ALU.is_gt).then_inc(s_fall, 1)
                dve.wait_ge(s_fall, 2)
                nc.vector.tensor_reduce(fall_sum[:, :], falls[:, :, :], AX.XY, ALU.add).then_inc(s_fall, 1)
                dve.wait_ge(s_total, 1)
                nc.vector.tensor_copy(k.unsorted[:, :], total[:, :]).then_inc(s_fall, 1)
                dve.wait_ge(s_turn, 1)
                done = Chain(dve, s_col)
                for n in range(4):
                    last = nc.vector.tensor_copy(k.rec[:, :, n].rearrange("p (c t) -> p c t", c=CH), turned[:, n, :, 0:ROWS])
                    done(last)
                done(nc.vector.tensor_copy(k.key_col[:, 0:TILES], k.rec[:, :, 1]))
                done(nc.vector.tensor_copy(key_i[:, 0, :], k.rec[:, :, 1]))
                done(nc.vector.tensor_scalar(key_i[:, 1, :], key_i[:, 0, :], 7, None, ALU.logical_shift_right))
                done(nc.vector.tensor_scalar(key_i[:, 2, :], key_i[:, 0, :], P - 1, None, ALU.bitwise_and))
                done(nc.vector.tensor_copy(k.hi_col[:, 0:TILES], key_i[:, 1, :]))
                done(nc.vector.tensor_copy(k.lo_col[:, 0:TILES], key_i[:, 2, :]))
                for pad in (k.hi_col, k.lo_col):
                    done(nc.vector.memset(pad[:, TILES:TILES + GT], 0.0))

            @block.tensor
            def _(pe):
                pe.wait_ge(s_row, 1)
                for n in range(4):
                    for c in range(CH):
                        source = rows_w[:, c, :] if n == 3 else rows_f[:, n, c, :]
                        last = nc.tensor.transpose(turned[:, n, c, 0:ROWS], source, k.ident[0:ROWS, 0:ROWS])
                last.then_inc(s_turn, 1)
                pe.wait_ge(s_fall, 3)
                nc.tensor.matmul(total[:, :], k.ones[0:ROWS, :], fall_sum[:, :], start=True, stop=True).then_inc(s_total, 1)


def degrees(nc, k):
    with ExitStack() as st:
        a = Names(nc, st)
        hot_hi = a.sb(k.tag + "dg_hot_hi", [P, 2, GT, NT], BF16)
        hot_lo = a.sb(k.tag + "dg_hot_lo", [P, 2, GT, P], BF16)
        hist = a.ps(k.tag + "dg_hist", [NT, P])
        s_hot, s_used, s_free, s_tot, s_pre, s_v, s_t, s_tt = (a.sem(k.tag + "dg_" + n) for n in
                                                 ("hot", "used", "free", "tot", "pre", "v", "t", "tt"))
        deg = a.sb(k.tag + "dg_deg", [NT, P])
        incl = a.sb(k.tag + "dg_incl", [NT, P])
        before = a.ps(k.tag + "dg_before", [NT, 1])
        ends = a.sb(k.tag + "dg_ends", [NT, 4, P])
        ei = a.sb(k.tag + "dg_ei", [NT, 8, P], I32)
        ef = a.sb(k.tag + "dg_ef", [NT, 8, P])
        turned = a.ps(k.tag + "dg_turned", [P, 3, 32])
        pairs = a.sb(k.tag + "dg_pairs", [NT, 3, P])
        spare = a.sb(k.tag + "dg_spare", [NT, P])
        s_spare, s_count, s_shift = (a.sem(k.tag + "dg_" + n) for n in ("sspare", "count", "shift"))
        with nc.Block() as block:
            @block.vector
            def _(dve):
                def body(b):
                    for h in range(HALVES):
                        cols = bass.ds(b * BODY + h * GT, GT)
                        wait(dve, s_free, b * 2 + (h - 1))
                        nc.vector.tensor_tensor(hot_hi[:, h, :, :], mid(k.iota[:, 0:NT], GT), bcast(k.hi_col[:, cols], NT), ALU.is_equal)
                        nc.vector.tensor_tensor(hot_lo[:, h, :, :], mid(k.iota[:, :], GT), bcast(k.lo_col[:, cols], P), ALU.is_equal).then_inc(s_hot, 1)
                repeat(dve, NB, body)
                dve.wait_ge(s_used, 1)
                done = Chain(dve, s_v)
                done(nc.vector.tensor_copy(deg[:, :], hist[:, :]))
                done(nc.vector.memset(ef[:, 0, :], 0.0))
                done(nc.vector.tensor_tensor_scan(incl[:, :], ef[:, 0, :], deg[:, :], 0.0, ALU.add, ALU.add))
                dve.sem_inc(s_tot, 1)
                dve.wait_ge(s_pre, 1)
                e0, e1 = ends[:, 0, :], ends[:, 1, :]
                done(nc.vector.tensor_scalar(e1, incl[:, :], before[:, 0:1], None, ALU.add))
                done(nc.vector.tensor_tensor(e0, e1, deg[:, :], ALU.subtract))
                done(nc.vector.tensor_copy(k.first_pos[:, :], e0))
                done(nc.vector.tensor_scalar(ends[:, 2, :], e1, 1.0, 0.0, ALU.subtract, ALU.max))
                done(nc.vector.tensor_copy(ei[:, 0, :], e0))
                done(nc.vector.tensor_copy(ei[:, 1, :], e1))
                done(nc.vector.tensor_copy(ei[:, 2, :], ends[:, 2, :]))
                done(nc.vector.tensor_scalar(ei[:, 3, :], ei[:, 0, :], 7, None, ALU.logical_shift_right))
                done(nc.vector.tensor_scalar(ei[:, 4, :], ei[:, 2, :], 7, None, ALU.logical_shift_right))
                done(nc.vector.tensor_scalar(ei[:, 5, :], ei[:, 1, :], P - 1, None, ALU.bitwise_and))
                done(nc.vector.tensor_copy(ef[:, 3:6, :], ei[:, 3:6, :]))
                t0, t1, tail = ef[:, 3, :], ef[:, 4, :], ef[:, 5, :]
                if k.attention:
                    touched, upto, row = (pairs[:, n, :] for n in range(3))
                    done(nc.vector.tensor_scalar(row, deg[:, :], 0.0, None, ALU.is_gt))
                    done(nc.vector.scalar_tensor_tensor(out=touched, in0=t1, scalar=1.0, in1=t0, op0=ALU.add, op1=ALU.subtract))
                    done(nc.vector.tensor_tensor(touched, touched, row, ALU.mult))
                    done(nc.vector.tensor_tensor_scan(upto, ef[:, 0, :], touched, 0.0, ALU.add, ALU.add))
                    dve.sem_inc(s_count, 1)
                    dve.wait_ge(s_shift, 1)
                    dve.wait_ge(s_spare, 1)
                    done(nc.vector.tensor_scalar(upto, upto, before[:, 0:1], None, ALU.add))
                    done(nc.vector.tensor_tensor(upto, upto, touched, ALU.subtract))
                    done(nc.vector.tensor_tensor(upto, upto, spare[:, :], ALU.subtract))
                    done(nc.vector.tensor_tensor(upto, upto, row, ALU.mult))
                    done(nc.vector.tensor_tensor(row, upto, spare[:, :], ALU.add))
                last, same, none, inside, across = (ef[:, n, :] for n in (6, 7, 0, 1, 2))
                done(nc.vector.tensor_scalar(last, tail, 0.0, None, ALU.is_equal))
                done(nc.vector.tensor_tensor(same, t0, t1, ALU.is_equal))
                done(nc.vector.tensor_scalar(inside, t0, float(P), float(P - 1), ALU.mult, ALU.add))
                done(nc.vector.tensor_tensor(inside, inside, e0, ALU.subtract))
                done(nc.vector.tensor_tensor(inside, inside, last, ALU.mult))
                done(nc.vector.tensor_tensor(inside, inside, e0, ALU.add))
                done(nc.vector.tensor_scalar(across, t1, 2.0, float(MERGED), ALU.mult, ALU.add))
                done(nc.vector.tensor_tensor(across, across, last, ALU.add))
                done(nc.vector.tensor_tensor(inside, inside, across, ALU.subtract))
                done(nc.vector.tensor_tensor(inside, inside, same, ALU.mult))
                done(nc.vector.tensor_tensor(inside, inside, across, ALU.add))
                done(nc.vector.tensor_scalar(none, deg[:, :], 0.0, None, ALU.is_equal))
                done(nc.vector.tensor_scalar(across, inside, -1.0, float(ZERO_ROW), ALU.mult, ALU.add))
                done(nc.vector.tensor_tensor(across, across, none, ALU.mult))
                done(nc.vector.tensor_tensor(inside, inside, across, ALU.add))
                dve.sem_inc(s_t, 1)
                dve.wait_ge(s_tt, 1)
                done(nc.vector.tensor_copy(k.sum_row[:, :], turned[:, 0, 0:NT]))
                done(nc.vector.tensor_copy(k.deg[:, :], turned[:, 1, 0:NT]))
                if k.attention:
                    done(nc.vector.tensor_copy(k.pair_row[:, :], turned[:, 2, 0:NT]))

            @block.gpsimd
            def _(pool):
                nc.gpsimd.iota(spare[:, :], [[1, P]], base=PAIRS, channel_multiplier=P,
                               allow_small_or_imprecise_dtypes=True).then_inc(s_spare, 1)

            @block.tensor
            def _(pe):
                nc.tensor.matmul(hist[:, :], k.zeros_bf[:, 0:NT], k.zeros_bf[:, :], start=True, stop=False)
                def body(b):
                    for h in range(HALVES):
                        pe.wait_ge(s_hot, b * 2 + (h + 1))
                        for j in range(GT):
                            last = nc.tensor.matmul(hist[:, :], hot_hi[:, h, j, :], hot_lo[:, h, j, :],
                                                    start=False, stop=False)
                        last.then_inc(s_free, 1)
                repeat(pe, NB, body)
                nc.tensor.matmul(hist[:, :], k.zeros_bf[:, 0:NT], k.zeros_bf[:, :], start=False, stop=True).then_inc(s_used, 1)
                pe.wait_ge(s_tot, 1)
                nc.tensor.matmul(before[:, :], k.tri_hi[0:NT, 0:NT], incl[:, P - 1:P], start=True, stop=True).then_inc(s_pre, 1)
                if k.attention:
                    pe.wait_ge(s_count, 1)
                    nc.tensor.matmul(before[:, :], k.tri_hi[0:NT, 0:NT], pairs[:, 1, P - 1:P], start=True, stop=True).then_inc(s_shift, 1)
                pe.wait_ge(s_t, 1)
                if k.attention:
                    nc.tensor.transpose(turned[:, 2, 0:NT], pairs[:, 2, :], k.ident[0:NT, 0:NT])
                nc.tensor.transpose(turned[:, 0, 0:NT], ef[:, 1, :], k.ident[0:NT, 0:NT])
                nc.tensor.transpose(turned[:, 1, 0:NT], deg[:, :], k.ident[0:NT, 0:NT]).then_inc(s_tt, 1)



def key_falls(nc, k, eng, kind):
    return eng.to_reg(nc.values_load(k.unsorted[0:1, 0:1], engines=(mybir.EngineType[kind],), min_val=0, max_val=EP))


def ranks(nc, k):
    with ExitStack() as st:
        a = Names(nc, st)
        hot_hi = a.sb(k.tag + "rk_hot_hi", [P, 2, GT, NT], BF16)
        hot_lo = a.sb(k.tag + "rk_hot_lo", [P, 2, GT, P], BF16)
        hot_hi_t = a.sb(k.tag + "rk_hot_hi_t", [NT, 2, GT, P], F16)
        snap = a.sb(k.tag + "rk_snap", [NT, 2, GT, P], F16)
        base = a.sb(k.tag + "rk_base", [NT, P])
        parts = a.sb(k.tag + "rk_parts", [NT, 2, 2, P], F16)
        key_row = a.sb(k.tag + "rk_key_row", [P, 2, GT * P])
        key_ring = a.sb(k.tag + "rk_key_ring", [P, 2, GT])
        junk = a.sb(k.tag + "rk_junk", [P, 2 * GT, P])
        part = a.sb(k.tag + "rk_part", [P, 2, 2 * GT])
        index = a.sb(k.tag + "rk_index", [P, 2, GT], I32)
        rec_ring = a.sb(k.tag + "rk_rec_ring", [P, 2, GT, 4])
        table = a.ps(k.tag + "rk_table", [NT, GT + 1, P])
        picked = [a.ps(k.tag + f"rk_picked{h}", [P, 8, P]) for h in range(2)]
        turned = [a.ps(k.tag + f"rk_turned{h}", [NT, 8, P], BF16) for h in range(2)]
        s_row = [a.sem(k.tag + f"rk_row{h}") for h in range(2)]
        s_scat = [a.dma_sem(k.tag + f"rk_scat{h}") for h in range(2)]
        s_hot, s_turn, s_turned, s_snap, s_table, s_pick, s_index, s_v, s_seen, s_free, s_taken, s_base = (
            a.sem(k.tag + "rk_" + n) for n in ("hot", "turn", "turned", "snap", "stable", "pick", "index", "v", "seen", "free", "taken", "sbase"))
        with nc.Block() as block:
            @block.sync
            def _(sp):
                with sp.If_ne(key_falls(nc, k, sp, "SP"), 0):
                    def body(b):
                        for h in range(HALVES):
                            wait(sp, s_free, b * 2 + (h - 1))
                            sp.dma_start(key_row[:, h, :], k.key_pad[bass.ds(b * (BODY * P) + h * GT * P, GT * P)]
                                         .partition_broadcast(P)).then_inc(s_row[h], 16)
                    repeat(sp, NB, body)

            @block.vector
            def _(dve):
                with dve.If_ne(key_falls(nc, k, dve, "DVE"), 0):
                    PER = 2 * 6

                    def one_hots(h, tile):
                        cols = bass.ds(tile, GT)
                        nc.vector.tensor_tensor(hot_hi[:, h, :, :], mid(k.iota[:, 0:NT], GT), bcast(k.hi_col[:, cols], NT), ALU.is_equal)
                        return nc.vector.tensor_tensor(hot_lo[:, h, :, :], mid(k.iota[:, :], GT), bcast(k.lo_col[:, cols], P), ALU.is_equal)

                    def split_base(done, h):
                        done(nc.vector.tensor_copy(parts[:, h, 0, :], base[:, :]))
                        done(nc.vector.tensor_tensor(parts[:, h, 1, :], base[:, :], parts[:, h, 0, :], ALU.subtract))
                        dve.sem_inc(s_base, 1)

                    start = Chain(dve, s_v)
                    start(one_hots(0, 0))
                    dve.sem_inc(s_hot, 1)
                    start(nc.vector.tensor_copy(base[:, :], k.first_pos[:, :]))
                    split_base(start, 0)

                    def body(b):
                        done = Chain(dve, s_v, b * PER + start.n)
                        for h in range(HALVES):
                            cols = bass.ds(b * BODY + h * GT, GT)
                            nc.vector.tensor_copy(key_ring[:, h, :], k.key_col[:, cols])
                            done(one_hots((h + 1) % 2, b * BODY + (h + 1) * GT))
                            dve.sem_inc(s_hot, 1)
                            dve.wait_ge(s_row[h], b * 16 + 16)
                            for j in range(GT):
                                last = nc.vector.scalar_tensor_tensor(
                                    out=junk[:, j, :], in0=key_row[:, h, j * P:(j + 1) * P], scalar=key_ring[:, h, j:j + 1],
                                    in1=k.tri[:, :], op0=ALU.is_equal, op1=ALU.mult, accum_out=part[:, h, j:j + 1])
                            last.then_inc(s_free, 1)
                            dve.wait_ge(s_snap, b * 2 + (h + 1))
                            done(nc.vector.tensor_tensor(base[:, :], base[:, :], snap[:, h, GT - 1, :], ALU.add))
                            split_base(done, (h + 1) % 2)
                            dve.wait_ge(s_pick, b * 2 + (h + 1))
                            for j in range(GT):
                                last = nc.vector.scalar_tensor_tensor(
                                    out=junk[:, GT + j, :], in0=picked[h][:, j, :], scalar=1.0, in1=hot_lo[:, h, j, :],
                                    op0=ALU.mult, op1=ALU.mult, accum_out=part[:, h, GT + j:GT + j + 1])
                            done(last)
                            wait(dve, s_scat[h], b * (16 * GT))
                            nc.vector.tensor_copy(rec_ring[:, h, :, :], k.rec[:, cols, :])
                            done(nc.vector.tensor_tensor(index[:, h, :], part[:, h, 0:GT], part[:, h, GT:2 * GT], ALU.add))
                            dve.sem_inc(s_index, 1)
                        assert done.n == PER
                    repeat(dve, NB, body)

            @block.scalar
            def _(act):
                with act.If_ne(key_falls(nc, k, act, "Activation"), 0):
                    def body(b):
                        for h in range(HALVES):
                            act.wait_ge(s_turn, b * 2 + (h + 1))
                            nc.scalar.copy(hot_hi_t[:, h, :, :], turned[h][:, 0:GT, :]).then_inc(s_turned, 1)
                            act.wait_ge(s_table, b * 2 + (h + 1))
                            nc.scalar.copy(snap[:, h, :, :], table[:, 0:GT, :]).then_inc(s_snap, 1)
                    repeat(act, NB, body)

            @block.tensor
            def _(pe):
                with pe.If_ne(key_falls(nc, k, pe, "PE"), 0):
                    def body(b):
                        for h in range(HALVES):
                            pe.wait_ge(s_hot, b * 2 + (h + 1))
                            for j in range(GT):
                                last = nc.tensor.transpose(turned[h][:, j, :], hot_hi[:, h, j, :], k.ident_bf[:, :])
                            last.then_inc(s_turn, 1)
                            hold(pe, s_taken, s_snap, b * 2 + h)
                            for lo, hi in ((0, 4), (4, GT)):
                                for j in range(hi):
                                    lo_j = max(lo, j)
                                    last = nc.tensor.matmul(table[:, lo_j:hi, :], hot_hi[:, h, j, :], mid(hot_lo[:, h, j, :], hi - lo_j),
                                                            start=(j == 0), stop=True, skip_group_check=(j > 0))
                            last.then_inc(s_table, 1)
                            hold(pe, s_taken, s_turned, b * 2 + (h + 1))
                            hold(pe, s_taken, s_snap, b * 2 + (h + 1))
                            hold(pe, s_taken, s_base, b * 2 + (h + 1))
                            hold(pe, s_taken, s_index, b * 2 + (h - 1))
                            for j in range(GT):
                                terms = [parts[:, h, 0, :], parts[:, h, 1, :]] + ([snap[:, h, j - 1, :]] if j else [])
                                for n, term in enumerate(terms):
                                    last = nc.tensor.matmul(picked[h][:, j, :], hot_hi_t[:, h, j, :], term, start=(n == 0), stop=(n == len(terms) - 1))
                            last.then_inc(s_pick, 1)
                    repeat(pe, NB, body)

            @block.gpsimd
            def _(pool):
                with pool.If_ne(key_falls(nc, k, pool, "Pool"), 0):
                    limit = pool.snap(pool.to_reg(EP - 1))
                    def body(b):
                        for h in range(HALVES):
                            pool.wait_ge(s_index, b * 2 + (h + 1))
                            pool.sem_inc(s_seen, 1)
                            for j in range(GT):
                                pool.indirect_dma_start(k.rec_sorted, bass.IndirectOffsetOnAxis(ap=index[:, h, j:j + 1], axis=0),
                                                        rec_ring[:, h, j, :], None, bounds_check=limit, oob_is_err=False).then_inc(s_scat[h], 16)
                    repeat(pool, NB, body)
                    for h in range(HALVES):
                        pool.wait_ge(s_scat[h], 16 * GT * NB)


def edge_meta(nc, k):
    with ExitStack() as st:
        a = Names(nc, st)
        rows = a.sb(k.tag + "em_rows", [ROWS, CH, P, 4])
        start = a.sb(k.tag + "em_start", [ROWS, CH, P])
        pos = a.sb(k.tag + "em_pos", [ROWS, CH, P])
        slot = a.sb(k.tag + "em_slot", [ROWS, CH, P])
        last = a.sb(k.tag + "em_last", [ROWS, CH, P])
        reset = a.sb(k.tag + "em_reset", [ROWS, 2, CH, P])
        rel = a.sb(k.tag + "em_rel", [ROWS, CH, P])
        ends = a.sb(k.tag + "em_ends", [ROWS, CH, 2])
        zero = a.sb(k.tag + "em_zero", [ROWS, P])
        key = a.sb(k.tag + "em_key", [P, NBR])
        local = a.sb(k.tag + "em_local", [ROWS, CH, P], BF16)
        count = a.sb(k.tag + "em_count", [ROWS, CH, P])
        first = a.sb(k.tag + "em_first", [ROWS, CH])
        ints = a.sb(k.tag + "em_ints", [ROWS, 2, CH], I32)
        ids = a.sb(k.tag + "em_ids", [P, NT], I32)
        none = a.sb(k.tag + "em_none", [PAIR_BLOCKS, P], I32)
        turned = [a.ps(k.tag + f"em_turned{n}", [P, CH, P]) for n in range(5)]
        sums = a.ps(k.tag + "em_sums", [P, 2, CH])
        s_count, s_sums, s_first, s_ids, s_none, s_pair = (a.sem(k.tag + "em_" + n) for n in ("scount", "ssums", "sfirst", "ids", "none", "pair"))
        s_node, s_tile = (a.dma_sem(k.tag + "em_" + n) for n in ("node", "tile"))
        s_load, s_v, s_rows, s_turn, s_store, s_key = (a.sem(k.tag + "em_" + n) for n in ("load", "v", "rows", "turn", "store", "key"))
        src, dst, typ, wgt = (rows[:, :, :, n] for n in range(4))
        with nc.Block() as block:
            @block.sync
            def _(sp):
                sp.dma_start(rows[:, :, :, :].rearrange("t c e q -> t c (e q)"),
                             k.rec_sorted.rearrange("(c t e) q -> t c (e q)", t=ROWS, e=P)).then_inc(s_load, 16)
                if k.attention:
                    sp.wait_ge(s_ids, 2)
                    sp.dma_start(k.pair_table[0:PAIRS, :].rearrange("(b p) o -> b (p o)", p=P), none[:, :]).then_inc(s_none, 16)
                    sp.wait_ge(s_first, 1)
                    with nc.allow_non_contiguous_dma("a value of each tile"):
                        sp.dma_start(k.tile_pairs.rearrange("(c t) -> t c", t=ROWS), ints[:, 0, :]).then_inc(s_pair, 16)
                    sp.dma_start(k.local.rearrange("(c t e) -> t c e", t=ROWS, e=P), local[:, :, :]).then_inc(s_pair, 16)
                    sp.wait_ge(s_pair, 32)
                    sp.dma_start(k.tile_pair[:, :], k.tile_pairs.rearrange("(o t) -> o t", o=1)).then_inc(s_pair, 16)
                    sp.wait_ge(s_tile, 16 * CH)
                    with nc.allow_non_contiguous_dma("a value of each pair"):
                        sp.dma_start(k.pair_node[:, :], k.pair_table[0:PAIRS, :].rearrange("(b p) o -> p (b o)", p=P)).then_inc(s_pair, 16)
                    sp.wait_ge(s_pair, 64)
                sp.wait_ge(s_rows, 1)
                for n in range(2 if k.attention else 0):
                    for heads in (8, 4):
                        for c in range(CH):
                            sp.dma_start(k.resets[n][heads][c * ROWS:(c + 1) * ROWS, :, :], mid(reset[:, n, c, :], heads)).then_inc(s_store, 16)
                sp.dma_start(k.ends.rearrange("(c t w) -> t c w", t=ROWS, w=2), ends[:, :, :]).then_inc(s_store, 16)
                sp.wait_ge(s_store, 16 * ((4 * CH if k.attention else 0) + 1))
                sp.dma_start(key[:, :], k.ends.partition_broadcast(P)).then_inc(s_key, 16)

            @block.vector
            def _(dve):
                done = Chain(dve, s_v)
                dve.wait_ge(s_load, 16)
                nc.vector.memset(zero[:, :], 0.0)
                nc.vector.memset(start[:, :, 0:1], 1.0)
                done(nc.vector.tensor_tensor(start[:, :, 1:P], dst[:, :, 1:P], dst[:, :, 0:P - 1], ALU.not_equal))
                if k.attention:
                    for c in range(CH):
                        nc.vector.tensor_tensor_scan(count[:, c, :], zero[:, :], start[:, c, :], 0.0, ALU.add, ALU.add).then_inc(s_count, 1)
                    dve.wait_ge(s_count, CH)
                    done(nc.vector.tensor_scalar(local[:, :, :], count[:, :, :], 1.0, None, ALU.subtract))
                    done(nc.vector.tensor_copy(ints[:, 1, :], dst[:, :, 0]))
                    dve.wait_ge(s_sums, 1)
                    done(nc.vector.tensor_copy(first[:, :], sums[0:ROWS, 0, :]))
                    for c in range(1, CH):
                        for before in range(c):
                            done(nc.vector.tensor_tensor(first[:, c:c + 1], first[:, c:c + 1], sums[0:ROWS, 1, before:before + 1], ALU.add))
                    done(nc.vector.tensor_copy(ints[:, 0, :], first[:, :]))
                    dve.sem_inc(s_first, 1)
                done(nc.vector.tensor_tensor(last[:, :, :], start[:, :, :], mid(k.iota[0:ROWS, :], CH), ALU.mult))
                for c in range(CH):
                    done(nc.vector.tensor_tensor_scan(pos[:, c, :], zero[:, :], last[:, c, :], 0.0, ALU.add, ALU.max))
                done(nc.vector.tensor_tensor(last[:, :, :], dst, dst[:, :, P - 1:P].to_broadcast([ROWS, CH, P]), ALU.is_equal))
                done(nc.vector.tensor_scalar(slot[:, :, :], pos[:, :, :], -1.0, float(P - 1), ALU.mult, ALU.add))
                done(nc.vector.tensor_tensor(slot[:, :, :], slot[:, :, :], last[:, :, :], ALU.mult))
                done(nc.vector.tensor_tensor(slot[:, :, :], slot[:, :, :], pos[:, :, :], ALU.add))
                nc.vector.tensor_scalar(reset[:, 0, :, :], start[:, :, :], -BIG, None, ALU.mult)
                nc.vector.tensor_scalar(reset[:, 1, :, 0:P - 1], start[:, :, 1:P], -BIG, None, ALU.mult)
                nc.vector.memset(reset[:, 1, :, P - 1:P], -BIG)
                nc.vector.tensor_copy(ends[:, :, 0:1], dst[:, :, 0:1])
                nc.vector.tensor_copy(ends[:, :, 1:2], dst[:, :, P - 1:P])
                done(nc.vector.tensor_scalar(rel[:, :, :], typ, float(NP), None, ALU.mult))
                done(nc.vector.tensor_tensor(rel[:, :, :], rel[:, :, :], src, ALU.add))
                dve.sem_inc(s_rows, 1)
                dve.wait_ge(s_turn, 1)
                for out, n in ((k.slot, 0), (k.weight, 1), (k.other_idx, 2)) + (((k.start, 3), (k.rel_idx, 4)) if k.attention else ()):
                    done(nc.vector.tensor_copy(out[:, :].rearrange("p (c t) -> p c t", c=CH), turned[n][:, :, 0:ROWS]))
                dve.wait_ge(s_key, 16)
                nc.vector.memset(k.keep[:, 0:1], 0.0)
                done(nc.vector.tensor_tensor(k.keep[:, 1:NBR], key[:, 1:NBR], key[:, 0:NBR - 1], ALU.is_equal))
                if k.attention:
                    nc.vector.tensor_scalar(k.cut[:, 0, :], k.keep[0:8, :], 1.0, BIG, ALU.subtract, ALU.mult)
                    nc.vector.memset(k.cut[:, 1, NBR - 1:NBR], -BIG)
                    done(nc.vector.tensor_scalar(k.cut[:, 1, 0:NBR - 1], k.keep[0:8, 1:NBR], 1.0, BIG, ALU.subtract, ALU.mult))

            @block.gpsimd
            def _(pool):
                if k.attention:
                    nc.gpsimd.iota(ids[:, :], [[P, NT]], base=0, channel_multiplier=1).then_inc(s_ids, 1)
                    pool.memset(none[:, :], 0).then_inc(s_ids, 1)
                    pool.wait_ge(s_ids, 2)
                    limit = pool.snap(pool.to_reg(PAIRS + NP - 1))
                    pool.wait_ge(s_none, 16)
                    for c in range(NT):
                        pool.indirect_dma_start(k.pair_table, bass.IndirectOffsetOnAxis(ap=k.pair_row[:, c:c + 1], axis=0),
                                                ids[:, c:c + 1], None, bounds_check=limit, oob_is_err=False).then_inc(s_node, 16)
                    pool.wait_ge(s_node, 16 * NT)
                    pool.wait_ge(s_first, 1)
                    for c in range(CH):
                        pool.indirect_dma_start(k.pair_table, bass.IndirectOffsetOnAxis(ap=ints[:, 0, c:c + 1], axis=0),
                                                ints[:, 1, c:c + 1], None, bounds_check=limit, oob_is_err=False).then_inc(s_tile, 16)
                    pool.wait_ge(s_tile, 16 * CH)

            @block.tensor
            def _(pe):
                if k.attention:
                    pe.wait_ge(s_count, CH)
                    nc.tensor.matmul(sums[0:ROWS, 0, :], k.tri_hi[0:ROWS, 0:ROWS], count[:, :, P - 1], start=True, stop=True)
                    nc.tensor.matmul(sums[:, 1, :], k.ones[0:ROWS, :], count[:, :, P - 1], start=True, stop=True).then_inc(s_sums, 1)
                pe.wait_ge(s_rows, 1)
                for n, q in enumerate((slot[:, :, :], wgt, src, start[:, :, :], rel[:, :, :])):
                    for c in range(CH):
                        ins = nc.tensor.transpose(turned[n][:, c, 0:ROWS], q[:, c, :], k.ident[0:ROWS, 0:ROWS])
                ins.then_inc(s_turn, 1)


class Shared:

    def __init__(self, a):
        self.iota, self.ident, self.tri, self.tri_hi = (
            a.sb(n, [P, w]) for n, w in (("iota", P), ("ident", P), ("tri", P), ("tri_hi", P)))
        self.ident_bf, self.zeros_bf = a.sb("ident_bf", [P, P], BF16), a.sb("zeros_bf", [P, P], BF16)
        self.ones, self.minus_p = a.sb("ones", [P, P]), a.sb("minus_p", [P, 1])
        self.type_row, self.tile_chunk = a.sb("type_row", [P, NT], I32), a.sb("tile_chunk", [P, KT], I32)
        self.pair_type_row = a.sb("pair_type_row", [P, PAIR_BLOCKS], I32)
        self.mask, self.gate, self.inv_root = a.sb("mask", [P, NT * TYPES]), a.sb("gate", [P, NT]), a.sb("inv_root", [P, NT])


class Order:

    def __init__(self, k):
        self.iota, self.ident, self.tri, self.tri_hi = k.iota, k.ident, k.tri, k.tri_hi
        self.ident_bf, self.zeros_bf, self.ones = k.ident_bf, k.zeros_bf, k.ones
        self.mask, self.gate, self.inv_root, self.minus_p = k.mask, k.gate, k.inv_root, k.minus_p
        self.type_row, self.tile_chunk, self.pair_type_row = k.type_row, k.tile_chunk, k.pair_type_row


def edge_order(nc, k, a, ins, tag, key, other, attention):
    o = Order(k)
    o.tag, o.attention = tag, attention
    o.slot, o.weight, o.other_idx = a.sb(tag + "slot", [P, TILES]), a.sb(tag + "weight", [P, TILES]), a.sb(tag + "other_idx", [P, TILES], I32)
    o.deg, o.sum_row = a.sb(tag + "deg", [P, NT]), a.sb(tag + "sum_row", [P, NT], I32)
    o.keep = a.sb(tag + "keep", [P, NBR])
    if attention:
        o.start = a.sb(tag + "start", [P, TILES])
        o.rel_idx = a.sb(tag + "rel_idx", [P, TILES], I32)
        o.pair_row, o.pair_node = a.sb(tag + "pair_row", [P, NT], I32), a.sb(tag + "pair_node", [P, PAIR_BLOCKS], I32)
        o.tile_pair = a.sb(tag + "tile_pair", [1, TILES], I32)
        o.pair_table = nc.dram_tensor(tag + "pair_table", (PAIRS + NP, 1), I32, kind="Internal").ap()
        o.local = nc.dram_tensor(tag + "local", (EP,), BF16, kind="Internal").ap()
        o.tile_pairs = nc.dram_tensor(tag + "tile_pairs", (TILES,), I32, kind="Internal").ap()
        o.cut = a.sb(tag + "cut", [8, 2, NBR])
        o.resets = [{heads: nc.dram_tensor(f"{tag}resets{n}_{heads}", (TILES, heads, P), F32, kind="Internal").ap()
                     for heads in (8, 4)} for n in range(2)]
    o.key_pad = nc.dram_tensor(tag + "key_pad", (EP,), F32, kind="Internal").ap()
    o.rec_sorted = nc.dram_tensor(tag + "rec_sorted", (EP, 4), F32, kind="Internal").ap()
    o.ends = nc.dram_tensor(tag + "ends", (NBR,), F32, kind="Internal").ap()
    with ExitStack() as st:
        t = Names(nc, st)
        o.rec = t.sb(tag + "rec", [P, TILES, 4])
        o.key_col, o.hi_col, o.lo_col = (t.sb(tag + n, [P, TILES + GT]) for n in ("key_col", "hi_col", "lo_col"))
        o.first_pos = t.sb(tag + "first_pos", [NT, P])
        o.unsorted = t.sb(tag + "unsorted", [P, 1], I32)
        edge_columns(nc, o, other, key, ins["etype"], ins["weight"])
        degrees(nc, o)
        ranks(nc, o)
    edge_meta(nc, o)
    return o


def sum_edges(nc, k, tag, table, partial, weighted):
    with ExitStack() as st:
        a = Names(nc, st)
        got = a.sb(tag + "got", [P, 2, GT, D])
        hot = a.sb(tag + "hot", [P, 2, GT, P])
        sums = a.sb(tag + "sums", [P, 2, GT, D])
        idx = a.sb(tag + "idx", [P, 2, GT], I32)
        acc = [a.ps(f"{tag}acc{j}", [P, 512]) for j in range(GT)]
        s_got = [a.dma_sem(f"{tag}s_got{h}") for h in range(2)]
        s_out = [a.sem(f"{tag}s_out{h}") for h in range(2)]
        s_idx, s_seen, s_hot, s_v, s_acc, s_sums = (a.sem(tag + n) for n in ("s_idx", "s_seen", "s_hot", "s_v", "s_acc", "s_sums"))
        with nc.Block() as block:
            @block.gpsimd
            def _(pool):
                limit = pool.snap(pool.to_reg(NP - 1))

                def body(b):
                    for h in range(HALVES):
                        hold(pool, s_seen, s_acc, b * BODY + (h - 1) * GT)
                        nc.gpsimd.tensor_copy(idx[:, h, :], k.other_idx[:, bass.ds(b * BODY + h * GT, GT)]).then_inc(s_idx, 1)
                        hold(pool, s_seen, s_idx, b * 2 + (h + 1))
                        for j in range(GT):
                            pool.indirect_dma_start(got[:, h, j, :], None, table, bass.IndirectOffsetOnAxis(ap=idx[:, h, j:j + 1], axis=0),
                                                    bounds_check=limit, oob_is_err=False).then_inc(s_got[h], 16)
                repeat(pool, NB, body)

            @block.vector
            def _(dve):
                def body(b):
                    for h in range(HALVES):
                        cols = bass.ds(b * BODY + h * GT, GT)
                        wait(dve, s_acc, b * BODY + (h - 1) * GT)
                        ins = nc.vector.tensor_tensor(hot[:, h, :, :], mid(k.iota[:, :], GT), bcast(k.slot[:, cols], P), ALU.is_equal)
                        if weighted:
                            ins.then_inc(s_v, 1)
                            dve.wait_ge(s_v, b * 2 + (h + 1))
                            ins = nc.vector.tensor_tensor(hot[:, h, :, :], hot[:, h, :, :], bcast(k.weight[:, cols], P), ALU.mult)
                        ins.then_inc(s_hot, 1)
                repeat(dve, NB, body)

            @block.tensor
            def _(pe):
                def body(b):
                    for h in range(HALVES):
                        pe.wait_ge(s_hot, b * 2 + (h + 1))
                        pe.wait_ge(s_got[h], b * (16 * GT) + 16 * GT)
                        for j in range(GT):
                            wait(pe, s_sums, b * BODY + ((h - 1) * GT + j + 1))
                            nc.tensor.matmul(acc[j][:, 0:D], hot[:, h, j, :], got[:, h, j, :], start=True, stop=True).then_inc(s_acc, 1)
                repeat(pe, NB, body)

            @block.scalar
            def _(act):
                def body(b):
                    for h in range(HALVES):
                        wait(act, s_out[h], b * 16)
                        for j in range(GT):
                            act.wait_ge(s_acc, b * BODY + (h * GT + j + 1))
                            nc.scalar.copy(sums[:, h, j, :], acc[j][:, 0:D]).then_inc(s_sums, 1)
                repeat(act, NB, body)

            @block.sync
            def _(sp):
                def body(b):
                    for h in range(HALVES):
                        sp.wait_ge(s_sums, b * BODY + (h + 1) * GT)
                        sp.dma_start(partial[bass.ds(b * (BODY * P) + h * GT * P, GT * P), :].rearrange("(t s) w -> s t w", s=P),
                                     sums[:, h, :, :]).then_inc(s_out[h], 16)
                repeat(sp, NB, body)
                for h in range(HALVES):
                    sp.wait_ge(s_out[h], 16 * NB)


def spread_rows(nc, k, tag, own, pair_rows):
    with ExitStack() as st:
        a = Names(nc, st)
        rows = a.sb(tag + "rows", [P, PAIR_BLOCKS, D])
        parts = [(lo, min(lo + GT, PAIR_BLOCKS)) for lo in range(0, PAIR_BLOCKS, GT)]
        s_in = [a.dma_sem(f"{tag}in{n}") for n in range(len(parts))]
        s_out = a.sem(tag + "out")
        with nc.Block() as block:
            @block.gpsimd
            def _(pool):
                limit = pool.snap(pool.to_reg(NP - 1))
                for n, (lo, hi) in enumerate(parts):
                    for c in range(lo, hi):
                        pool.indirect_dma_start(rows[:, c, :], None, own, bass.IndirectOffsetOnAxis(ap=k.pair_node[:, c:c + 1], axis=0),
                                                bounds_check=limit, oob_is_err=False).then_inc(s_in[n], 16)

            @block.sync
            def _(sp):
                for n, (lo, hi) in enumerate(parts):
                    sp.wait_ge(s_in[n], 16 * (hi - lo))
                    sp.dma_start(pair_rows[lo * P:hi * P, :].rearrange("(c p) w -> p c w", p=P), rows[:, lo:hi, :]).then_inc(s_out, 16)
                sp.wait_ge(s_out, 16 * len(parts))


def attend_edges(nc, k, tag, table, main_idx, limit_rows, pair_rows, heads, scale, partial, free):
    W = D + 2 * heads
    dk = D // heads
    HT = GT * heads
    with ExitStack() as st:
        a = Names(nc, st)
        got = a.sb(tag + "got", [P, 2, GT, 2 * D])
        window = a.sb(tag + "window", [P, 2, GT, D])
        local = a.sb(tag + "local", [P, 2, GT * P], BF16)
        apart = a.sb(tag + "apart", [P, GT * P])
        spread = a.sb(tag + "spread", [P, 2, GT * P])
        prod = a.sb(tag + "prod", [P, GT, D])
        hot = a.sb(tag + "hot", [P, 2, GT, P])
        val, sums = (t[:, 0:2 * GT, 0:W].rearrange("p (h t) w -> p h t w", h=2) for t in free)
        idx = a.sb(tag + "idx", [P, 2, GT], I32)
        cuts = a.sb(tag + "cuts", [HT, 2, 2, P])
        score = a.sb(tag + "score", [P, 2, HT])
        diff = a.sb(tag + "diff", [P, 2, HT])
        run = a.sb(tag + "run", [HT, 2, P])
        segmax = a.sb(tag + "segmax", [HT, 2, P])
        own = a.ps(tag + "own", [P, 8, D])
        BANKS = 3
        acc = [a.ps(f"{tag}acc{j}", [P, 512]) for j in range(BANKS)]
        flip = a.ps(tag + "flip", [P, 4, P])
        s_got = [a.dma_sem(f"{tag}s_got{h}") for h in range(2)]
        s_out = [a.sem(f"{tag}s_out{h}") for h in range(2)]
        s_cut = [a.sem(f"{tag}s_cut{h}") for h in range(2)]
        s_window = [a.sem(f"{tag}s_window{h}") for h in range(2)]
        s_local = [a.sem(f"{tag}s_local{h}") for h in range(2)]
        s_idx, s_seen, s_v, s_read, s_score, s_flip, s_segmax, s_back, s_diff, s_exp, s_val, s_acc, s_sums, s_apart, s_spread, s_own, s_mult = (
            a.sem(tag + "s_" + n) for n in ("idx", "seen", "v", "read", "score", "flip", "segmax", "back", "diff", "exp",
                                            "val", "acc", "sums", "apart", "spread", "own", "mult"))

        def bank(h, j):
            return (h * GT + j) % BANKS

        def bank_user(h, j):
            if h * GT + j >= BANKS:
                return BANKS
            return next(d for d in range(1, BODY) if (BODY + j - d) % BANKS == bank(0, j) and d > j)

        def group(b, h, ahead):
            body, half = b + (h + ahead) // HALVES, (h + ahead) % HALVES
            if isinstance(b, int) and not 0 <= body < NB:
                return None
            return body, half

        with nc.Block() as block:
            @block.gpsimd
            def _(pool):
                limit = pool.snap(pool.to_reg(limit_rows - 1))

                def body(b):
                    for h in range(HALVES):
                        cols = bass.ds(b * BODY + h * GT, GT)
                        hold(pool, s_seen, s_val, b * 2 + (h - 1))
                        nc.gpsimd.tensor_copy(idx[:, h, :], main_idx[:, cols]).then_inc(s_idx, 1)
                        hold(pool, s_seen, s_idx, b * 2 + (h + 1))
                        for j in range(GT):
                            pool.indirect_dma_start(got[:, h, j, :], None, table, bass.IndirectOffsetOnAxis(ap=idx[:, h, j:j + 1], axis=0),
                                                    bounds_check=limit, oob_is_err=False).then_inc(s_got[h], 16)
                repeat(pool, NB, body)

            @block.sync
            def _(sp):
                def body(b):
                    for h in range(HALVES):
                        wait(sp, s_spread, b * 2 + (h - 1))
                        sp.dma_start(local[:, h, :], k.local[bass.ds(b * (BODY * P) + h * GT * P, GT * P)].partition_broadcast(P)).then_inc(s_local[h], 16)
                        wait(sp, s_own, b * 2 + (h - 1))
                        for j in range(GT):
                            row = nc.values_load(k.tile_pair[0:1, bass.ds(b * BODY + h * GT + j, 1)], engines=(mybir.EngineType.SP,),
                                                 min_val=0, max_val=PAIRS - P)
                            sp.dma_start(window[:, h, j, :], pair_rows[bass.ds(row, P), :]).then_inc(s_window[h], 16)
                        wait(sp, s_segmax, b * 2 + (h - 1))
                        for n in range(2):
                            sp.dma_start(cuts[:, h, n, :], k.resets[n][heads].rearrange("t h e -> (t h) e")[bass.ds(b * (BODY * heads) + h * GT * heads, HT), :]).then_inc(s_cut[h], 16)
                repeat(sp, NB, body)

            @block.vector
            def _(dve):
                PER = 2 * 8

                def body(b):
                    done = Chain(dve, s_v, b * PER)
                    for h in range(HALVES):
                        cols = bass.ds(b * BODY + h * GT, GT)
                        dve.wait_ge(s_got[h], b * (16 * GT) + 16 * GT)
                        dve.wait_ge(s_own, b * 2 + (h + 1))
                        done(nc.vector.tensor_tensor(prod[:, :, :], got[:, h, :, 0:D], own[:, 0:GT, :], ALU.mult))
                        dve.sem_inc(s_mult, 1)
                        done(nc.vector.tensor_reduce(score[:, h, :], prod[:, :, :].rearrange("p t (h d) -> p (t h) d", d=dk), AX.X, ALU.add))
                        dve.sem_inc(s_score, 1)
                        wait(dve, s_acc, b * BODY + (h - 1) * GT)
                        done(nc.vector.tensor_tensor(hot[:, h, :, :], mid(k.iota[:, :], GT), bcast(k.slot[:, cols], P), ALU.is_equal))
                        dve.wait_ge(s_cut[h], b * 32 + 32)
                        dve.wait_ge(s_flip, b * 2 + (h + 1))
                        done(nc.vector.tensor_tensor_scan(run[:, h, :], cuts[:, h, 0, :], flip[0:HT, h, :], -BIG, ALU.add, ALU.max))
                        done(nc.vector.tensor_tensor_scan(segmax[:, h, ::-1], cuts[:, h, 1, ::-1], run[:, h, ::-1], -BIG, ALU.add, ALU.max))
                        dve.sem_inc(s_segmax, 1)
                        dve.wait_ge(s_back, b * 2 + (h + 1))
                        done(nc.vector.tensor_tensor(diff[:, h, :], score[:, h, :], flip[:, 2 + h, 0:HT], ALU.subtract))
                        dve.sem_inc(s_diff, 1)
                        done(nc.vector.tensor_tensor(val[:, h, :, D + heads:W], flip[:, 2 + h, 0:HT].rearrange("p (t h) -> p t h", h=heads),
                                                     bcast(k.start[:, cols], heads), ALU.mult))
                        dve.wait_ge(s_exp, b * 2 + (h + 1))
                        done(nc.vector.tensor_tensor(val[:, h, :, 0:D].rearrange("p t (h d) -> p t h d", d=dk),
                                                     got[:, h, :, D:2 * D].rearrange("p t (h d) -> p t h d", d=dk),
                                                     val[:, h, :, D:D + heads].unsqueeze(3).to_broadcast([P, GT, heads, dk]), ALU.mult))
                        dve.sem_inc(s_val, 1)
                    assert done.n == PER
                repeat(dve, NB, body)

            @block.tensor
            def _(pe):
                def spread_group(b, h):
                    pe.wait_ge(s_spread, b * 2 + (h + 1))
                    hold(pe, s_read, s_mult, b * 2 + h)
                    pe.wait_ge(s_window[h], b * (16 * GT) + 16 * GT)
                    for j in range(GT):
                        last = nc.tensor.matmul(own[:, j, :], spread[:, h, j * P:(j + 1) * P], window[:, h, j, :], start=True, stop=True)
                    last.then_inc(s_own, 1)

                def products(b, h):
                    pe.wait_ge(s_val, b * 2 + (h + 1))
                    for j in range(GT):
                        wait(pe, s_sums, b * BODY + (h * GT + j + 1 - bank_user(h, j)))
                        nc.tensor.matmul(acc[bank(h, j)][:, 0:W], hot[:, h, j, :], val[:, h, j, :], start=True, stop=True).then_inc(s_acc, 1)

                def body(b):
                    for h in range(HALVES):
                        following, previous = group(b, h, 1), group(b, h, -1)
                        if following:
                            spread_group(*following)
                        hold(pe, s_read, s_score, b * 2 + (h + 1))
                        nc.tensor.transpose(flip[0:HT, h, :], score[:, h, :], k.ident[:, :]).then_inc(s_flip, 1)
                        hold(pe, s_read, s_segmax, b * 2 + (h + 1))
                        nc.tensor.transpose(flip[:, 2 + h, 0:HT], segmax[:, h, :], k.ident[0:HT, 0:HT]).then_inc(s_back, 1)
                        if previous:
                            products(*previous)
                spread_group(0, 0)
                repeat_between(pe, NB, body)
                products(NB - 1, HALVES - 1)

            @block.scalar
            def _(act):
                def spread_one_hots(b, h):
                    act.wait_ge(s_local[h], b * 16 + 16)
                    wait(act, s_own, b * 2 + (h - 1))
                    wait(act, s_spread, b * 2 + h)
                    nc.scalar.activation(apart[:, :], local[:, h, :], ACT.Abs, bias=k.minus_p[:, 0:1]).then_inc(s_apart, 1)
                    act.wait_ge(s_apart, b * 2 + (h + 1))
                    nc.scalar.activation(spread[:, h, :], apart[:, :], ACT.Relu, bias=k.ones[:, 0:1], scale=-1.0).then_inc(s_spread, 1)

                def copy_sums(b, h):
                    wait(act, s_out[h], b * 16)
                    for j in range(GT):
                        act.wait_ge(s_acc, b * BODY + (h * GT + j + 1))
                        nc.scalar.copy(sums[:, h, j, :], acc[bank(h, j)][:, 0:W]).then_inc(s_sums, 1)
                    act.wait_ge(s_sums, b * BODY + (h + 1) * GT)
                    act.dma_start(partial[bass.ds(b * (BODY * P) + h * GT * P, GT * P), :].rearrange("(t s) w -> s t w", s=P),
                                  sums[:, h, :, :]).then_inc(s_out[h], 16)

                def body(b):
                    for h in range(HALVES):
                        following, previous = group(b, h, 2), group(b, h, -1)
                        if following:
                            spread_one_hots(*following)
                        act.wait_ge(s_diff, b * 2 + (h + 1))
                        nc.scalar.activation(val[:, h, :, D:D + heads], diff[:, h, :].rearrange("p (t h) -> p t h", h=heads),
                                             ACT.Exp, scale=scale).then_inc(s_exp, 1)
                        if previous:
                            copy_sums(*previous)
                spread_one_hots(0, 0)
                spread_one_hots(0, 1)
                repeat_between(act, NB, body)
                copy_sums(NB - 1, HALVES - 1)
                for h in range(HALVES):
                    act.wait_ge(s_out[h], 16 * NB)


def merge(nc, k, tag, partial, heads, scale):
    W = D + 2 * heads
    with ExitStack() as st:
        a = Names(nc, st)
        rows = a.sb(tag + "rows", [BR, BC, W])
        cols = a.sb(tag + "cols", [P, 2, NBR])
        total = a.sb(tag + "total", [P, 2, NBR])
        small = a.sb(tag + "small", [8, 6, NBR]) if heads else None
        pick = a.sb(tag + "pick", [8, 2, P]) if heads else None
        back = a.sb(tag + "back", [BR, BC, W])
        zero = a.sb(tag + "zero", [1, W])
        SPLIT = (4, BC - 4)
        turn = [a.ps(f"{tag}turn{n}", [P, 2, 512]) for n in range(4 if heads else 2)]
        s_load, s_zero, s_turn, s_cols, s_v, s_f, s_scaled, s_total, s_back, s_rows, s_store, s_pick, s_exp, s_fac = (
            a.sem(tag + n) for n in ("load", "zero", "turn", "cols", "v", "f", "scaled", "total", "back", "rows", "store", "pick", "exp", "fac"))

        def parts(n):
            return ((0, 0, SPLIT[0] * BR), (1, SPLIT[0] * BR, NBR))

        with nc.Block() as block:
            @block.gpsimd
            def _(pool):
                pool.memset(zero[:, :], 0.0).then_inc(s_zero, 1)
                if heads:
                    dk = D // heads
                    done = Chain(pool, s_pick)
                    done(pool.memset(pick[:, :, :], 1.0))
                    flat = pick[0:heads, :, :].rearrange("h f p -> h (f p)")
                    done(pool.affine_select(out=flat, in_=flat, compare_op=ALU.is_ge, fill=0.0, base=0,
                                            pattern=[[1, D]], channel_multiplier=-dk))
                    done(pool.affine_select(out=flat, in_=flat, compare_op=ALU.is_ge, fill=0.0, base=dk - 1,
                                            pattern=[[-1, D]], channel_multiplier=dk))

            @block.sync
            def _(sp):
                view = partial[0:EP, :].rearrange("(c t s) w -> t c s w", t=BR // 2, s=P)
                for n in range(2):
                    sp.dma_start(rows[n:BR:2, :, :], view[:, :, n * (P - 1), :]).then_inc(s_load, 16)
                sp.wait_ge(s_zero, 1)
                sp.dma_start(partial[ZERO_ROW:ZERO_ROW + 1, :], zero[:, :]).then_inc(s_store, 16)
                sp.wait_ge(s_rows, 1)
                sp.dma_start(partial[MERGED:MERGED + NBR, :].rearrange("(c p) w -> p c w", p=BR), back[:, :, :]).then_inc(s_store, 16)
                sp.wait_ge(s_store, 32)

            @block.tensor
            def _(pe):
                pe.wait_ge(s_load, 32)
                for n, (lo, hi) in enumerate(((0, P), (P, D)) + (((D, D + heads), (D + heads, W)) if heads else ())):
                    for c in range(BC):
                        col = (c % 4) * BR
                        ins = nc.tensor.transpose(turn[n][0:hi - lo, c // 4, col:col + BR], rows[:, c, lo:hi], k.ident[0:BR, 0:BR])
                ins.then_inc(s_turn, 1)
                if heads:
                    pe.wait_ge(s_pick, 3)
                    pe.wait_ge(s_exp, 1)
                    pe.wait_ge(s_cols, 1)
                    for f in range(2):
                        for bank, lo, hi in parts(f):
                            ins = nc.tensor.matmul(turn[f][:, bank, 0:hi - lo], pick[0:heads, f, :], small[0:heads, 5, lo:hi], start=True, stop=True)
                    ins.then_inc(s_fac, 1)
                pe.wait_ge(s_total, 1)
                for c in range(BC):
                    for f in range(2):
                        ins = nc.tensor.transpose(turn[f][0:BR, c // 4, (c % 4) * P:(c % 4 + 1) * P], total[:, f, c * BR:(c + 1) * BR], k.ident[:, :])
                    if heads:
                        ins = nc.tensor.transpose(turn[2][0:BR, c // 4, (c % 4) * P:(c % 4) * P + heads],
                                                  small[0:heads, 4, c * BR:(c + 1) * BR], k.ident[0:heads, 0:heads])
                ins.then_inc(s_back, 1)

            @block.scalar
            def _(act):
                if heads:
                    act.wait_ge(s_f, 1)
                    nc.scalar.activation(small[0:heads, 5, :], small[0:heads, 3, :], ACT.Exp, scale=scale).then_inc(s_exp, 1)

            @block.vector
            def _(dve):
                done = Chain(dve, s_v)
                dve.wait_ge(s_turn, 1)
                for f in range(2):
                    for bank, lo, hi in parts(f):
                        done(nc.vector.tensor_copy(cols[:, f, lo:hi], turn[f][:, bank, 0:hi - lo]))
                if heads:
                    z, m, run, top, zsum = (small[0:heads, n, :] for n in range(5))
                    for n, q in ((2, 0), (3, 1)):
                        for bank, lo, hi in parts(n):
                            done(nc.vector.tensor_copy(small[0:heads, q, lo:hi], turn[n][0:heads, bank, 0:hi - lo]))
                    dve.sem_inc(s_cols, 1)
                    done(nc.vector.tensor_scalar(run, z, 0.0, -BIG, ALU.is_equal, ALU.mult))
                    done(nc.vector.tensor_tensor(m, m, run, ALU.add))
                    done(nc.vector.tensor_tensor_scan(run, k.cut[0:heads, 0, :], m, -BIG, ALU.add, ALU.max))
                    done(nc.vector.tensor_tensor_scan(small[0:heads, 3, ::-1], k.cut[0:heads, 1, ::-1], small[0:heads, 2, ::-1], -BIG, ALU.add, ALU.max))
                    done(nc.vector.tensor_tensor(top, m, top, ALU.subtract))
                    dve.sem_inc(s_f, 1)
                    dve.wait_ge(s_exp, 1)
                    done(nc.vector.tensor_tensor(z, z, small[0:heads, 5, :], ALU.mult))
                    done(nc.vector.tensor_tensor_scan(zsum, k.keep[0:heads, :], z, 0.0, ALU.mult, ALU.add))
                    dve.wait_ge(s_fac, 1)
                    for f in range(2):
                        for bank, lo, hi in parts(f):
                            done(nc.vector.tensor_tensor(cols[:, f, lo:hi], cols[:, f, lo:hi], turn[f][:, bank, 0:hi - lo], ALU.mult))
                for f in range(2):
                    done(nc.vector.tensor_tensor_scan(total[:, f, :], k.keep[:, :], cols[:, f, :], 0.0, ALU.mult, ALU.add))
                dve.sem_inc(s_total, 1)
                if heads:
                    done(nc.vector.memset(back[:, :, D:W], 0.0))
                dve.wait_ge(s_back, 1)
                for bank in range(2):
                    c0, c1 = bank * 4, min(bank * 4 + 4, BC)
                    for f in range(2):
                        done(nc.vector.tensor_copy(back[:, c0:c1, f * P:(f + 1) * P],
                                                   turn[f][0:BR, bank, 0:(c1 - c0) * P].rearrange("p (c w) -> p c w", w=P)))
                    if heads:
                        done(nc.vector.tensor_copy(back[:, c0:c1, D:D + heads],
                                                   turn[2][0:BR, bank, 0:(c1 - c0) * P].rearrange("p (c w) -> p c w", w=P)[:, :, 0:heads]))
                dve.sem_inc(s_rows, 1)


def gather_sums(nc, k, tag, partial, W, sums, loads):
    with ExitStack() as st:
        a = Names(nc, st)
        s_in, s_load = a.dma_sem(tag + "in"), a.sem(tag + "load")
        with nc.Block() as block:
            @block.gpsimd
            def _(pool):
                limit = pool.snap(pool.to_reg(PROWS - 1))
                for c in range(NT):
                    pool.indirect_dma_start(sums[:, c, 0:W], None, partial, bass.IndirectOffsetOnAxis(ap=k.sum_row[:, c:c + 1], axis=0),
                                            bounds_check=limit, oob_is_err=False).then_inc(s_in, 16)
                pool.wait_ge(s_in, 16 * NT)

            @block.sync
            def _(sp):
                for out, source in loads:
                    sp.dma_start(out, source).then_inc(s_load, 16)
                sp.wait_ge(s_load, 16 * len(loads))


def linear(nc, k, tag, source, chunks, weights, width, dest=None, relu=False, bias=None, types=1, stores=(), take=None, put=None):
    KC = chunks * types
    banks = -(-width // 512)
    with ExitStack() as st:
        a = Names(nc, st)
        turned = a.sb(tag + "turned", [P, 2, KC, P])
        masked = a.sb(tag + "masked", [P, 2, types, chunks * P])
        ring = a.sb(tag + "ring", [P, 2, width]) if stores else None
        flip = [a.ps(f"{tag}flip{n}", [P, max(KC * P, 512)]) for n in range(2)]
        acc = [a.ps(f"{tag}acc{n}", [P, 512 * banks]) for n in range(2)]
        s_mask, s_flip, s_turned, s_acc, s_out, s_seen = (a.sem(tag + n) for n in ("mask", "flip", "turned", "acc", "out", "seen"))
        s_store = [a.sem(f"{tag}store{n}") for n in range(2)]
        spans = [(lo, min(lo + 512, width)) for lo in range(0, width, 512)]
        with nc.Block() as block:
            @block.tensor
            def _(pe):
                def flips(c, n):
                    pe.wait_ge(s_mask, c + 1)
                    hold(pe, s_seen, s_turned, c - 1)
                    for q in range(KC):
                        last = nc.tensor.transpose(flip[n][:, q * P:(q + 1) * P],
                                                   masked[:, n, q // chunks, (q % chunks) * P:(q % chunks + 1) * P], k.ident[:, :])
                    last.then_inc(s_flip, 1)

                def step(c, n, b):
                    if not (isinstance(c, int) and c == NT - 1):
                        flips(c + 1, 1 - n)
                    pe.wait_ge(s_turned, c + 1)
                    wait(pe, s_out, c - 1)
                    for lo, hi in spans:
                        for q in range(KC):
                            last = nc.tensor.matmul(acc[n][:, lo:hi], turned[:, n, q, :], weights[:, q, lo:hi],
                                                    start=(q == 0), stop=(q == KC - 1 and bias is None))
                        if bias is not None:
                            last = nc.tensor.matmul(acc[n][:, lo:hi], k.ones[:, :], bias[:, lo:hi], start=False, stop=True)
                    last.then_inc(s_acc, 1)
                flips(0, 0)
                node_tiles(pe, step)

            @block.vector
            def _(dve):
                def make_source(c, n):
                    wait(dve, s_flip, c - 1)
                    if types > 1:
                        ins = nc.vector.tensor_tensor(masked[:, n, :, :],
                                                      source[:, bass.ds(c, 1), :].to_broadcast([P, types, chunks * P]),
                                                      bcast(k.mask[:, bass.ds(c * types, types)], chunks * P), ALU.mult)
                    elif take is not None:
                        ins = take(masked[:, n, 0, :], c)
                    else:
                        ins = nc.vector.tensor_copy(masked[:, n, :, :], source[:, bass.ds(c, 1), :])
                    ins.then_inc(s_mask, 1)

                def put_result(c, n):
                    dve.wait_ge(s_acc, c + 1)
                    put(c, acc[n][:, 0:width]).then_inc(s_out, 1)

                def step(c, n, b):
                    if not (isinstance(c, int) and c == NT - 1):
                        make_source(c + 1, 1 - n)
                    if put is not None and not (isinstance(c, int) and c == 0):
                        put_result(c - 1, 1 - n)
                make_source(0, 0)
                node_tiles(dve, step)
                if put is not None:
                    put_result(NT - 1, (NT - 1) % 2)

            @block.scalar
            def _(act):
                def copy_turned(c, n):
                    act.wait_ge(s_flip, c + 1)
                    wait(act, s_acc, c - 1)
                    nc.scalar.copy(turned[:, n, :, :].rearrange("p q w -> p (q w)"), flip[n][:, 0:KC * P]).then_inc(s_turned, 1)

                def step(c, n, b):
                    if not (isinstance(c, int) and c == NT - 1):
                        copy_turned(c + 1, 1 - n)
                    if put is not None:
                        return
                    act.wait_ge(s_acc, c + 1)
                    if dest is None:
                        wait(act, s_store[n], b * (16 * len(stores)))
                        out = ring[:, n, :]
                    else:
                        out = dest[:, bass.ds(c, 1), 0:width].rearrange("p o w -> p (o w)")
                    nc.scalar.activation(out, acc[n][:, 0:width], ACT.Relu if relu else ACT.Copy).then_inc(s_out, 1)
                copy_turned(0, 0)
                node_tiles(act, step)

            @block.sync
            def _(sp):
                def step(c, n, b):
                    sp.wait_ge(s_out, c + 1)
                    for table, col, lo, w in stores:
                        sp.dma_start(table[bass.ds(c * P, P), col:col + w], ring[:, n, lo:lo + w]).then_inc(s_store[n], 16)
                if stores:
                    node_tiles(sp, step)
                    for n in range(2):
                        sp.wait_ge(s_store[n], 16 * len(stores) * ((NT + 1 - n) // 2))


def normalise(nc, k, tag, y, eps, scale=None, add=None, store=None):
    split = NL * 3 if add is None else NT

    def tile(t, c):
        return t[:, bass.ds(c, 1), :].rearrange("p o w -> p (o w)")
    with ExitStack() as st:
        a = Names(nc, st)
        stats, mv = a.sb(tag + "stats", [P, NT, 6]), a.sb(tag + "mv", [P, NT, 2])
        std, inv, shift = a.sb(tag + "std", [P, NT]), a.sb(tag + "inv", [P, NT]), a.sb(tag + "shift", [P, NT])
        s_v, s_std, s_stats, s_apply, s_shift, s_scaled, s_store = (
            a.sem(tag + n) for n in ("v", "sstd", "sstats", "apply", "sshift", "scaled", "store"))
        with nc.Block() as block:
            @block.vector
            def _(dve):
                def measure(b):
                    for j in range(NL):
                        last = nc.vector.bn_stats(tile(stats, b * NL + j), tile(y, b * NL + j))
                    last.then_inc(s_stats, 1)
                repeat(dve, NT // NL, measure)
                dve.wait_ge(s_stats, NT // NL)
                for c in range(NT):
                    last = nc.vector.bn_aggr(mv[:, c, :], stats[:, c, :])
                done = Chain(dve, s_v)
                done(last)
                done(nc.vector.tensor_scalar(shift[:, :], mv[:, :, 1], eps, None, ALU.add))
                dve.wait_ge(s_std, 1)
                done(nc.vector.reciprocal(inv[:, :], std[:, :]))
                if add is None:
                    ins = nc.vector.scalar_tensor_tensor(out=shift[:, :], in0=mv[:, :, 0], scalar=-1.0, in1=inv[:, :],
                                                         op0=ALU.mult, op1=ALU.mult)
                else:
                    ins = nc.vector.tensor_scalar(shift[:, :], mv[:, :, 0], -1.0, None, ALU.mult)
                ins.then_inc(s_shift, 1)
                dve.wait_ge(s_shift, 1)

                def apply(b):
                    for j in range(NL):
                        c = b * NL + j
                        if add is None:
                            nc.vector.tensor_scalar(tile(y, c), tile(y, c), inv[:, bass.ds(c, 1)], shift[:, bass.ds(c, 1)],
                                                    ALU.mult, ALU.add).then_inc(s_apply, 1)
                        else:
                            nc.vector.scalar_tensor_tensor(out=tile(y, c), in0=tile(y, c), scalar=shift[:, bass.ds(c, 1)],
                                                           in1=scale, op0=ALU.add, op1=ALU.mult).then_inc(s_apply, 1)
                repeat(dve, split // NL, apply)
                if add is not None:
                    dve.wait_ge(s_apply, split)

                    def finish(b):
                        for j in range(NL):
                            c = b * NL + j
                            nc.vector.scalar_tensor_tensor(out=tile(y, c), in0=tile(y, c), scalar=inv[:, bass.ds(c, 1)],
                                                           in1=tile(add, c), op0=ALU.mult, op1=ALU.add)
                    repeat(dve, NT // NL, finish)

            @block.scalar
            def _(act):
                act.wait_ge(s_v, 2)
                nc.scalar.activation(std[:, :], shift[:, :], ACT.Sqrt).then_inc(s_std, 1)
                act.wait_ge(s_shift, 1)

                def apply(b):
                    for j in range(NL):
                        c = b * NL + (j + split)
                        nc.scalar.activation(tile(y, c), tile(y, c), ACT.Identity, bias=shift[:, bass.ds(c, 1)],
                                             scale=inv[:, bass.ds(c, 1)]).then_inc(s_scaled, 1)
                if split < NT:
                    repeat(act, (NT - split) // NL, apply)

            @block.sync
            def _(sp):
                if store is not None:
                    assert add is None
                    for lo in range(0, split, NL):
                        later = split + lo
                        for ready, first in ((s_apply, lo), (s_scaled, later)):
                            if first >= NT:
                                continue
                            sp.wait_ge(ready, lo + NL)
                            rows = min(store.shape[0] - first * P, NL * P)
                            n = rows // P
                            sp.dma_start(store[first * P:(first + n) * P, :].rearrange("(c p) w -> p c w", p=P),
                                         y[:, first:first + n, :]).then_inc(s_store, 16)
                            if rows % P:
                                sp.dma_start(store[(first + n) * P:first * P + rows, :], y[0:rows % P, first + n, :]).then_inc(s_store, 16)
                    sp.wait_ge(s_store, 16 * (NT // NL + (store.shape[0] % P > 0)))


def vector_steps(nc, k, tag, steps):
    with ExitStack() as st:
        a = Names(nc, st)
        s_v = a.sem(tag + "v")
        with nc.Block() as block:
            @block.vector
            def _(dve):
                done = Chain(dve, s_v)
                for step in steps:
                    done(step())


def zero_fill(nc, k, tag, *tensors):
    with ExitStack() as st:
        s_fill = Names(nc, st).sem(tag + "fill")
        with nc.Block() as block:
            @block.vector
            def _(dve):
                for t in tensors:
                    nc.vector.memset(t[:, :], 0.0).then_inc(s_fill, 1)


def copies(nc, k, tag, moves):
    with ExitStack() as st:
        a = Names(nc, st)
        s_dma = a.sem(tag + "dma")
        with nc.Block() as block:
            @block.sync
            def _(sp):
                for out, src in moves:
                    sp.dma_start(out, src).then_inc(s_dma, 16)
                sp.wait_ge(s_dma, 16 * len(moves))


def relate(nc, k, tag, kv, weights, table, own, pair_rows):
    with ExitStack() as st:
        a = Names(nc, st)
        rows = a.sb(tag + "rows", [P, 2, 2 * D])
        turned = a.sb(tag + "turned", [P, 2, 4 * P])
        ring = a.sb(tag + "ring", [P, 2, RELS, 2 * D])
        flip = [a.ps(f"{tag}flip{n}", [P, 512]) for n in range(2)]
        acc = [a.ps(f"{tag}acc{n}", [P, RELS * P]) for n in range(2)]
        own_rows = a.sb(tag + "own_rows", [P, PAIR_BLOCKS, D])
        parts = [(lo, min(lo + GT, PAIR_BLOCKS)) for lo in range(0, PAIR_BLOCKS, GT)]
        s_own = [a.dma_sem(f"{tag}own{n}") for n in range(len(parts))]
        s_pairs = a.dma_sem(tag + "pairs")
        s_load = [a.dma_sem(f"{tag}load{n}") for n in range(2)]
        s_store = [a.sem(f"{tag}store{n}") for n in range(2)]
        s_flip, s_turned, s_seen2 = (a.sem(tag + n) for n in ("s_flip", "s_turned", "seen2"))
        s_acc = [a.sem(f"{tag}acc_s{n}") for n in range(2)]
        s_out = [a.sem(f"{tag}out{n}") for n in range(2)]

        def copied(eng, copy, c, n, b, side):
            wait(eng, s_store[n], b * 16)
            for q in (side, side + 2):
                eng.wait_ge(s_acc[side], c * 2 + (q // 2 + 1))
                copy(ring[:, n, :, q * P:(q + 1) * P], acc[side][:, :].rearrange("p (r w) -> p r w", w=P)).then_inc(s_out[side], 1)

        with nc.Block() as block:
            @block.sync
            def _(sp):
                def step(c, n, b):
                    for side in range(2):
                        sp.wait_ge(s_out[side], c * 2 + 2)
                    sp.dma_start(table.rearrange("(r n) w -> n r w", r=RELS)[bass.ds(c * P, P), :, :],
                                 ring[:, n, :, :]).then_inc(s_store[n], 16)
                node_tiles(sp, step)
                for n in range(2):
                    sp.wait_ge(s_store[n], 16 * ((NT + 1 - n) // 2))

            @block.gpsimd
            def _(pool):
                limit = pool.snap(pool.to_reg(KT * P - 1))

                def gather_own(c):
                    pool.indirect_dma_start(own_rows[:, c, :], None, own, bass.IndirectOffsetOnAxis(ap=k.pair_type_row[:, c:c + 1], axis=0),
                                            bounds_check=limit, oob_is_err=False).then_inc(s_own[c // GT], 16)

                def store_part(n):
                    lo, hi = parts[n]
                    pool.wait_ge(s_own[n], 16 * (hi - lo))
                    pool.dma_start(pair_rows[lo * P:hi * P, :].rearrange("(c p) w -> p c w", p=P), own_rows[:, lo:hi, :]).then_inc(s_pairs, 16)
                for c in range(NT):
                    wait(pool, s_flip, c - 1)
                    pool.indirect_dma_start(rows[:, c % 2, :], None, kv, bass.IndirectOffsetOnAxis(ap=k.type_row[:, c:c + 1], axis=0),
                                            bounds_check=limit, oob_is_err=False).then_inc(s_load[c % 2], 16)
                    gather_own(c)
                    if c % GT == GT // 2 and c > GT:
                        store_part(c // GT - 1)
                for c in range(NT, PAIR_BLOCKS):
                    gather_own(c)
                for n in range(NT // GT - (NT % GT <= GT // 2), len(parts)):
                    store_part(n)
                pool.wait_ge(s_pairs, 16 * len(parts))

            @block.tensor
            def _(pe):
                def flips(c, n, b):
                    wait(pe, s_turned, c - 1)
                    hold(pe, s_seen2, s_load[n], b * 16 + 16)
                    for q in range(4):
                        last = nc.tensor.transpose(flip[n][:, q * P:(q + 1) * P], rows[:, n, q * P:(q + 1) * P], k.ident[:, :])
                    last.then_inc(s_flip, 1)

                def step(c, n, b):
                    if not (isinstance(c, int) and c == NT - 1):
                        flips(c + 1, 1 - n, b + n)
                    pe.wait_ge(s_turned, c + 1)
                    for q in range(4):
                        wait(pe, s_out[q % 2], c * 2 + q // 2)
                        for lo in range(0, RELS * P, 512):
                            last = nc.tensor.matmul(acc[q % 2][:, lo:lo + 512], turned[:, n, q * P:(q + 1) * P],
                                                    weights[:, q, lo:lo + 512], start=True, stop=True)
                        last.then_inc(s_acc[q % 2], 1)
                flips(0, 0, 0)
                node_tiles(pe, step)

            @block.scalar
            def _(act):
                def copy_turned(c, n):
                    act.wait_ge(s_flip, c + 1)
                    wait(act, s_acc[1], (c - 1) * 2)
                    nc.scalar.copy(turned[:, n, :], flip[n][:, :]).then_inc(s_turned, 1)

                def step(c, n, b):
                    if not (isinstance(c, int) and c == NT - 1):
                        copy_turned(c + 1, 1 - n)
                    copied(act, nc.scalar.copy, c, n, b, 0)
                copy_turned(0, 0)
                node_tiles(act, step)

            @block.vector
            def _(dve):
                node_tiles(dve, lambda c, n, b: copied(dve, nc.vector.tensor_copy, c, n, b, 1))


def relation_weights(nc, k, a, ins, out):
    dk = D // 4
    with ExitStack() as st:
        t = Names(nc, st)
        att = t.sb("rw_att", [P, 2, RELS, P])
        pri = t.sb("rw_pri", [P, 2 * RELS])
        flip = t.ps("rw_flip", [P, 2 * RELS, P])
        s_zero, s_load, s_flip, s_v = (t.sem("rw_" + n) for n in ("zero", "load", "flip", "v"))
        with nc.Block() as block:
            @block.gpsimd
            def _(pool):
                pool.memset(att[:, :, :, :], 0.0).then_inc(s_zero, 1)
                pool.memset(out[:, 2:4, :], 0.0).then_inc(s_zero, 1)

            @block.sync
            def _(sp):
                sp.wait_ge(s_zero, 2)
                for kc in range(2):
                    for h2 in range(2):
                        lo, hi = h2 * dk, (h2 + 1) * dk
                        sp.dma_start(att[lo:hi, kc, :, lo:hi], ins["relation_att"][:, 2 * kc + h2].rearrange("r d e -> d r e")).then_inc(s_load, 16)
                        sp.dma_start(out[lo:hi, 2 + kc, :].rearrange("p (r e) -> p r e", e=P)[:, :, lo:hi],
                                     ins["relation_msg"][:, 2 * kc + h2].rearrange("r d e -> d r e")).then_inc(s_load, 16)
                        with nc.allow_non_contiguous_dma("32 values"):
                            sp.dma_start(pri[lo:hi, kc * RELS:(kc + 1) * RELS],
                                         ins["relation_pri"][:, 2 * kc + h2].partition_broadcast(dk)).then_inc(s_load, 16)
                sp.wait_ge(s_load, 16 * 12)

            @block.tensor
            def _(pe):
                pe.wait_ge(s_load, 16 * 12)
                for kc in range(2):
                    for r in range(RELS):
                        last = nc.tensor.transpose(flip[:, kc * RELS + r, :], att[:, kc, r, :], k.ident[:, :])
                last.then_inc(s_flip, 1)

            @block.vector
            def _(dve):
                done = Chain(dve, s_v)
                dve.wait_ge(s_load, 16 * 12)
                done(nc.vector.tensor_scalar(pri[:, :], pri[:, :], float(dk) ** -0.5, None, ALU.mult))
                dve.wait_ge(s_flip, 1)
                done(nc.vector.tensor_tensor(out[:, 0:2, :].rearrange("p c (r w) -> p (c r) w", w=P), flip[:, :, :],
                                             bcast(pri[:, :], P), ALU.mult))


def node_constants(nc, k, ins):
    with ExitStack() as st:
        a = Names(nc, st)
        rows = a.sb("nc_rows", [NT, P], I32)
        rows_f = a.sb("nc_rows_f", [NT, P])
        kind = a.ps("nc_kind", [P, 512])
        gate = a.sb("nc_gate", [P, NT, TYPES])
        skip = a.sb("nc_skip", [P, TYPES])
        root = a.sb("nc_root", [P, NT])
        some = a.sb("nc_some", [P, NT])
        s_pad, s_load, s_v, s_row, s_kind, s_deg, s_root, s_exp = (a.sem("nc_" + n) for n in ("pad", "load", "v", "row", "skind", "deg", "sroot", "exp"))
        full = N_NODES // P
        with nc.Block() as block:
            @block.gpsimd
            def _(pool):
                pool.memset(rows[:, :], 0).then_inc(s_pad, 1)

            @block.sync
            def _(sp):
                sp.wait_ge(s_pad, 1)
                sp.dma_start(rows[0:full, :], ins["node_type"][0:full * P].rearrange("(t n) -> t n", n=P)).then_inc(s_load, 16)
                sp.dma_start(rows[full:full + 1, 0:N_NODES - full * P], ins["node_type"][full * P:N_NODES].rearrange("(t n) -> t n", t=1)).then_inc(s_load, 16)
                sp.dma_start(skip[:, :], ins["skip"].partition_broadcast(P)).then_inc(s_load, 16)

            @block.tensor
            def _(pe):
                pe.wait_ge(s_row, 1)
                nc.tensor.transpose(kind[:, 0:NT], rows_f[:, :], k.ident[0:NT, 0:NT]).then_inc(s_kind, 1)

            @block.scalar
            def _(act):
                act.wait_ge(s_load, 48)
                nc.scalar.activation(skip[:, :], skip[:, :], ACT.Exp, scale=-1.0).then_inc(s_exp, 1)
                act.wait_ge(s_deg, 1)
                nc.scalar.activation(root[:, :], some[:, :], ACT.Sqrt).then_inc(s_root, 1)

            @block.vector
            def _(dve):
                done = Chain(dve, s_v)
                dve.wait_ge(s_load, 48)
                done(nc.vector.tensor_copy(rows_f[:, :], rows[:, :]))
                dve.sem_inc(s_row, 1)
                done(nc.vector.tensor_scalar(some[:, :], k.deg[:, :], 1.0, None, ALU.max))
                dve.sem_inc(s_deg, 1)
                dve.wait_ge(s_exp, 1)
                done(nc.vector.tensor_scalar(skip[:, :], skip[:, :], 1.0, None, ALU.add))
                done(nc.vector.reciprocal(skip[:, :], skip[:, :]))
                dve.wait_ge(s_kind, 1)
                mask = k.mask[:, :].rearrange("p (c t) -> p c t", t=TYPES)
                for t in range(TYPES):
                    done(nc.vector.tensor_scalar(mask[:, :, t], kind[:, 0:NT], float(t), None, ALU.is_equal))
                done(nc.vector.tensor_tensor(gate[:, :, :], mask, mid(skip[:, :], NT), ALU.mult))
                done(nc.vector.tensor_reduce(k.gate[:, :], gate[:, :, :], AX.X, ALU.add))
                dve.wait_ge(s_root, 1)
                done(nc.vector.reciprocal(k.inv_root[:, :], root[:, :]))
                done(nc.vector.tensor_scalar(some[:, :], k.deg[:, :], 0.0, None, ALU.is_gt))
                done(nc.vector.tensor_tensor(k.inv_root[:, :], k.inv_root[:, :], some[:, :], ALU.mult))


def type_order(nc, k, by_type, type_rows):
    with ExitStack() as st:
        a = Names(nc, st)
        zero = a.sb("to_zero", [P, D])
        none = a.sb("to_none", [P, NT])
        total = a.sb("to_total", [P, NT, TYPES])
        upto = a.sb("to_upto", [P, TYPES, NT])
        place = a.sb("to_place", [P, NT, TYPES])
        ends = a.sb("to_ends", [P, 3, TYPES])
        ends_i = a.sb("to_ends_i", [P, TYPES], I32)
        row = a.sb("to_row", [P, NT])
        begin, chunk, behind = (a.sb("to_" + n, [P, KT]) for n in ("begin", "chunk", "behind"))
        ranks = a.ps("to_ranks", [P, 2, 256])
        s_v, s_zero, s_ranks, s_row, s_store = (a.sem("to_" + n) for n in ("v", "szero", "sranks", "srow", "store"))
        with nc.Block() as block:
            @block.tensor
            def _(pe):
                nc.tensor.matmul(ranks[:, 0, 0:NT * TYPES], k.tri_hi[:, :], k.mask[:, :], start=True, stop=True)
                nc.tensor.matmul(ranks[:, 1, 0:NT * TYPES], k.ones[:, :], k.mask[:, :], start=True, stop=True).then_inc(s_ranks, 1)

            @block.sync
            def _(sp):
                sp.wait_ge(s_zero, 1)
                sp.dma_start(by_type.rearrange("(c p) w -> p c w", p=P), mid(zero[:, :], KT)).then_inc(s_store, 16)
                sp.wait_ge(s_row, 1)
                with nc.allow_non_contiguous_dma("a value of each node"):
                    sp.dma_start(type_rows.rearrange("(c p) o -> p (c o)", p=P), k.type_row[:, :]).then_inc(s_store, 16)
                sp.wait_ge(s_store, 32)

            @block.vector
            def _(dve):
                done = Chain(dve, s_v)
                nc.vector.memset(none[:, :], 0.0)
                done(nc.vector.memset(zero[:, :], 0.0))
                dve.sem_inc(s_zero, 1)
                dve.wait_ge(s_ranks, 1)
                done(nc.vector.tensor_copy(total[:, :, :], ranks[:, 1, 0:NT * TYPES].rearrange("p (c t) -> p c t", t=TYPES)))
                for t in range(TYPES):
                    done(nc.vector.tensor_tensor_scan(upto[:, t, :], none[:, :], total[:, :, t], 0.0, ALU.add, ALU.add))
                size, end, start = (ends[:, n, :] for n in range(3))
                done(nc.vector.tensor_scalar(size, upto[:, :, NT - 1], float(P - 1), None, ALU.add))
                done(nc.vector.tensor_copy(ends_i[:, :], size))
                done(nc.vector.tensor_scalar(ends_i[:, :], ends_i[:, :], 7, None, ALU.logical_shift_right))
                done(nc.vector.tensor_copy(size, ends_i[:, :]))
                done(nc.vector.tensor_scalar(size, size, float(P), None, ALU.mult))
                done(nc.vector.tensor_copy(end[:, 0:1], size[:, 0:1]))
                for t in range(1, TYPES):
                    done(nc.vector.tensor_tensor(end[:, t:t + 1], end[:, t - 1:t], size[:, t:t + 1], ALU.add))
                done(nc.vector.tensor_tensor(start, end, size, ALU.subtract))
                done(nc.vector.tensor_tensor(place[:, :, :], upto[:, :, :].rearrange("p t c -> p c t"), total[:, :, :], ALU.subtract))
                done(nc.vector.tensor_tensor(place[:, :, :], place[:, :, :], ranks[:, 0, 0:NT * TYPES].rearrange("p (c t) -> p c t", t=TYPES), ALU.add))
                done(nc.vector.tensor_tensor(place[:, :, :], place[:, :, :], mid(start, NT), ALU.add))
                done(nc.vector.tensor_tensor(place[:, :, :], place[:, :, :], k.mask[:, :].rearrange("p (c t) -> p c t", t=TYPES), ALU.mult))
                done(nc.vector.tensor_reduce(row[:, :], place[:, :, :], AX.X, ALU.add))
                done(nc.vector.tensor_copy(k.type_row[:, :], row[:, :]))
                dve.sem_inc(s_row, 1)
                done(nc.vector.tensor_scalar(begin[:, :], k.iota[:, 0:KT], float(P), None, ALU.mult))
                done(nc.vector.memset(chunk[:, :], 0.0))
                for t in range(TYPES - 1):
                    done(nc.vector.tensor_scalar(behind[:, :], begin[:, :], end[:, t:t + 1], 2.0, ALU.is_ge, ALU.mult))
                    done(nc.vector.tensor_tensor(chunk[:, :], chunk[:, :], behind[:, :], ALU.add))
                done(nc.vector.tensor_copy(k.tile_chunk[:, :], chunk[:, :]))


def by_type_rows(nc, k, tag, source, by_type):
    with ExitStack() as st:
        s_out = Names(nc, st).dma_sem(tag + "out")
        with nc.Block() as block:
            @block.gpsimd
            def _(pool):
                limit = pool.snap(pool.to_reg(KT * P - 1))
                for c in range(NT):
                    pool.indirect_dma_start(by_type, bass.IndirectOffsetOnAxis(ap=k.type_row[:, c:c + 1], axis=0),
                                            source[:, c, 0:D], None, bounds_check=limit, oob_is_err=False).then_inc(s_out, 16)
                pool.wait_ge(s_out, 16 * NT)


def typed_linear(nc, k, tag, by_type, weights, width, stores, type_rows):
    spans = [(lo, min(lo + 512, width)) for lo in range(0, width, 512)]
    with ExitStack() as st:
        a = Names(nc, st)
        rows = a.sb(tag + "rows", [P, 2, D])
        turned = a.sb(tag + "turned", [P, 2, 2, P])
        ring = a.sb(tag + "ring", [P, 2, width])
        flip = [a.ps(f"{tag}flip{n}", [P, 512]) for n in range(2)]
        acc = [a.ps(f"{tag}acc{n}", [P, 512 * len(spans)]) for n in range(2)]
        s_load, s_store = [a.dma_sem(f"{tag}load{n}") for n in range(2)], [a.sem(f"{tag}store{n}") for n in range(2)]
        s_flip, s_turned, s_acc, s_out, s_seen = (a.sem(tag + n) for n in ("sflip", "sturned", "sacc", "sout", "sseen"))
        s_pair = a.dma_sem(tag + "pair")
        with nc.Block() as block:
            @block.gpsimd
            def _(pool):
                limit = pool.snap(pool.to_reg(NP - 1))
                for c in range(max(KT, PAIR_BLOCKS)):
                    if c < KT:
                        wait(pool, s_flip, c - 1)
                        pool.dma_start(rows[:, c % 2, :], by_type[c * P:(c + 1) * P, :]).then_inc(s_load[c % 2], 16)
                    if c >= PAIR_BLOCKS:
                        continue
                    pool.indirect_dma_start(k.pair_type_row[:, c:c + 1], None, type_rows,
                                            bass.IndirectOffsetOnAxis(ap=k.pair_node[:, c:c + 1], axis=0),
                                            bounds_check=limit, oob_is_err=False).then_inc(s_pair, 16)
                pool.wait_ge(s_pair, 16 * PAIR_BLOCKS)

            @block.sync
            def _(sp):
                def step(c, n, b):
                    sp.wait_ge(s_out, c + 1)
                    for table, col, lo, w in stores:
                        sp.dma_start(table[bass.ds(c * P, P), col:col + w], ring[:, n, lo:lo + w]).then_inc(s_store[n], 16)
                node_tiles(sp, step, KT)
                for n in range(2):
                    sp.wait_ge(s_store[n], 16 * len(stores) * ((KT + 1 - n) // 2))

            @block.tensor
            def _(pe):
                def flips(c, n, b):
                    wait(pe, s_turned, c - 1)
                    hold(pe, s_seen, s_load[n], b * 16 + 16)
                    for q in range(2):
                        last = nc.tensor.transpose(flip[n][:, q * P:(q + 1) * P], rows[:, n, q * P:(q + 1) * P], k.ident[:, :])
                    last.then_inc(s_flip, 1)

                def step(c, n, b):
                    if not (isinstance(c, int) and c == KT - 1):
                        flips(c + 1, 1 - n, b + n)
                    chunk = nc.values_load(k.tile_chunk[0:1, bass.ds(c, 1)], engines=(mybir.EngineType.PE,),
                                           min_val=0, max_val=2 * (TYPES - 1))
                    pe.wait_ge(s_turned, c + 1)
                    hold(pe, s_seen, s_out, c - 1)
                    for lo, hi in spans:
                        for q in range(2):
                            last = nc.tensor.matmul(acc[n][:, lo:hi], turned[:, n, q, :],
                                                    weights[:, bass.ds(chunk + q, 1), lo:hi].rearrange("p o w -> p (o w)"),
                                                    start=(q == 0), stop=(q == 1))
                    last.then_inc(s_acc, 1)
                flips(0, 0, 0)
                node_tiles(pe, step, KT)

            @block.scalar
            def _(act):
                def step(c, n, b):
                    act.wait_ge(s_flip, c + 1)
                    wait(act, s_acc, c - 1)
                    nc.scalar.copy(turned[:, n, :, :].rearrange("p q w -> p (q w)"), flip[n][:, 0:D]).then_inc(s_turned, 1)
                node_tiles(act, step, KT)

            @block.vector
            def _(dve):
                def step(c, n, b):
                    dve.wait_ge(s_acc, c + 1)
                    wait(dve, s_store[n], b * (16 * len(stores)))
                    nc.vector.tensor_copy(ring[:, n, :], acc[n][:, 0:width]).then_inc(s_out, 1)
                node_tiles(dve, step, KT)


def head_average(nc, k, tag, sums, out, heads):
    dk = D // heads

    def per_head(ap):
        return ap.rearrange("p c (h d) -> p c h d", d=dk)
    z = sums[:, :, D:D + heads]
    vector_steps(nc, k, tag, [
        lambda: nc.vector.tensor_scalar(z, z, 1e-16, None, ALU.max),
        lambda: nc.vector.reciprocal(z, z),
        lambda: nc.vector.tensor_tensor(per_head(out[:, :, 0:D]), per_head(sums[:, :, 0:D]),
                                        z.unsqueeze(3).to_broadcast([P, NT, heads, dk]), ALU.mult)])


def program(nc, ins, out):
    WMAX = D + 16
    full = N_NODES // P
    with ExitStack() as st:
        a = Names(nc, st)
        k = Shared(a)
        constants(nc, k)
        into = edge_order(nc, k, a, ins, "into_", ins["dst"], ins["src"], True)
        outof = edge_order(nc, k, a, ins, "outof_", ins["src"], ins["dst"], False)
        node_constants(nc, into, ins)
        bufs = [a.sb(f"nodes{n}", [P, NT, WMAX]) for n in range(3)]
        X, H, S = (b[:, :, 0:D] for b in bufs)

        def table(name, rows, width):
            return nc.dram_tensor(name, (rows, width), F32, kind="Internal").ap()

        def node_rows(t):
            return t.rearrange("(c p) w -> p c w", p=P)

        def row(t, c):
            return t[:, bass.ds(c, 1), 0:D].rearrange("p o w -> p (o w)")

        def weight_rows(w):
            return w.rearrange("(q p) n -> p q n", p=P)

        def bias_row(b):
            return b.rearrange("(o n) -> o n", o=1)

        by_type = table("by_type", KT * P, D)
        type_rows = nc.dram_tensor("type_rows", (NP, 1), I32, kind="Internal").ap()
        type_order(nc, k, by_type, type_rows)

        vector_steps(nc, k, "x0", [lambda: nc.vector.memset(X[:, full, :], 0.0)])
        copies(nc, k, "xl", [(X[:, 0:full, :], node_rows(ins["x"][0:full * P, :])),
                             (X[0:N_NODES - full * P, full, :], ins["x"][full * P:N_NODES, :])])

        t0, p0 = table("t0", NP, D), table("p0", PROWS, D)
        vector_steps(nc, k, "l0a", [lambda: nc.vector.tensor_tensor(H, X, bcast(k.inv_root[:, :], D), ALU.mult)])
        copies(nc, k, "l0b", [(node_rows(t0), H)])
        sum_edges(nc, into, "l0c", t0, p0, False)
        merge(nc, into, "l0d", p0, 0, None)
        with ExitStack() as ws:
            w = Names(nc, ws).sb("l0w", [P, 2, D])
            gather_sums(nc, into, "l0e", p0, D, bufs[2], [(w[:, :, :], weight_rows(ins["W0"]))])
            linear(nc, k, "l0h", S, 2, w, D,
                   take=lambda out, c: nc.vector.tensor_scalar(out, row(S, c), k.inv_root[:, bass.ds(c, 1)], None, ALU.mult),
                   put=lambda c, products: nc.vector.tensor_tensor(row(X, c), row(X, c), products, ALU.add))

        t1, p1 = table("t1", NP, D), table("p1", PROWS, D)
        normalise(nc, k, "l0j", X, 1e-5, store=t1)
        sum_edges(nc, outof, "l1b", t1, p1, True)
        merge(nc, outof, "l1c", p1, 0, None)
        with ExitStack() as ws:
            w = Names(nc, ws)
            w1, w2 = w.sb("l1w1", [P, 2, D]), w.sb("l1w2", [P, 2, D])
            b1, b2 = w.sb("l1b1", [P, D]), w.sb("l1b2", [P, D])
            eps, scale, offset = w.sb("l1eps", [P, 1]), w.sb("l1scale", [P, D]), w.sb("l1offset", [P, D])
            zero_fill(nc, k, "l1z", b1, b2)
            gather_sums(nc, outof, "l1d", p1, D, bufs[2], [
                (w1[:, :, :], weight_rows(ins["W1"])), (w2[:, :, :], weight_rows(ins["W2"])),
                (b1[0:1, :], bias_row(ins["b1"])), (b2[0:1, :], bias_row(ins["b2"])),
                (eps[:, :], ins["eps"].partition_broadcast(P)), (scale[:, :], ins["scale"].partition_broadcast(P)),
                (offset[:, :], ins["offset"].partition_broadcast(P))])
            vector_steps(nc, k, "l1f", [lambda: nc.vector.tensor_scalar(eps[:, :], eps[:, :], 1.0, None, ALU.add)])
            linear(nc, k, "l1g", S, 2, w1, D, dest=H, relu=True, bias=b1,
                   take=lambda out, c: nc.vector.scalar_tensor_tensor(out=out, in0=row(X, c), scalar=eps[:, 0:1], in1=row(S, c),
                                                                      op0=ALU.mult, op1=ALU.add))
            linear(nc, k, "l1h", H, 2, w2, D, dest=S, relu=True, bias=b2)
            vector_steps(nc, k, "l1o", [lambda: nc.vector.tensor_tensor(X, X, mid(offset[:, :], NT), ALU.add)])
            normalise(nc, k, "l1i", S, 1e-10, scale=scale[:, :], add=X)
        normalise(nc, k, "l1j", S, 1e-5)
        bufs = [bufs[2], bufs[1], bufs[0]]
        X, H, S = (b[:, :, 0:D] for b in bufs)

        qv2, k2, p2 = table("qv2", NP, 2 * D), table("k2", NP, D), table("p2", PROWS, D + 16)
        with ExitStack() as ws:
            w = Names(nc, ws)
            wq, bq = w.sb("l2w", [P, 2, 3 * D]), w.sb("l2b", [P, 3 * D])
            zero_fill(nc, k, "l2z", bq)
            copies(nc, k, "l2a", [m for n, (wt, bt) in enumerate(((ins["Wq"], ins["bq"]), (ins["Wv"], ins["bv"]), (ins["Wk"], ins["bk"])))
                                  for m in ((wq[:, :, n * D:(n + 1) * D], weight_rows(wt)), (bq[0:1, n * D:(n + 1) * D], bias_row(bt)))])
            linear(nc, k, "l2b", X, 2, wq, 3 * D, bias=bq, stores=((qv2, 0, 0, 2 * D), (k2, 0, 2 * D, D)))
        pair_rows = table("pair_rows", PAIRS, D)
        spread_rows(nc, into, "l2s", k2, pair_rows)
        attend_edges(nc, into, "l2c", qv2, into.other_idx, NP, pair_rows, 8, 32.0 ** -0.5, p2, bufs[1:])
        merge(nc, into, "l2d", p2, 8, 32.0 ** -0.5)

        kv3, q3 = table("kv3", KT * P, 2 * D), table("q3", KT * P, D)
        r3, p3 = table("r3", RELS * NP, 2 * D), table("p3", PROWS, D + 8)
        with ExitStack() as ws:
            w3 = Names(nc, ws).sb("l3w", [P, 2 * TYPES, 3 * D])
            gather_sums(nc, into, "l2e", p2, D + 16, bufs[2],
                        [(w3[:, 2 * t:2 * t + 2, n * D:(n + 1) * D], weight_rows(wt[t]))
                         for n, wt in enumerate((ins["k_linears"], ins["v_linears"], ins["q_linears"])) for t in range(TYPES)])
            head_average(nc, k, "l2f", bufs[2], bufs[1], 8)
            vector_steps(nc, k, "l2g", [lambda: nc.vector.tensor_tensor(X, X, H, ALU.add)])
            normalise(nc, k, "l2h", X, 1e-5)
            by_type_rows(nc, k, "l3x", X, by_type)
            typed_linear(nc, into, "l3b", by_type, w3, 3 * D, ((kv3, 0, 0, 2 * D), (q3, 0, 2 * D, D)), type_rows)
        with ExitStack() as ws:
            wr = Names(nc, ws).sb("l3r", [P, 4, RELS * P])
            relation_weights(nc, k, a, ins, wr)
            relate(nc, k, "l3c", kv3, wr, r3, q3, pair_rows)
        attend_edges(nc, into, "l3d", r3, into.rel_idx, RELS * NP, pair_rows, 4, 1.0, p3, bufs[1:])
        merge(nc, into, "l3e", p3, 4, 1.0)
        with ExitStack() as ws:
            wa = Names(nc, ws).sb("l3wa", [P, 2 * TYPES, D])
            gather_sums(nc, into, "l3f", p3, D + 8, bufs[2],
                        [(wa[:, 2 * t:2 * t + 2, :], weight_rows(ins["a_linears"][t])) for t in range(TYPES)])
            head_average(nc, k, "l3g", bufs[2], bufs[1], 4)
            linear(nc, k, "l3i", H, 2, wa, D, types=TYPES,
                   put=lambda c, products: nc.vector.scalar_tensor_tensor(out=row(X, c), in0=products, scalar=k.gate[:, bass.ds(c, 1)],
                                                                          in1=row(X, c), op0=ALU.mult, op1=ALU.add))
        normalise(nc, k, "l3k", X, 1e-5, store=out)


_INS = {"x": "x", "src": "src", "dst": "dst", "edge_type_8": "etype", "edge_weight": "weight", "node_type_4": "node_type",
        "L0_gnn_W": "W0", "L1_gnn_W1": "W1", "L1_gnn_b1": "b1", "L1_gnn_W2": "W2", "L1_gnn_b2": "b2", "L1_gnn_eps": "eps",
        "L1_gnn_offset": "offset", "L1_gnn_scale": "scale", "L2_gnn_Wq": "Wq", "L2_gnn_bq": "bq", "L2_gnn_Wk": "Wk",
        "L2_gnn_bk": "bk", "L2_gnn_Wv": "Wv", "L2_gnn_bv": "bv", "L3_gnn_k_linears": "k_linears",
        "L3_gnn_q_linears": "q_linears", "L3_gnn_v_linears": "v_linears", "L3_gnn_a_linears": "a_linears",
        "L3_gnn_relation_att": "relation_att", "L3_gnn_relation_msg": "relation_msg",
        "L3_gnn_relation_pri": "relation_pri", "L3_gnn_skip": "skip"}


def kernel(x, src, dst, edge_type_8, edge_weight, node_type_4, L0_gnn_W, L1_gnn_W1, L1_gnn_b1, L1_gnn_W2, L1_gnn_b2,
           L1_gnn_eps, L1_gnn_offset, L1_gnn_scale, L2_gnn_Wq, L2_gnn_bq, L2_gnn_Wk, L2_gnn_bk, L2_gnn_Wv, L2_gnn_bv,
           L3_gnn_k_linears, L3_gnn_q_linears, L3_gnn_v_linears, L3_gnn_a_linears, L3_gnn_relation_att,
           L3_gnn_relation_msg, L3_gnn_relation_pri, L3_gnn_skip):
    import numpy as _np
    import concourse.bacc as _bacc
    from concourse.bass_utils import run_bass_kernel_spmd as _run

    given = dict(x=x, src=src, dst=dst, edge_type_8=edge_type_8, edge_weight=edge_weight, node_type_4=node_type_4,
                 L0_gnn_W=L0_gnn_W, L1_gnn_W1=L1_gnn_W1, L1_gnn_b1=L1_gnn_b1, L1_gnn_W2=L1_gnn_W2, L1_gnn_b2=L1_gnn_b2,
                 L1_gnn_eps=L1_gnn_eps, L1_gnn_offset=L1_gnn_offset, L1_gnn_scale=L1_gnn_scale, L2_gnn_Wq=L2_gnn_Wq,
                 L2_gnn_bq=L2_gnn_bq, L2_gnn_Wk=L2_gnn_Wk, L2_gnn_bk=L2_gnn_bk, L2_gnn_Wv=L2_gnn_Wv, L2_gnn_bv=L2_gnn_bv,
                 L3_gnn_k_linears=L3_gnn_k_linears, L3_gnn_q_linears=L3_gnn_q_linears, L3_gnn_v_linears=L3_gnn_v_linears,
                 L3_gnn_a_linears=L3_gnn_a_linears, L3_gnn_relation_att=L3_gnn_relation_att,
                 L3_gnn_relation_msg=L3_gnn_relation_msg, L3_gnn_relation_pri=L3_gnn_relation_pri, L3_gnn_skip=L3_gnn_skip)
    nc = _bacc.Bacc("TRN2", target_bir_lowering=False, num_devices=1)
    arrays, aps = {}, {}
    for name, short in _INS.items():
        v = _np.ascontiguousarray(given[name])
        arrays["in_" + name] = v
        aps[short] = nc.dram_tensor("in_" + name, v.shape, mybir.dt.from_np(v.dtype), kind="ExternalInput").ap()
    out = nc.dram_tensor("out_0", (N_NODES, D), F32, kind="ExternalOutput").ap()
    program(nc, aps, out)
    r = _run(nc, [arrays], core_ids=[0])
    return r.results[0]["out_0"]
```
